# Optimizing a Trainium2 kernel written in Bass

```python
import numpy as np
import jax
import jax.numpy as jnp

def _softmax(x, axis=-1):
    return jax.nn.softmax(x, axis=axis)

def _gelu(x):
    return jax.nn.gelu(x, approximate=True)

def _silu(x):
    return jax.nn.silu(x)

def _sigmoid(x):
    return jax.nn.sigmoid(x)

def _layernorm(x, axis=-1, eps=1e-05):
    m = jnp.mean(x, axis=axis, keepdims=True)
    v = jnp.var(x, axis=axis, keepdims=True)
    return (x - m) / jnp.sqrt(v + eps)

def _scatter_add(tgt, idx, src, axis=0):
    return tgt.at[idx].add(src)

def _segment_sum(src, seg, n):
    return jax.ops.segment_sum(src, seg, n)
kernel_name = 'mk_gnn_preln_d2_gnn_r64_96c50f'

def setup_inputs(seed: int=0):
    np.random.seed(seed)
    _w = jnp.asarray

    def _rec_inputs():
        import jax
        import jax.numpy as jnp
        _gk = jax.random.key(seed)
        x = -0.000202 + 1 * jax.random.normal(jax.random.fold_in(_gk, 1), (50000, 128), jnp.float32)
        src = jax.random.randint(jax.random.fold_in(_gk, 2), (12500,), 0, 50000, jnp.int32)
        dst = jnp.minimum((50000 * jax.random.uniform(jax.random.fold_in(_gk, 3), (12500,)) ** 2.0).astype(jnp.int32), 49999)
        _o = jnp.argsort(dst, stable=True)
        src = src[_o]
        dst = dst[_o]
        edge_attr_128 = 5.93493e-05 + 1.00006 * jax.random.normal(jax.random.fold_in(_gk, 12), (12500, 128), jnp.float32)
        edge_weight1 = jax.random.uniform(jax.random.fold_in(_gk, 14), (12500, 1), jnp.float32, 0.0, 0.999998)
        return (x, src, dst, edge_attr_128, edge_weight1)
    x, src, dst, edge_attr_128, edge_weight1 = _rec_inputs()

    def _L0_gnn_setup():
        import jax, jax.numpy as jnp
        import numpy as np
        N, E, IN_DIM, HID, HEADS, LAYERS = (50000, 5000, 128, 128, 4, 2)
        C = HID // HEADS
        EPS = 1e-05

        def _init(key, shape, fan_in):
            return jax.random.normal(key, shape, dtype=jnp.float32) / np.sqrt(fan_in)

        def _transformer_conv(h, src, tgt, edge_attr, Wq, bq, Wk, bk, Wv, bv, We, Wskip, bskip, Wbeta):
            n = h.shape[0]
            q = (h @ Wq + bq).reshape(n, HEADS, C)
            k = (h @ Wk + bk).reshape(n, HEADS, C)
            v = (h @ Wv + bv).reshape(n, HEADS, C)
            e = (edge_attr @ We).reshape(-1, HEADS, C)
            k_j = k[src] + e
            alpha = jnp.einsum('ehc,ehc->eh', q[tgt], k_j) / jnp.sqrt(jnp.float32(C))
            amax = jax.ops.segment_max(alpha, tgt, num_segments=n)
            ex = jnp.exp(alpha - amax[tgt])
            denom = jax.ops.segment_sum(ex, tgt, num_segments=n)
            a = ex / denom[tgt]
            msg = (v[src] + e) * a[..., None]
            out = jax.ops.segment_sum(msg, tgt, num_segments=n).reshape(n, HID)
            x_r = h @ Wskip + bskip
            beta = jax.nn.sigmoid(jnp.concatenate([out, x_r, out - x_r], axis=-1) @ Wbeta)
            return beta * x_r + (1.0 - beta) * out

        def _batchnorm(h, gamma, beta):
            mu = h.mean(axis=0)
            var = h.var(axis=0)
            return gamma * (h - mu) * jax.lax.rsqrt(var + EPS) + beta
        key = jax.random.key(seed)
        ks = jax.random.split(key, 20)
        x = jax.random.normal(ks[0], (N, IN_DIM), dtype=jnp.float32)
        edge_index = jax.random.randint(ks[1], (2, E), 0, N, dtype=jnp.int64)
        edge_attr = jax.random.uniform(ks[2], (E, 1), dtype=jnp.float32)
        inp = {'x': x, 'edge_index': edge_index, 'edge_attr': edge_attr, 'W_in': _init(ks[3], (IN_DIM, HID), IN_DIM), 'b_in': jnp.zeros((HID,), jnp.float32), 'Wq': _init(ks[4], (LAYERS, HID, HID), HID), 'bq': jnp.zeros((LAYERS, HID), jnp.float32), 'Wk': _init(ks[5], (LAYERS, HID, HID), HID), 'bk': jnp.zeros((LAYERS, HID), jnp.float32), 'Wv': _init(ks[6], (LAYERS, HID, HID), HID), 'bv': jnp.zeros((LAYERS, HID), jnp.float32), 'We': _init(ks[7], (LAYERS, 1, HID), 1), 'Wskip': _init(ks[8], (LAYERS, HID, HID), HID), 'bskip': jnp.zeros((LAYERS, HID), jnp.float32), 'Wbeta': _init(ks[9], (LAYERS, 3 * HID, 1), 3 * HID), 'bn_gamma': jnp.ones((LAYERS, HID), jnp.float32), 'bn_beta': jnp.zeros((LAYERS, HID), jnp.float32)}
        return inp
    _L0_gnn_all = _L0_gnn_setup()
    _L0_gnn_in = {k: v for k, v in _L0_gnn_all.items() if k in ('W_in', 'b_in', 'Wq', 'bq', 'Wk', 'bk', 'Wv', 'bv', 'We', 'Wskip', 'bskip', 'Wbeta', 'bn_gamma', 'bn_beta')}
    del _L0_gnn_all

    def _L1_gnn_setup():
        import jax, jax.numpy as jnp
        import numpy as np
        N_NODES = 50000
        N_EDGES = 9375
        D = 128
        N_GRAPHS = 64
        key = jax.random.key(seed)
        ks = jax.random.split(key, 10)
        inp = {'x': jax.random.normal(ks[0], (N_NODES, D), jnp.float32), 'edge_index': jax.random.randint(ks[1], (2, N_EDGES), 0, N_NODES, jnp.int64), 'edge_attr': jax.random.normal(ks[2], (N_EDGES, D), jnp.float32), 'u': jax.random.normal(ks[3], (N_GRAPHS, D), jnp.float32), 'batch': jnp.sort(jax.random.randint(ks[4], (N_NODES,), 0, N_GRAPHS, jnp.int64)), 'W1a': jax.random.normal(ks[5], (2 * D, 256), jnp.float32) * (1.0 / np.sqrt(2 * D)), 'b1a': jnp.zeros((256,), jnp.float32), 'W1b': jax.random.normal(ks[6], (256, D), jnp.float32) * (1.0 / 16.0), 'b1b': jnp.zeros((D,), jnp.float32), 'W2a': jax.random.normal(ks[7], (3 * D, 256), jnp.float32) * (1.0 / np.sqrt(3 * D)), 'b2a': jnp.zeros((256,), jnp.float32), 'W2b': jax.random.normal(ks[8], (256, D), jnp.float32) * (1.0 / 16.0), 'b2b': jnp.zeros((D,), jnp.float32)}
        return inp
    _L1_gnn_all = _L1_gnn_setup()
    _L1_gnn_in = {k: v for k, v in _L1_gnn_all.items() if k in ('u', 'W1a', 'b1a', 'W1b', 'b1b', 'W2a', 'b2a', 'W2b', 'b2b')}
    del _L1_gnn_all
    return {'x': x, 'src': src, 'dst': dst, 'edge_attr_128': edge_attr_128, 'edge_weight1': edge_weight1, 'L0_gnn_W_in': _L0_gnn_in['W_in'], 'L0_gnn_b_in': _L0_gnn_in['b_in'], 'L0_gnn_Wq': _L0_gnn_in['Wq'], 'L0_gnn_bq': _L0_gnn_in['bq'], 'L0_gnn_Wk': _L0_gnn_in['Wk'], 'L0_gnn_bk': _L0_gnn_in['bk'], 'L0_gnn_Wv': _L0_gnn_in['Wv'], 'L0_gnn_bv': _L0_gnn_in['bv'], 'L0_gnn_We': _L0_gnn_in['We'], 'L0_gnn_Wskip': _L0_gnn_in['Wskip'], 'L0_gnn_bskip': _L0_gnn_in['bskip'], 'L0_gnn_Wbeta': _L0_gnn_in['Wbeta'], 'L0_gnn_bn_gamma': _L0_gnn_in['bn_gamma'], 'L0_gnn_bn_beta': _L0_gnn_in['bn_beta'], 'L1_gnn_u': _L1_gnn_in['u'], 'L1_gnn_W1a': _L1_gnn_in['W1a'], 'L1_gnn_b1a': _L1_gnn_in['b1a'], 'L1_gnn_W1b': _L1_gnn_in['W1b'], 'L1_gnn_b1b': _L1_gnn_in['b1b'], 'L1_gnn_W2a': _L1_gnn_in['W2a'], 'L1_gnn_b2a': _L1_gnn_in['b2a'], 'L1_gnn_W2b': _L1_gnn_in['W2b'], 'L1_gnn_b2b': _L1_gnn_in['b2b']}

def reference(x, src, dst, edge_attr_128, edge_weight1, L0_gnn_W_in, L0_gnn_b_in, L0_gnn_Wq, L0_gnn_bq, L0_gnn_Wk, L0_gnn_bk, L0_gnn_Wv, L0_gnn_bv, L0_gnn_We, L0_gnn_Wskip, L0_gnn_bskip, L0_gnn_Wbeta, L0_gnn_bn_gamma, L0_gnn_bn_beta, L1_gnn_u, L1_gnn_W1a, L1_gnn_b1a, L1_gnn_W1b, L1_gnn_b1b, L1_gnn_W2a, L1_gnn_b2a, L1_gnn_W2b, L1_gnn_b2b):
    import jax
    import jax.numpy as jnp

    def _L0_gnn_ref(x, edge_index, edge_attr, W_in, b_in, Wq, bq, Wk, bk, Wv, bv, We, Wskip, bskip, Wbeta, bn_gamma, bn_beta):
        import jax, jax.numpy as jnp
        import numpy as np
        N, E, IN_DIM, HID, HEADS, LAYERS = (50000, 5000, 128, 128, 4, 2)
        C = HID // HEADS
        EPS = 1e-05

        def _init(key, shape, fan_in):
            return jax.random.normal(key, shape, dtype=jnp.float32) / np.sqrt(fan_in)

        def _transformer_conv(h, src, tgt, edge_attr, Wq, bq, Wk, bk, Wv, bv, We, Wskip, bskip, Wbeta):
            n = h.shape[0]
            q = (h @ Wq + bq).reshape(n, HEADS, C)
            k = (h @ Wk + bk).reshape(n, HEADS, C)
            v = (h @ Wv + bv).reshape(n, HEADS, C)
            e = (edge_attr @ We).reshape(-1, HEADS, C)
            k_j = k[src] + e
            alpha = jnp.einsum('ehc,ehc->eh', q[tgt], k_j) / jnp.sqrt(jnp.float32(C))
            amax = jax.ops.segment_max(alpha, tgt, num_segments=n)
            ex = jnp.exp(alpha - amax[tgt])
            denom = jax.ops.segment_sum(ex, tgt, num_segments=n)
            a = ex / denom[tgt]
            msg = (v[src] + e) * a[..., None]
            out = jax.ops.segment_sum(msg, tgt, num_segments=n).reshape(n, HID)
            x_r = h @ Wskip + bskip
            beta = jax.nn.sigmoid(jnp.concatenate([out, x_r, out - x_r], axis=-1) @ Wbeta)
            return beta * x_r + (1.0 - beta) * out

        def _batchnorm(h, gamma, beta):
            mu = h.mean(axis=0)
            var = h.var(axis=0)
            return gamma * (h - mu) * jax.lax.rsqrt(var + EPS) + beta
        src, tgt = (edge_index[0], edge_index[1])
        h = jax.nn.relu(x @ W_in + b_in)
        for l in range(LAYERS):
            h_res = h
            h = _transformer_conv(h, src, tgt, edge_attr, Wq[l], bq[l], Wk[l], bk[l], Wv[l], bv[l], We[l], Wskip[l], bskip[l], Wbeta[l])
            h = jax.nn.relu(_batchnorm(h, bn_gamma[l], bn_beta[l]))
            h = h + h_res
        return h

    def _L1_gnn_ref(x, edge_index, edge_attr, u, batch, W1a, b1a, W1b, b1b, W2a, b2a, W2b, b2b):
        import jax, jax.numpy as jnp
        import numpy as np
        N_NODES = 50000
        N_EDGES = 9375
        D = 128
        N_GRAPHS = 64
        row, col = (edge_index[0], edge_index[1])
        h = jnp.concatenate([x[row], edge_attr], axis=1)
        h = jax.nn.relu(h @ W1a + b1a) @ W1b + b1b
        s = jax.ops.segment_sum(h, col, num_segments=x.shape[0])
        cnt = jax.ops.segment_sum(jnp.ones((col.shape[0],), x.dtype), col, num_segments=x.shape[0])
        agg = s / jnp.maximum(cnt, 1.0)[:, None]
        h2 = jnp.concatenate([x, agg, u[batch]], axis=1)
        return jax.nn.relu(h2 @ W2a + b2a) @ W2b + b2b
    edge_index = jnp.stack([src, dst])
    batch0 = jnp.zeros((50000,), jnp.int32)
    h = jnp.maximum(_layernorm(x, axis=-1), 0.0)
    x = x + _L0_gnn_ref(h, edge_index, edge_weight1, L0_gnn_W_in, L0_gnn_b_in, L0_gnn_Wq, L0_gnn_bq, L0_gnn_Wk, L0_gnn_bk, L0_gnn_Wv, L0_gnn_bv, L0_gnn_We, L0_gnn_Wskip, L0_gnn_bskip, L0_gnn_Wbeta, L0_gnn_bn_gamma, L0_gnn_bn_beta)
    h = jnp.maximum(_layernorm(x, axis=-1), 0.0)
    x = x + _L1_gnn_ref(h, edge_index, edge_attr_128, L1_gnn_u, batch0, L1_gnn_W1a, L1_gnn_b1a, L1_gnn_W1b, L1_gnn_b1b, L1_gnn_W2a, L1_gnn_b2a, L1_gnn_W2b, L1_gnn_b2b)
    return x

_drawn_inputs = setup_inputs


def setup_inputs(seed=0):
    import zlib

    import numpy as np

    out = dict(_drawn_inputs(seed))
    spreads = {'L0_gnn_b_in': (0.0, 0.1),
     'L0_gnn_bq': (0.0, 2.0),
     'L0_gnn_bk': (0.0, 2.0),
     'L0_gnn_bv': (0.0, 0.1),
     'L0_gnn_bskip': (0.0, 0.276),
     'L0_gnn_bn_gamma': (1.0, 0.2),
     'L0_gnn_bn_beta': (0.0, 0.1),
     'L1_gnn_b1a': (0.0, 0.8),
     'L1_gnn_b1b': (0.0, 0.789),
     'L1_gnn_b2a': (0.0, 0.1),
     'L1_gnn_b2b': (0.0, 0.1)}
    factors = {}
    for name, (base, spread) in spreads.items():
        noise = np.random.default_rng([zlib.crc32(name.encode()), seed]).standard_normal(out[name].shape)
        drawn = base * np.exp(spread * noise) if base else spread * noise
        out[name] = jnp.asarray(drawn.astype(out[name].dtype))
    for name, factor in factors.items():
        out[name] = (out[name] * factor).astype(out[name].dtype)
    return out
```

```python
from collections import namedtuple
from contextlib import ExitStack, contextmanager

import concourse.bass as bass
from concourse import mybir

ALU = mybir.AluOpType
ACT = mybir.ActivationFunctionType
F32 = mybir.dt.float32
I32 = mybir.dt.int32

NODES, EDGES, D, HEADS, LAYERS = 50000, 12500, 128, 4, 2
HD = D // HEADS
TILE, TILES = 125, 4
CH = TILE * TILES
NCHUNK, ECHUNK = NODES // CH, EDGES // CH
SPLIT = 112
EPS = 1e-5
BIG = 3.0e38
MAPW = 16
NOWHERE = 1 << 20
AHEAD = 16


def Group(**named):
    return namedtuple("Group", named)(**named)


def made(k):
    return k + AHEAD + 1


def pipeline(eng, n, unroll, stages, peel=0):
    head = max(lag for lag, _ in stages) + peel
    turns = (n - head) // unroll

    def peeled(t):
        for lag, stage in stages:
            if 0 <= t - lag < n:
                stage(t - lag, (t - lag) % unroll, (t - lag) // unroll)

    for t in range(head):
        peeled(t)
    with eng.Fori(0, turns) as i:
        for s in range(unroll):
            for lag, stage in stages:
                d = head + s - lag
                stage(unroll * i + d, d % unroll, i + d // unroll)
    for t in range(head + unroll * turns, n + head - peel):
        peeled(t)


@contextmanager
def phase(nc, name):
    sems, begin = [], []

    def sem(n, at=0):
        sems.append(nc.alloc_semaphore(f"{name}_{n}"))
        if at:
            begin.append((sems[-1], at))
        return sems[-1]

    def start(eng):
        for s, at in begin:
            eng.sem_inc(s, at)

    with ExitStack() as ctx:
        yield Group(
            sb=lambda n, s, d=F32: ctx.enter_context(nc.sbuf_tensor(f"{name}_{n}", s, d)),
            ps=lambda n, s=(128, 512): ctx.enter_context(nc.psum_tensor(f"{name}_{n}", list(s), F32)),
            stage=lambda n: sem(n, AHEAD),
            count=lambda n: sem(n),
            loaded=lambda n, u: [sem(f"{n}{s}") for s in range(u)],
            stored=lambda n, u: [sem(f"{n}{s}", 16) for s in range(u)],
            seen=sem("sp_seen"), start=start)
        nc.all_engine_barrier()
        nc.clear_and_free_semaphores(sems)
        nc.all_engine_barrier()


def hold(sp, seen, sem, value):
    sp.wait_ge(sem, value)
    sp.sem_inc(seen, 1)



def rows_of(table, row0):
    return table[bass.ds(row0, CH), :].rearrange("(p j) f -> p (j f)", j=TILES)


def cols_of(table, col0):
    return table[:, bass.ds(col0, CH)]


def move_rows(eng, out, in_, sem, n=16):
    eng.dma_start(out[0:SPLIT], in_[0:SPLIT]).then_inc(sem, n)
    eng.dma_start(out[SPLIT:TILE], in_[SPLIT:TILE]).then_inc(sem, n)


def flat(buf, q):
    return buf[:, q].rearrange("p j f -> p (j f)")


def tile_cols(t, j, ordered):
    return t[:, j:CH:TILES] if ordered else t[:, j * TILE:(j + 1) * TILE]


def by_tile(ps):
    return ps[:, 0:CH].rearrange("f (j p) -> f j p", j=TILES)


def in_order(t, ordered):
    return t.rearrange("f (p j) -> f j p", j=TILES) if ordered else t.rearrange("f (j p) -> f j p", j=TILES)



def prepare(nc, a, w, scratch):
    with phase(nc, "prep") as ph, nc.Block() as block:
        loaded, ones_made, pool_made = ph.count("loaded"), ph.count("ones_made"), ph.count("pool_made")
        dve_made, pe_made, act_made, written = (ph.count(n) for n in ("dve_made", "pe_made", "act_made", "written"))
        beta3 = ph.sb("beta3", [128, LAYERS, 3])
        wskipT = ph.sb("wskipT", [128, LAYERS, D])
        gate_x = ph.sb("gate_x", [128, LAYERS, D])
        gate_cols = ph.sb("gate_cols", [128, LAYERS, 2])
        ucol = ph.sb("ucol", [128, 1])
        b2a = ph.sb("b2a", [128, 2])
        w2u = ph.sb("w2u", [128, 256])
        ones = ph.sb("ones", [128, D])
        dsti = ph.sb("dsti", [TILE, ECHUNK, TILES], I32)
        nxt = ph.sb("nxt", [TILE, ECHUNK, TILES], I32)
        f1 = ph.sb("f1", [TILE, ECHUNK * TILES])
        f2 = ph.sb("f2", [TILE, ECHUNK * TILES])
        endi = ph.sb("endi", [TILE, ECHUNK, TILES], I32)
        ident_map = ph.sb("ident_map", [TILE, NODES // TILE, MAPW], I32)
        edge_rows = ph.sb("edge_rows", [TILE, ECHUNK, TILES, MAPW], I32)
        minus1 = ph.sb("minus1", [1, 2], I32)
        ps = ph.ps("small")
        psg = ph.ps("gate")
        n_loads = []

        @block.sync
        def _(sp):
            def load(dst, src):
                sp.dma_start(dst, src).then_inc(loaded, 16)
                n_loads.append(1)
            load(w.W_in[:], a["L0_gnn_W_in"])
            for l in range(LAYERS):
                load(w.Wq[:, l], a["L0_gnn_Wq"][l])
                load(w.Wk[:, l], a["L0_gnn_Wk"][l])
                load(w.Wv[:, l], a["L0_gnn_Wv"][l])
                load(w.Wskip[:, l], a["L0_gnn_Wskip"][l])
            load(w.W1a[:], a["L1_gnn_W1a"].rearrange("(b k) m -> k b m", k=128))
            load(w.W1b[:], a["L1_gnn_W1b"].rearrange("(b k) m -> k b m", k=128))
            load(w.W2a[:], a["L1_gnn_W2a"][0:256].rearrange("(b k) m -> k b m", k=128))
            load(w2u[:], a["L1_gnn_W2a"][256:384])
            load(w.W2b[:], a["L1_gnn_W2b"].rearrange("(b k) m -> k b m", k=128))
            load(w.We[:], a["L0_gnn_We"].rearrange("l o f -> o l f"))
            load(w.b2b[:], a["L1_gnn_b2b"].rearrange("(o f) -> o f", o=1).to_broadcast([TILE, D]))
            with nc.allow_non_contiguous_dma(reason="one word a partition"):
                load(w.b_in[:], a["L0_gnn_b_in"].rearrange("(f o) -> f o", o=1))
                for name, t in (("bq", w.bq), ("bk", w.bk), ("bv", w.bv), ("bskip", w.bskip),
                                ("bn_gamma", w.gamma), ("bn_beta", w.beta)):
                    load(t[:], a["L0_gnn_" + name].rearrange("l f -> f l"))
                load(beta3[:], a["L0_gnn_Wbeta"].rearrange("l (t f) o -> f l (t o)", t=3))
                load(ucol[:], a["L1_gnn_u"][0:1].rearrange("o f -> f o"))
                load(b2a[:], a["L1_gnn_b2a"].rearrange("(h f) -> f h", h=2))
                load(w.b1a[:], a["L1_gnn_b1a"].rearrange("(h f) -> f h", h=2))
                load(w.b1b[:], a["L1_gnn_b1b"].rearrange("(f o) -> f o", o=1))
            load(dsti[:], a["dst"].rearrange("(c p j) -> p c j", p=TILE, j=TILES))
            sp.wait_ge(pool_made, 1)
            c_last = ECHUNK - 1
            head = a["dst"][1:1 + c_last * CH]
            load(nxt[:, 0:c_last], head.rearrange("(c p j) -> p c j", p=TILE, j=TILES))
            tail = a["dst"][1 + c_last * CH:1 + c_last * CH + (TILE - 1) * TILES]
            load(nxt[0:TILE - 1, c_last], tail.rearrange("(p j) -> p j", j=TILES))
            load(nxt[TILE - 1:TILE, c_last, 0:TILES - 1], a["dst"][EDGES - TILES + 1:EDGES].rearrange("(o j) -> o j", o=1))
            sp.wait_ge(pool_made, 2)
            sp.dma_start(scratch.dst_pad[:, 0:1], minus1[:, 0:1]).then_inc(written, 16)
            sp.dma_start(scratch.dst_pad[:, EDGES + 1:EDGES + 2], minus1[:, 1:2]).then_inc(written, 16)
            sp.dma_start(scratch.dst_pad[:, 1:EDGES + 1], a["dst"].rearrange("(o e) -> o e", o=1)).then_inc(written, 16)
            sp.wait_ge(pool_made, 4)
            sp.dma_start(scratch.node_map.rearrange("(p n) w -> p (n w)", p=TILE), ident_map[:].rearrange("p n w -> p (n w)")).then_inc(written, 16)
            for c in range(ECHUNK):
                sp.dma_start(scratch.edge_row[c * CH:(c + 1) * CH].rearrange("(p j) w -> p (j w)", j=TILES),
                             edge_rows[:, c].rearrange("p j w -> p (j w)")).then_inc(written, 16)
            sp.wait_ge(dve_made, 99)
            sp.dma_start(scratch.end_index.rearrange("(c p j) -> p c j", p=TILE, j=TILES), endi[:]).then_inc(written, 16)
            sp.wait_ge(written, 16 * (5 + ECHUNK))

        all_loaded = 16 * len(n_loads)

        @block.gpsimd
        def _(pool):
            pool.memset(nxt[:], -1).then_inc(pool_made, 1)
            pool.memset(minus1[:], -1).then_inc(pool_made, 1)
            pool.iota(ident_map[:], [[1, NODES // TILE], [0, MAPW]], base=0, channel_multiplier=NODES // TILE).then_inc(pool_made, 1)
            pool.iota(edge_rows[:], [[CH, ECHUNK], [1, TILES], [0, MAPW]], base=NODES, channel_multiplier=TILES).then_inc(pool_made, 1)
            pool.memset(ones[:], 1.0).then_inc(ones_made, 1)
            pool.memset(w.ident[:], 0.0).then_inc(ones_made, 1)
            pool.memset(w.heads[:], 0.0).then_inc(ones_made, 1)
            pool.memset(w.power[:], -0.5).then_inc(ones_made, 1)
            pool.memset(w.eps[:], EPS).then_inc(ones_made, 1)
            pool.wait_ge(ones_made, 5)
            pool.affine_select(out=w.ident[:], in_=w.ident[:], compare_op=ALU.not_equal, fill=1.0, base=0,
                               pattern=[[-1, 128]], channel_multiplier=1).then_inc(ones_made, 1)

        @block.vector
        def _(dve):
            n = 0

            def after(ins):
                nonlocal n
                n += 1
                ins.then_inc(dve_made, 1)
                dve.wait_ge(dve_made, n)

            dve.wait_ge(loaded, all_loaded)
            dve.wait_ge(ones_made, 6)
            for h in range(HEADS):
                dve.memset(w.heads[h * HD:(h + 1) * HD, h * HD:(h + 1) * HD], float(HD) ** -0.5)
            for l in range(LAYERS):
                after(dve.tensor_tensor(gate_cols[:, l, 0:1], beta3[:, l, 0:1], beta3[:, l, 2:3], ALU.add))
                after(dve.tensor_tensor(gate_cols[:, l, 1:2], beta3[:, l, 1:2], beta3[:, l, 2:3], ALU.subtract))
                after(dve.tensor_scalar(w.gate_out[:, l], ones[:], gate_cols[:, l, 0:1], None, ALU.mult))
                after(dve.tensor_scalar(gate_x[:, l], ones[:], gate_cols[:, l, 1:2], None, ALU.mult))
            dve.wait_ge(pe_made, 1)
            after(dve.tensor_copy(wskipT[:].rearrange("p l f -> p (l f)"), ps[:, 0:LAYERS * D]))
            dve.wait_ge(pe_made, 2)
            after(dve.tensor_copy(w.gate_h[:].rearrange("p l f -> p (l f)"), psg[:, 0:LAYERS * D]))
            after(dve.tensor_copy(w.gate_b[:], psg[:, LAYERS * D:LAYERS * D + LAYERS]))
            after(dve.tensor_scalar(w.gate_bh[:], w.gate_b[:], 0.5, None, ALU.mult))
            after(dve.tensor_tensor(w.b2u[:], psg[:, 300:302], b2a[:], ALU.add))
            d, e = dsti[:].rearrange("p c j -> p (c j)"), nxt[:].rearrange("p c j -> p (c j)")
            after(dve.tensor_tensor(f1[:], d, e, ALU.not_equal))
            after(dve.scalar_tensor_tensor(out=f2[:], in0=d, scalar=float(-NOWHERE), in1=f1[:], op0=ALU.add, op1=ALU.mult))
            after(dve.tensor_scalar(endi[:].rearrange("p c j -> p (c j)"), f2[:], float(NOWHERE), None, ALU.add))
            dve.sem_inc(dve_made, 99 - n)

        @block.tensor
        def _(pe):
            pe.wait_ge(loaded, all_loaded)
            pe.wait_ge(ones_made, 6)
            for l in range(LAYERS):
                last = pe.transpose(ps[:, l * D:(l + 1) * D], w.Wskip[:, l], w.ident[:])
            last.then_inc(pe_made, 1)
            pe.wait_ge(dve_made, 4 * LAYERS + 1)
            for l in range(LAYERS):
                pe.matmul(psg[:, l * D:(l + 1) * D], wskipT[:, l], gate_x[:, l], start=True, stop=True)
                pe.matmul(psg[:, LAYERS * D + l:LAYERS * D + l + 1], gate_x[:, l], w.bskip[:, l:l + 1], start=True, stop=True)
            for h in range(2):
                last = pe.matmul(psg[:, 300 + h:301 + h], w2u[:, h * 128:(h + 1) * 128], ucol[:], start=True, stop=True)
            last.then_inc(pe_made, 1)



def norm_stats(dve, x, st, stats_made):
    for j in range(x.shape[1]):
        last = dve.bn_stats(st[:, j], x[:, j])
    last.then_inc(stats_made, 1)


def norm_aggr(dve, st, mv, stats_seen, aggr_made):
    dve.sem_inc(stats_seen, 1)
    for j in range(st.shape[1]):
        last = dve.bn_aggr(mv[:, j], st[:, j])
    last.then_inc(aggr_made, 1)


def norm_apply(dve, xn, x, mv, rstd, norm_made):
    for j in range(x.shape[1]):
        last = dve.tensor_scalar(xn[:, j], x[:, j], mv[:, j, 0:1], rstd[:, j:j + 1], ALU.subtract, ALU.mult)
    last.then_inc(norm_made, 1)


def to_T(pe, ps, rows, ident, sem):
    for j in range(TILES):
        last = pe.transpose(ps[:, j * TILE:(j + 1) * TILE], rows[:, j], ident[0:TILE, 0:TILE])
    last.then_inc(sem, 1)


def to_rows(pe, ps, t, ident, ordered, sem):
    for j in range(TILES):
        last = pe.transpose(ps[0:TILE, j * D:(j + 1) * D], tile_cols(t, j, ordered), ident[:])
    last.then_inc(sem, 1)


def dense_first(nc, a, w, scratch):
    U = 4
    with phase(nc, "first") as ph:
        x = ph.sb("x", [TILE, U, TILES, D])
        xn = ph.sb("xn", [TILE, 2, TILES, D])
        st = ph.sb("st", [TILE, 2, TILES, 6])
        mv = ph.sb("mv", [TILE, 2, TILES, 2])
        ve = ph.sb("ve", [TILE, 2, TILES])
        rstd = ph.sb("rstd", [TILE, 2, TILES])
        h0 = ph.sb("h0", [128, 2, CH])
        h1 = ph.sb("h1", [128, U, CH])
        sig = ph.sb("sig", [128, 2, CH])
        y = ph.sb("y", [128, U, CH])
        psT = [ph.ps(f"psT{s}") for s in range(2)]
        psW = [ph.ps(f"psW{s}") for s in range(2)]
        psX = [ph.ps(f"psX{s}") for s in range(2)]
        psZ = [ph.ps(f"psZ{s}") for s in range(2)]
        x_loaded = ph.loaded("x_loaded", U)
        h1_stored, y_stored = ph.stored("h1_stored", U), ph.stored("y_stored", U)
        names = "stats seen aggr eps rstd xn xT h0 w_in h1 xz sig y ystats".split()
        m = Group(**{n: ph.stage(n + "_made") for n in names})
        with nc.Block() as block:
            @block.sync
            def _(sp):
                ph.start(sp)

                def load(k, q, r):
                    hold(sp, ph.seen, m.xn, made(k - U))
                    move_rows(sp, flat(x, q), rows_of(a["x"], k * CH), x_loaded[q])

                def store_h(k, q, r):
                    hold(sp, ph.seen, m.h1, made(k))
                    sp.dma_start(cols_of(scratch.hT, k * CH), h1[:, q]).then_inc(h1_stored[q], 16)

                def store_y(k, q, r):
                    hold(sp, ph.seen, m.y, made(k))
                    sp.dma_start(cols_of(scratch.yT, k * CH), y[:, q]).then_inc(y_stored[q], 16)

                pipeline(sp, NCHUNK, U, [(0, load), (6, store_h), (7, store_y)])
                for q in range(U):
                    sp.wait_ge(h1_stored[q], 16 + 16 * (NCHUNK // U))
                    sp.wait_ge(y_stored[q], 16 + 16 * (NCHUNK // U))

            @block.vector
            def _(dve):
                def stats(k, q, r):
                    dve.wait_ge(x_loaded[q], 32 * r + 32)
                    dve.wait_ge(m.aggr, made(k - 2))
                    norm_stats(dve, x[:, q], st[:, q % 2], m.stats)

                def aggr(k, q, r):
                    dve.wait_ge(m.stats, made(k))
                    dve.wait_ge(m.xn, made(k - 2))
                    norm_aggr(dve, st[:, q % 2], mv[:, q % 2], m.seen, m.aggr)

                def apply(k, q, r):
                    dve.wait_ge(m.rstd, made(k))
                    dve.wait_ge(m.xT, made(k - 2))
                    norm_apply(dve, xn[:, q % 2], x[:, q], mv[:, q % 2], rstd[:, q % 2], m.xn)

                def make_h1(k, q, r):
                    dve.wait_ge(m.w_in, made(k))
                    dve.wait_ge(m.xz, made(k - U))
                    dve.wait_ge(h1_stored[q], 16 * r + 16)
                    dve.tensor_scalar(h1[:, q], psW[q % 2][:, 0:CH], w.b_in[:, 0:1], 0.0, ALU.add, ALU.max).then_inc(m.h1, 1)

                def make_y(k, q, r):
                    dve.wait_ge(m.sig, made(k))
                    dve.wait_ge(m.ystats, made(k - U))
                    dve.wait_ge(y_stored[q], 16 * r + 16)
                    dve.scalar_tensor_tensor(out=y[:, q], in0=psX[q % 2][:, 0:CH], scalar=w.bskip[:, 0:1],
                                             in1=sig[:, q % 2], op0=ALU.add, op1=ALU.mult).then_inc(m.y, 1)

                def ystats(k, q, r):
                    dve.wait_ge(m.y, made(k))
                    dve.bn_stats(w.ystats[:, bass.ds(k * 6, 6)], y[:, q]).then_inc(m.ystats, 1)

                pipeline(dve, NCHUNK, U, [(0, stats), (3, make_h1), (0, aggr), (4, make_y), (1, apply), (4, ystats)])

            @block.gpsimd
            def _(pool):
                def make_rstd(k, q, r):
                    pool.wait_ge(m.aggr, made(k))
                    pool.wait_ge(m.xn, made(k - 2))
                    pool.tensor_tensor(ve[:, q % 2], mv[:, q % 2, :, 1], w.eps[0:TILE, 0:TILES], ALU.add).then_inc(m.eps, 1)
                    pool.wait_ge(m.eps, made(k))
                    pool.tensor_tensor(rstd[:, q % 2], ve[:, q % 2], w.power[0:TILE, 0:TILES], ALU.pow).then_inc(m.rstd, 1)
                pipeline(pool, NCHUNK, U, [(0, make_rstd)])

            @block.tensor
            def _(pe):
                def turn(k, q, r):
                    pe.wait_ge(m.xn, made(k))
                    pe.wait_ge(m.h0, made(k - 2))
                    to_T(pe, psT[q % 2], xn[:, q % 2], w.ident, m.xT)

                def first(k, q, r):
                    pe.wait_ge(m.h0, made(k))
                    pe.wait_ge(m.h1, made(k - 2))
                    pe.matmul(psW[q % 2][:, 0:CH], w.W_in[:], h0[:, q % 2], start=True, stop=True).then_inc(m.w_in, 1)

                def skip(k, q, r):
                    pe.wait_ge(m.h1, made(k))
                    pe.wait_ge(m.y, made(k - 2))
                    pe.matmul(psZ[q % 2][:, 0:CH], w.gate_h[:, 0], h1[:, q], start=True, stop=True)
                    pe.matmul(psX[q % 2][:, 0:CH], w.Wskip[:, 0], h1[:, q], start=True, stop=True).then_inc(m.xz, 1)

                pipeline(pe, NCHUNK, U, [(0, turn), (1, first), (2, skip)])

            @block.scalar
            def _(act):
                def make_h0(k, q, r):
                    act.wait_ge(m.xT, made(k))
                    act.wait_ge(m.w_in, made(k - 2))
                    act.activation(h0[:, q % 2], psT[q % 2][:, 0:CH], ACT.Relu).then_inc(m.h0, 1)

                def make_sig(k, q, r):
                    act.wait_ge(m.xz, made(k))
                    act.wait_ge(m.y, made(k - 2))
                    act.activation(sig[:, q % 2], psZ[q % 2][:, 0:CH], ACT.Sigmoid, bias=w.gate_b[:, 0:1]).then_inc(m.sig, 1)

                pipeline(act, NCHUNK, U, [(0, make_h0), (2, make_sig)])


def batch_norm_params(nc, w, l):
    with phase(nc, f"bn{l}") as ph, nc.Block() as block:
        done, pool_done = ph.count("dve_done"), ph.count("pool_done")
        agg = ph.sb("agg", [128, 3, 2])
        sq = ph.sb("sq", [128, 3])
        tmp = ph.sb("tmp", [128, 8])
        rs = ph.sb("rs", [128, 4])
        ratio = EDGES / NODES

        @block.vector
        def _(dve):
            n = 0

            def after(ins):
                nonlocal n
                n += 1
                ins.then_inc(done, 1)
                dve.wait_ge(done, n)
            after(dve.bn_aggr(agg[:, 0], w.ystats[:]))
            after(dve.bn_aggr(agg[:, 1], w.wends[:]))
            after(dve.bn_aggr(agg[:, 2], w.ends[:]))
            after(dve.tensor_tensor(sq[:], agg[:, :, 0], agg[:, :, 0], ALU.mult))
            after(dve.tensor_tensor(sq[:], sq[:], agg[:, :, 1], ALU.add))
            after(dve.tensor_tensor(tmp[:, 0:1], agg[:, 1, 0:1], agg[:, 2, 0:1], ALU.subtract))
            after(dve.scalar_tensor_tensor(out=tmp[:, 1:2], in0=tmp[:, 0:1], scalar=ratio, in1=agg[:, 0, 0:1], op0=ALU.mult, op1=ALU.add))
            after(dve.tensor_tensor(tmp[:, 2:3], sq[:, 2:3], sq[:, 1:2], ALU.subtract))
            after(dve.scalar_tensor_tensor(out=tmp[:, 3:4], in0=tmp[:, 2:3], scalar=ratio, in1=sq[:, 0:1], op0=ALU.mult, op1=ALU.add))
            after(dve.tensor_tensor(tmp[:, 4:5], tmp[:, 1:2], tmp[:, 1:2], ALU.mult))
            after(dve.tensor_tensor(tmp[:, 5:6], tmp[:, 3:4], tmp[:, 4:5], ALU.subtract))
            after(dve.tensor_scalar(rs[:, 0:1], tmp[:, 5:6], 0.0, EPS, ALU.max, ALU.add))
            dve.wait_ge(pool_done, 1)
            after(dve.tensor_tensor(w.bn[:, 0:1], w.gamma[:, l:l + 1], rs[:, 1:2], ALU.mult))
            after(dve.tensor_tensor(tmp[:, 6:7], tmp[:, 1:2], w.bn[:, 0:1], ALU.mult))
            after(dve.tensor_tensor(w.bn[:, 1:2], w.beta[:, l:l + 1], tmp[:, 6:7], ALU.subtract))

        @block.gpsimd
        def _(pool):
            pool.wait_ge(done, 12)
            pool.tensor_tensor(rs[:, 1:2], rs[:, 0:1], w.power[:, 0:1], ALU.pow).then_inc(pool_done, 1)


def dense_second(nc, a, w, scratch):
    U = 4
    with phase(nc, "second") as ph:
        yin = ph.sb("yin", [128, U, CH])
        hin = ph.sb("hin", [128, U, CH])
        act1 = ph.sb("act1", [128, 2, CH])
        h2 = ph.sb("h2", [128, U, CH])
        rows = ph.sb("rows", [TILE, U, TILES, D])
        sig = ph.sb("sig", [128, 2, CH])
        y = ph.sb("y", [128, U, CH])
        psR = [ph.ps(f"psR{s}") for s in range(2)]
        psX = [ph.ps(f"psX{s}") for s in range(2)]
        psZ = [ph.ps(f"psZ{s}") for s in range(2)]
        y_loaded, h_loaded = ph.loaded("y_loaded", U), ph.loaded("h_loaded", U)
        h2_stored, rows_stored, y_stored = (ph.stored(n, U) for n in ("h2_stored", "rows_stored", "y_stored"))
        rows_stored2 = ph.stored("rows_stored2", U)
        m = Group(**{n: ph.stage(n + "_made") for n in "bn h2 turned rows xz sig y ystats".split()})
        with nc.Block() as block:
            @block.sync
            def _(sp):
                ph.start(sp)

                def load(k, q, r):
                    hold(sp, ph.seen, m.bn, made(k - U))
                    sp.dma_start(yin[:, q], cols_of(scratch.yT, k * CH)).then_inc(y_loaded[q], 16)
                    hold(sp, ph.seen, m.h2, made(k - U))
                    sp.dma_start(hin[:, q], cols_of(scratch.hT, k * CH)).then_inc(h_loaded[q], 16)

                def store_h(k, q, r):
                    hold(sp, ph.seen, m.h2, made(k))
                    sp.dma_start(cols_of(scratch.hT, k * CH), h2[:, q]).then_inc(h2_stored[q], 16)

                def store_rows(k, q, r):
                    hold(sp, ph.seen, m.rows, made(k))
                    dst = rows_of(scratch.h2, k * CH)
                    sp.dma_start(dst[0:SPLIT], flat(rows, q)[0:SPLIT]).then_inc(rows_stored[q], 16)
                    sp.dma_start(dst[SPLIT:TILE], flat(rows, q)[SPLIT:TILE]).then_inc(rows_stored2[q], 16)

                def store_y(k, q, r):
                    hold(sp, ph.seen, m.y, made(k))
                    sp.dma_start(cols_of(scratch.yT, k * CH), y[:, q]).then_inc(y_stored[q], 16)

                pipeline(sp, NCHUNK, U, [(0, load), (5, store_h), (6, store_rows), (7, store_y)])
                for sems in (h2_stored, rows_stored, rows_stored2, y_stored):
                    for q in range(U):
                        sp.wait_ge(sems[q], 16 + 16 * (NCHUNK // U))

            @block.scalar
            def _(act):
                def bn(k, q, r):
                    act.wait_ge(y_loaded[q], 16 * r + 16)
                    act.wait_ge(m.h2, made(k - 2))
                    act.activation(act1[:, q % 2], yin[:, q], ACT.Relu, bias=w.bn[:, 1:2], scale=w.bn[:, 0:1]).then_inc(m.bn, 1)

                def make_rows(k, q, r):
                    act.wait_ge(m.turned, made(k))
                    act.wait_ge(rows_stored[q], 16 * r + 16)
                    act.wait_ge(rows_stored2[q], 16 * r + 16)
                    act.copy(flat(rows, q), psR[q % 2][0:TILE]).then_inc(m.rows, 1)

                def make_sig(k, q, r):
                    act.wait_ge(m.xz, made(k))
                    act.wait_ge(m.y, made(k - 2))
                    act.activation(sig[:, q % 2], psZ[q % 2][:, 0:CH], ACT.Sigmoid, bias=w.gate_b[:, 1:2]).then_inc(m.sig, 1)

                pipeline(act, NCHUNK, U, [(0, bn), (2, make_rows), (2, make_sig)])

            @block.vector
            def _(dve):
                def make_h2(k, q, r):
                    dve.wait_ge(m.bn, made(k))
                    dve.wait_ge(h_loaded[q], 16 * r + 16)
                    dve.wait_ge(h2_stored[q], 16 * r + 16)
                    dve.wait_ge(m.xz, made(k - U))
                    dve.tensor_tensor(h2[:, q], act1[:, q % 2], hin[:, q], ALU.add).then_inc(m.h2, 1)

                def make_y(k, q, r):
                    dve.wait_ge(m.sig, made(k))
                    dve.wait_ge(m.ystats, made(k - U))
                    dve.wait_ge(y_stored[q], 16 * r + 16)
                    dve.scalar_tensor_tensor(out=y[:, q], in0=psX[q % 2][:, 0:CH], scalar=w.bskip[:, 1:2],
                                             in1=sig[:, q % 2], op0=ALU.add, op1=ALU.mult).then_inc(m.y, 1)

                def ystats(k, q, r):
                    dve.wait_ge(m.y, made(k))
                    dve.bn_stats(w.ystats[:, bass.ds(k * 6, 6)], y[:, q]).then_inc(m.ystats, 1)

                pipeline(dve, NCHUNK, U, [(0, make_h2), (3, make_y), (4, ystats)])

            @block.tensor
            def _(pe):
                def turn(k, q, r):
                    pe.wait_ge(m.h2, made(k))
                    pe.wait_ge(m.rows, made(k - 2))
                    to_rows(pe, psR[q % 2], h2[:, q], w.ident, False, m.turned)

                def skip(k, q, r):
                    pe.wait_ge(m.y, made(k - 2))
                    pe.matmul(psZ[q % 2][:, 0:CH], w.gate_h[:, 1], h2[:, q], start=True, stop=True)
                    pe.matmul(psX[q % 2][:, 0:CH], w.Wskip[:, 1], h2[:, q], start=True, stop=True).then_inc(m.xz, 1)

                pipeline(pe, NCHUNK, U, [(0, turn), (0, skip)])


def dense_last(nc, a, w, scratch, out):
    U = 8
    with phase(nc, "last") as ph:
        yin = ph.sb("yin", [128, 4, CH])
        hin = ph.sb("hin", [128, 4, CH])
        xin = ph.sb("xin", [TILE, 4, TILES, D])
        act1 = ph.sb("act1", [128, 2, CH])
        h3 = ph.sb("h3", [128, 2, CH])
        x1 = ph.sb("x1", [TILE, 8, TILES, D])
        x1b = ph.sb("x1b", [TILE, 8, TILES, D])
        xn = ph.sb("xn", [TILE, 2, TILES, D])
        st = ph.sb("st", [TILE, 2, TILES, 6])
        mv = ph.sb("mv", [TILE, 2, TILES, 2])
        ve = ph.sb("ve", [TILE, 2, TILES])
        rstd = ph.sb("rstd", [TILE, 2, TILES])
        g = ph.sb("g", [128, 2, CH])
        hid = ph.sb("hid", [128, 2, 2, CH])
        o = ph.sb("o", [TILE, 4, TILES, D])
        psR, psT = ph.ps("psR"), ph.ps("psT")
        psH = [[ph.ps(f"psH{s}{h}") for h in range(2)] for s in range(2)]
        psO = [ph.ps(f"psO{s}") for s in range(2)]
        y_loaded, h_loaded, x_loaded = (ph.loaded(n, 4) for n in ("y_loaded", "h_loaded", "x_loaded"))
        x1_stored, x1_stored2 = ph.stored("x1_stored", 8), ph.stored("x1_stored2", 8)
        o_stored, o_stored2 = ph.stored("o_stored", 4), ph.stored("o_stored2", 4)
        names = "bn h3 turned x1 x1b stats seen aggr eps rstd xn xT g hidden hid0 hid1 o_ps o"
        m = Group(**{n: ph.stage(n + "_made") for n in names.split()})
        with nc.Block() as block:
            @block.sync
            def _(sp):
                ph.start(sp)

                def load(k, q, r):
                    q4, r4 = q % 4, 2 * r + q // 4
                    hold(sp, ph.seen, m.bn, made(k - 4))
                    sp.dma_start(yin[:, q4], cols_of(scratch.yT, k * CH)).then_inc(y_loaded[q4], 16)
                    hold(sp, ph.seen, m.h3, made(k - 4))
                    sp.dma_start(hin[:, q4], cols_of(scratch.hT, k * CH)).then_inc(h_loaded[q4], 16)
                    hold(sp, ph.seen, m.x1, made(k - 4))
                    move_rows(sp, flat(xin, q4), rows_of(a["x"], k * CH), x_loaded[q4])

                def store_x1(k, q, r):
                    hold(sp, ph.seen, m.x1, made(k))
                    dst = rows_of(scratch.x1, k * CH)
                    sp.dma_start(dst[0:SPLIT], flat(x1, q)[0:SPLIT]).then_inc(x1_stored[q], 16)
                    sp.dma_start(dst[SPLIT:TILE], flat(x1, q)[SPLIT:TILE]).then_inc(x1_stored2[q], 16)

                def store_o(k, q, r):
                    q4 = q % 4
                    hold(sp, ph.seen, m.o, made(k))
                    dst = rows_of(out, k * CH)
                    sp.dma_start(dst[0:SPLIT], flat(o, q4)[0:SPLIT]).then_inc(o_stored[q4], 16)
                    sp.dma_start(dst[SPLIT:TILE], flat(o, q4)[SPLIT:TILE]).then_inc(o_stored2[q4], 16)

                pipeline(sp, NCHUNK, U, [(0, load), (7, store_x1), (11, store_o)])
                for q in range(8):
                    for sems in (x1_stored, x1_stored2):
                        sp.wait_ge(sems[q], 16 + 16 * len(range(q, NCHUNK, 8)))
                for q in range(4):
                    for sems in (o_stored, o_stored2):
                        sp.wait_ge(sems[q], 16 + 16 * len(range(q, NCHUNK, 4)))

            @block.scalar
            def _(act):
                def bn(k, q, r):
                    q4, r4 = q % 4, 2 * r + q // 4
                    act.wait_ge(y_loaded[q4], 16 * r4 + 16)
                    act.wait_ge(m.h3, made(k - 2))
                    act.activation(act1[:, q % 2], yin[:, q4], ACT.Relu, bias=w.bn[:, 1:2], scale=w.bn[:, 0:1]).then_inc(m.bn, 1)

                def make_g(k, q, r):
                    act.wait_ge(m.xT, made(k))
                    act.wait_ge(m.hidden, made(k - 2))
                    act.activation(g[:, q % 2], psT[:, 0:CH], ACT.Relu).then_inc(m.g, 1)

                def make_hid0(k, q, r):
                    act.wait_ge(m.hidden, made(k))
                    act.wait_ge(m.o_ps, made(k - 2))
                    act.activation(hid[:, q % 2, 0], psH[q % 2][0][:, 0:CH], ACT.Relu, bias=w.b2u[:, 0:1]).then_inc(m.hid0, 1)

                pipeline(act, NCHUNK, U, [(0, bn), (5, make_g), (6, make_hid0)])

            @block.gpsimd
            def _(pool):
                def make_rstd(k, q, r):
                    pool.wait_ge(m.aggr, made(k))
                    pool.wait_ge(m.xn, made(k - 2))
                    pool.tensor_tensor(ve[:, q % 2], mv[:, q % 2, :, 1], w.eps[0:TILE, 0:TILES], ALU.add).then_inc(m.eps, 1)
                    pool.wait_ge(m.eps, made(k))
                    pool.tensor_tensor(rstd[:, q % 2], ve[:, q % 2], w.power[0:TILE, 0:TILES], ALU.pow).then_inc(m.rstd, 1)

                def add_bias(k, q, r):
                    pool.wait_ge(m.x1, made(k))
                    pool.wait_ge(m.o, made(k - 8))
                    pool.tensor_tensor(x1b[:, q], x1[:, q], w.b2b[:].rearrange("p (o f) -> p o f", o=1).to_broadcast([TILE, TILES, D]), ALU.add).then_inc(m.x1b, 1)

                pipeline(pool, NCHUNK, U, [(0, make_rstd), (1, add_bias)])

            @block.vector
            def _(dve):
                def make_h3(k, q, r):
                    q4, r4 = q % 4, 2 * r + q // 4
                    dve.wait_ge(m.bn, made(k))
                    dve.wait_ge(h_loaded[q4], 16 * r4 + 16)
                    dve.wait_ge(m.turned, made(k - 2))
                    dve.tensor_tensor(h3[:, q % 2], act1[:, q % 2], hin[:, q4], ALU.add).then_inc(m.h3, 1)

                def make_x1(k, q, r):
                    q4, r4 = q % 4, 2 * r + q // 4
                    dve.wait_ge(m.turned, made(k))
                    dve.wait_ge(x_loaded[q4], 32 * r4 + 32)
                    dve.wait_ge(x1_stored[q], 16 * r + 16)
                    dve.wait_ge(x1_stored2[q], 16 * r + 16)
                    dve.wait_ge(m.x1b, made(k - 8))
                    dve.tensor_tensor(flat(x1, q), psR[0:TILE], flat(xin, q4), ALU.add).then_inc(m.x1, 1)

                def stats(k, q, r):
                    dve.wait_ge(m.x1, made(k))
                    dve.wait_ge(m.aggr, made(k - 2))
                    norm_stats(dve, x1[:, q], st[:, q % 2], m.stats)

                def aggr(k, q, r):
                    dve.wait_ge(m.stats, made(k))
                    dve.wait_ge(m.xn, made(k - 2))
                    norm_aggr(dve, st[:, q % 2], mv[:, q % 2], m.seen, m.aggr)

                def apply(k, q, r):
                    dve.wait_ge(m.rstd, made(k))
                    dve.wait_ge(m.xT, made(k - 2))
                    norm_apply(dve, xn[:, q % 2], x1[:, q], mv[:, q % 2], rstd[:, q % 2], m.xn)

                def make_hid1(k, q, r):
                    dve.wait_ge(m.hidden, made(k))
                    dve.wait_ge(m.o_ps, made(k - 2))
                    dve.tensor_scalar(hid[:, q % 2, 1], psH[q % 2][1][:, 0:CH], w.b2u[:, 1:2], 0.0, ALU.add, ALU.max).then_inc(m.hid1, 1)

                def make_o(k, q, r):
                    q4, r4 = q % 4, 2 * r + q // 4
                    dve.wait_ge(m.o_ps, made(k))
                    dve.wait_ge(m.x1b, made(k))
                    dve.wait_ge(o_stored[q4], 16 * r4 + 16)
                    dve.wait_ge(o_stored2[q4], 16 * r4 + 16)
                    dve.tensor_tensor(flat(o, q4), psO[q % 2][0:TILE], flat(x1b, q), ALU.add).then_inc(m.o, 1)

                pipeline(dve, NCHUNK, U, [(0, make_h3), (2, make_x1), (8, make_o), (2, stats), (6, make_hid1), (2, aggr), (3, apply)])

            @block.tensor
            def _(pe):
                def turn(k, q, r):
                    pe.wait_ge(m.h3, made(k))
                    pe.wait_ge(m.x1, made(k - 1))
                    to_rows(pe, psR, h3[:, q % 2], w.ident, False, m.turned)

                def turn_back(k, q, r):
                    pe.wait_ge(m.xn, made(k))
                    pe.wait_ge(m.g, made(k - 1))
                    to_T(pe, psT, xn[:, q % 2], w.ident, m.xT)

                def hidden(k, q, r):
                    pe.wait_ge(m.g, made(k))
                    pe.wait_ge(m.hid0, made(k - 2))
                    pe.wait_ge(m.hid1, made(k - 2))
                    for h in range(2):
                        last = pe.matmul(psH[q % 2][h][:, 0:CH], w.W2a[:, 0, h * 128:(h + 1) * 128], g[:, q % 2], start=True, stop=True)
                    last.then_inc(m.hidden, 1)

                def output(k, q, r):
                    pe.wait_ge(m.hid0, made(k))
                    pe.wait_ge(m.hid1, made(k))
                    pe.wait_ge(m.o, made(k - 2))
                    for j in range(TILES):
                        for h in range(2):
                            last = pe.matmul(psO[q % 2][0:TILE, j * D:(j + 1) * D], tile_cols(hid[:, q % 2, h], j, False), w.W2b[:, h],
                                             start=(h == 0), stop=(h == 1))
                    last.then_inc(m.o_ps, 1)

                pipeline(pe, NCHUNK, U, [(0, turn), (3, turn_back), (4, hidden), (6, output)])

def by_edge(t):
    return t.rearrange("f (p j) -> f j p", j=TILES)


def edge_window(scratch, col0):
    return scratch.dst_pad[0:1, bass.ds(col0, CH + 2)].to_broadcast([128, CH + 2])


def index_slot(table, e0):
    return table[bass.ds(e0, CH)].rearrange("(p j) -> p j", j=TILES)


def gather(pool, seen, rows, table, index, sem):
    pool.sem_inc(seen, 1)
    for j in range(TILES):
        pool.indirect_dma_start(rows[:, j], None, table, bass.IndirectOffsetOnAxis(index[:, j:j + 1], 0),
                                bounds_check=table.shape[0] - 1, oob_is_err=False).then_inc(sem, 16)


def scatter_ends(pool, seen, table, rows, index, sem):
    pool.sem_inc(seen, 1)
    for j in range(TILES):
        pool.indirect_dma_start(table, bass.IndirectOffsetOnAxis(index[:, j:j + 1], 0), rows[:, j], None,
                                bounds_check=table.shape[0] - 1, oob_is_err=False).then_inc(sem, 16)


def edge_first(nc, a, w, scratch):
    U = 2
    N2 = 2 * TILES
    with phase(nc, "efirst") as ph:
        di, si, ei = (ph.sb(n, [TILE, U, TILES], I32) for n in ("di", "si", "ei"))
        er = ph.sb("er", [TILE, U, TILES, MAPW], I32)
        x = ph.sb("x", [TILE, U, N2, D])
        xn = ph.sb("xn", [TILE, U, N2, D])
        st = ph.sb("st", [TILE, U, N2, 6])
        mv = ph.sb("mv", [TILE, U, N2, 2])
        ve = ph.sb("ve", [TILE, U, N2])
        rstd = ph.sb("rstd", [TILE, U, N2])
        h0 = ph.sb("h0", [128, U, 2, CH])
        h1 = ph.sb("h1", [128, U, 2, CH])
        win = ph.sb("win", [128, U, CH + 2], I32)
        cont = ph.sb("cont", [128, CH])
        sig = ph.sb("sig", [128, CH])
        yw = ph.sb("yw", [128, U, CH])
        ywn = ph.sb("ywn", [128, CH])
        psT = [ph.ps(f"psT{s}") for s in range(2)]
        psW = [ph.ps(f"psW{s}") for s in range(2)]
        psX, psZ = ph.ps("psX"), ph.ps("psZ")
        idx_loaded, win_loaded = ph.loaded("idx_loaded", U), ph.loaded("win_loaded", U)
        moved = ph.loaded("moved", U)
        xd_stored, hd_stored, hs_stored, yw_stored = (ph.stored(n, U) for n in ("xd_stored", "hd_stored", "hs_stored", "yw_stored"))
        names = "stats aggr_seen aggr eps rstd xn xT h0 w_in h1d h1s xz sig yw cont ywn ywstats"
        m = Group(**{n: ph.stage(n + "_made") for n in names.split()})
        per = 16 * 3 * TILES
        with nc.Block() as block:
            @block.sync
            def _(sp):
                ph.start(sp)

                def load(k, q, r):
                    hold(sp, ph.seen, m.stats, made(k - U))
                    sp.dma_start(di[:, q], index_slot(a["dst"], k * CH)).then_inc(idx_loaded[q], 16)
                    sp.dma_start(si[:, q], index_slot(a["src"], k * CH)).then_inc(idx_loaded[q], 16)
                    sp.dma_start(ei[:, q], index_slot(scratch.end_index, k * CH)).then_inc(idx_loaded[q], 16)
                    sp.dma_start(er[:, q].rearrange("p j w -> p (j w)"), scratch.edge_row[bass.ds(k * CH, CH), :].rearrange(
                        "(p j) w -> p (j w)", j=TILES)).then_inc(idx_loaded[q], 16)
                    hold(sp, ph.seen, m.cont, made(k - U))
                    sp.dma_start(win[:, q], edge_window(scratch, k * CH)).then_inc(win_loaded[q], 16)

                def store_x(k, q, r):
                    hold(sp, ph.seen, moved[q], per * r + per)
                    move_rows(sp, rows_of(scratch.xd, k * CH), x[:, q, 0:TILES].rearrange("p j f -> p (j f)"), xd_stored[q])

                def store_h(k, q, r):
                    hold(sp, ph.seen, m.h1d, made(k))
                    sp.dma_start(cols_of(scratch.hdT, k * CH), h1[:, q, 0]).then_inc(hd_stored[q], 16)
                    hold(sp, ph.seen, m.h1s, made(k))
                    sp.dma_start(cols_of(scratch.hsT, k * CH), h1[:, q, 1]).then_inc(hs_stored[q], 16)

                def store_y(k, q, r):
                    hold(sp, ph.seen, m.yw, made(k))
                    sp.dma_start(cols_of(scratch.ywT, k * CH), yw[:, q]).then_inc(yw_stored[q], 16)

                pipeline(sp, ECHUNK, U, [(0, load), (1, store_x), (2, store_h), (3, store_y)])
                for q in range(U):
                    n = len(range(q, ECHUNK, U))
                    sp.wait_ge(moved[q], per * n)
                    sp.wait_ge(xd_stored[q], 16 + 32 * n)
                    for sems in (hd_stored, hs_stored, yw_stored):
                        sp.wait_ge(sems[q], 16 + 16 * n)

            @block.gpsimd
            def _(pool):
                def fetch(k, q, r):
                    pool.wait_ge(idx_loaded[q], 64 * r + 64)
                    pool.wait_ge(m.xn, made(k - U))
                    pool.wait_ge(xd_stored[q], 32 * r + 16)
                    gather(pool, ph.seen, x[:, q, 0:TILES], a["x"], di[:, q], moved[q])
                    gather(pool, ph.seen, x[:, q, TILES:N2], a["x"], si[:, q], moved[q])
                    scatter_ends(pool, ph.seen, scratch.node_map, er[:, q], ei[:, q], moved[q])

                def make_rstd(k, q, r):
                    pool.wait_ge(m.aggr, made(k))
                    pool.wait_ge(m.xn, made(k - U))
                    pool.tensor_tensor(ve[:, q], mv[:, q, :, 1], w.eps[0:TILE, 0:N2], ALU.add).then_inc(m.eps, 1)
                    pool.wait_ge(m.eps, made(k))
                    pool.tensor_tensor(rstd[:, q], ve[:, q], w.power[0:TILE, 0:N2], ALU.pow).then_inc(m.rstd, 1)

                pipeline(pool, ECHUNK, U, [(0, fetch), (1, make_rstd)])

            @block.vector
            def _(dve):
                def stats(k, q, r):
                    dve.wait_ge(moved[q], per * r + per)
                    dve.wait_ge(m.aggr, made(k - U))
                    norm_stats(dve, x[:, q], st[:, q], m.stats)

                def aggr(k, q, r):
                    dve.wait_ge(m.stats, made(k))
                    dve.wait_ge(m.xn, made(k - U))
                    norm_aggr(dve, st[:, q], mv[:, q], m.aggr_seen, m.aggr)

                def apply(k, q, r):
                    dve.wait_ge(m.rstd, made(k))
                    dve.wait_ge(m.xT, made(k - U))
                    norm_apply(dve, xn[:, q], x[:, q], mv[:, q], rstd[:, q], m.xn)

                def make_h1(k, q, r):
                    dve.wait_ge(m.w_in, made(k))
                    dve.wait_ge(m.xz, made(k - U))
                    dve.wait_ge(hd_stored[q], 16 * r + 16)
                    dve.wait_ge(hs_stored[q], 16 * r + 16)
                    dve.tensor_scalar(h1[:, q, 0], psW[0][:, 0:CH], w.b_in[:, 0:1], 0.0, ALU.add, ALU.max).then_inc(m.h1d, 1)
                    dve.tensor_scalar(h1[:, q, 1], psW[1][:, 0:CH], w.b_in[:, 0:1], 0.0, ALU.add, ALU.max).then_inc(m.h1s, 1)

                def make_cont(k, q, r):
                    dve.wait_ge(win_loaded[q], 16 * r + 16)
                    dve.wait_ge(m.ywn, made(k - 1))
                    dve.tensor_tensor(cont[:], win[:, q, 2:CH + 2], win[:, q, 1:CH + 1], ALU.is_equal).then_inc(m.cont, 1)

                def make_yw(k, q, r):
                    dve.wait_ge(m.sig, made(k))
                    dve.wait_ge(yw_stored[q], 16 * r + 16)
                    dve.scalar_tensor_tensor(out=yw[:, q], in0=psX[:, 0:CH], scalar=w.bskip[:, 0:1],
                                             in1=sig[:], op0=ALU.add, op1=ALU.mult).then_inc(m.yw, 1)
                    dve.wait_ge(m.yw, made(k))
                    dve.wait_ge(m.cont, made(k))
                    dve.wait_ge(m.ywstats, made(k - 1))
                    dve.scalar_tensor_tensor(out=ywn[:], in0=cont[:], scalar=-1.0, in1=yw[:, q], op0=ALU.add, op1=ALU.mult).then_inc(m.ywn, 1)
                    dve.wait_ge(m.ywn, made(k))
                    dve.bn_stats(w.wends[:, bass.ds(k * 6, 6)], ywn[:]).then_inc(m.ywstats, 1)

                pipeline(dve, ECHUNK, U, [(0, stats), (0, aggr), (1, apply), (1, make_h1), (1, make_cont), (1, make_yw)])

            @block.tensor
            def _(pe):
                def turn(k, q, r):
                    pe.wait_ge(m.xn, made(k))
                    pe.wait_ge(m.h0, made(k - 1))
                    for j in range(N2):
                        last = pe.transpose(psT[j // TILES][:, (j % TILES) * TILE:(j % TILES + 1) * TILE], xn[:, q, j], w.ident[0:TILE, 0:TILE])
                    last.then_inc(m.xT, 1)

                def first(k, q, r):
                    pe.wait_ge(m.h0, made(k))
                    pe.wait_ge(m.h1s, made(k - 1))
                    for s in range(2):
                        last = pe.matmul(psW[s][:, 0:CH], w.W_in[:], h0[:, q, s], start=True, stop=True)
                    last.then_inc(m.w_in, 1)

                def skip(k, q, r):
                    pe.wait_ge(m.h1d, made(k))
                    pe.wait_ge(m.yw, made(k - 1))
                    pe.matmul(psZ[:, 0:CH], w.gate_h[:, 0], h1[:, q, 0], start=True, stop=True)
                    pe.matmul(psX[:, 0:CH], w.Wskip[:, 0], h1[:, q, 0], start=True, stop=True).then_inc(m.xz, 1)

                pipeline(pe, ECHUNK, U, [(0, turn), (0, first), (0, skip)])

            @block.scalar
            def _(act):
                def make_h0(k, q, r):
                    act.wait_ge(m.xT, made(k))
                    act.wait_ge(m.w_in, made(k - U))
                    act.activation(by_edge(h0[:, q, 0]), by_tile(psT[0]), ACT.Relu)
                    act.activation(by_edge(h0[:, q, 1]), by_tile(psT[1]), ACT.Relu).then_inc(m.h0, 1)

                def make_sig(k, q, r):
                    act.wait_ge(m.xz, made(k))
                    act.wait_ge(m.yw, made(k - 1))
                    act.activation(sig[:], psZ[:, 0:CH], ACT.Sigmoid, bias=w.gate_b[:, 0:1]).then_inc(m.sig, 1)

                pipeline(act, ECHUNK, U, [(0, make_h0), (0, make_sig)])


def map_sources(nc, a, scratch):
    U = 2
    with phase(nc, "map") as ph:
        si = ph.sb("si", [TILE, U, TILES], I32)
        rows = ph.sb("rows", [TILE, U, TILES, MAPW], I32)
        sr = ph.sb("sr", [TILE, U, TILES], I32)
        idx_loaded = ph.loaded("idx_loaded", U)
        moved, stored = ph.loaded("moved", U), ph.stored("stored", U)
        taken = ph.stage("taken")
        per = 16 * TILES
        with nc.Block() as block:
            @block.sync
            def _(sp):
                ph.start(sp)

                def load(k, q, r):
                    hold(sp, ph.seen, taken, made(k - U))
                    sp.dma_start(si[:, q], index_slot(a["src"], k * CH)).then_inc(idx_loaded[q], 16)

                def store(k, q, r):
                    hold(sp, ph.seen, taken, made(k))
                    sp.dma_start(index_slot(scratch.src_row, k * CH), sr[:, q]).then_inc(stored[q], 16)

                pipeline(sp, ECHUNK, U, [(0, load), (1, store)])
                for q in range(U):
                    sp.wait_ge(stored[q], 16 + 16 * len(range(q, ECHUNK, U)))

            @block.gpsimd
            def _(pool):
                def fetch(k, q, r):
                    pool.wait_ge(idx_loaded[q], 16 * r + 16)
                    pool.wait_ge(taken, made(k - U))
                    gather(pool, ph.seen, rows[:, q], scratch.node_map, si[:, q], moved[q])
                pipeline(pool, ECHUNK, U, [(0, fetch)])

            @block.vector
            def _(dve):
                def take(k, q, r):
                    dve.wait_ge(moved[q], per * r + per)
                    dve.wait_ge(stored[q], 16 * r + 16)
                    dve.tensor_copy(sr[:, q], rows[:, q, :, 0]).then_inc(taken, 1)
                pipeline(dve, ECHUNK, U, [(0, take)])


def attention(nc, a, w, scratch, l):
    U = 2
    with phase(nc, f"att{l}") as ph:
        hd, hs = ph.sb("hd", [128, U, CH]), ph.sb("hs", [128, U, CH])
        ew = ph.sb("ew", [1, U, CH])
        win = ph.sb("win", [128, U, CH + 2], I32)
        qs, prod = ph.sb("qs", [128, U, CH]), ph.sb("prod", [128, U, CH])
        cont, apart = ph.sb("cont", [128, U, CH + 1]), ph.sb("apart", [128, U, CH])
        mx = ph.sb("mx", [128, U, CH + 1])
        ex, ee = ph.sb("ex", [128, U, 2, CH]), ph.sb("ee", [128, U, 2, CH])
        keep, pv = ph.sb("keep", [128, U, CH]), ph.sb("pv", [128, U, CH])
        den, num, rden = (ph.sb(n, [128, U, CH]) for n in ("den", "num", "rden"))
        o, th, dx, gx, y, yn = (ph.sb(n, [128, U, CH]) for n in ("o", "th", "dx", "gx", "y", "yn"))
        psQ, psK, psV, psA, psX, psZ = (ph.ps(n) for n in ("psQ", "psK", "psV", "psA", "psX", "psZ"))
        in_loaded = ph.loaded("in_loaded", U)
        yn_stored = ph.stored("yn_stored", U)
        names = "qkv qs prod score cont apart mx0 mx ex ee keep pv den num rden o xz th dx gx y yn ystats init"
        m = Group(**{n: ph.stage(n + "_made") for n in names.split()})
        with nc.Block() as block:
            @block.sync
            def _(sp):
                ph.start(sp)

                def load(k, q, r):
                    hold(sp, ph.seen, m.xz, made(k - U))
                    sp.dma_start(hd[:, q], cols_of(scratch.hdT, k * CH)).then_inc(in_loaded[q], 16)
                    sp.dma_start(hs[:, q], cols_of(scratch.hsT, k * CH)).then_inc(in_loaded[q], 16)
                    sp.dma_start(ew[:, q], a["edge_weight1"][bass.ds(k * CH, CH), :].rearrange("e o -> o e")).then_inc(in_loaded[q], 16)
                    hold(sp, ph.seen, m.cont, made(k - U))
                    sp.dma_start(win[:, q], edge_window(scratch, k * CH)).then_inc(in_loaded[q], 16)

                def store(k, q, r):
                    hold(sp, ph.seen, m.yn, made(k))
                    sp.dma_start(cols_of(scratch.ydT, k * CH), yn[:, q]).then_inc(yn_stored[q], 16)

                pipeline(sp, ECHUNK, U, [(0, load), (1, store)])
                for q in range(U):
                    sp.wait_ge(yn_stored[q], 16 + 16 * len(range(q, ECHUNK, U)))

            @block.tensor
            def _(pe):
                def qkv(k, q, r):
                    pe.wait_ge(in_loaded[q], 64 * r + 64)
                    pe.wait_ge(m.pv, made(k - 1))
                    pe.matmul(psQ[:, 0:CH], w.Wq[:, l], hd[:, q], start=True, stop=True)
                    pe.matmul(psK[:, 0:CH], w.Wk[:, l], hs[:, q], start=True, stop=False)
                    pe.matmul(psK[:, 0:CH], w.We[:, l], ew[:, q], start=False, stop=True)
                    pe.matmul(psV[:, 0:CH], w.Wv[:, l], hs[:, q], start=True, stop=False)
                    pe.matmul(psV[:, 0:CH], w.We[:, l], ew[:, q], start=False, stop=True).then_inc(m.qkv, 1)

                def score(k, q, r):
                    pe.wait_ge(m.prod, made(k))
                    pe.wait_ge(m.ex, made(k - 1))
                    pe.matmul(psA[:, 0:CH], w.heads[:], prod[:, q], start=True, stop=True).then_inc(m.score, 1)

                def skip(k, q, r):
                    pe.wait_ge(m.dx, made(k - 1))
                    pe.wait_ge(m.th, made(k - 1))
                    pe.wait_ge(m.o, made(k))
                    pe.matmul(psX[:, 0:CH], w.Wskip[:, l], hd[:, q], start=True, stop=True)
                    pe.matmul(psZ[:, 0:CH], w.gate_h[:, l], hd[:, q], start=True, stop=False)
                    pe.matmul(psZ[:, 0:CH], w.gate_out[:, l], o[:, q], start=False, stop=True).then_inc(m.xz, 1)

                pipeline(pe, ECHUNK, U, [(0, qkv), (0, score), (0, skip)])

            @block.scalar
            def _(act):
                def step(k, q, r):
                    act.wait_ge(m.qkv, made(k))
                    act.wait_ge(m.prod, made(k - U))
                    act.activation(qs[:, q], psQ[:, 0:CH], ACT.Identity, bias=w.bq[:, l:l + 1]).then_inc(m.qs, 1)
                    act.wait_ge(m.ex, made(k))
                    act.wait_ge(m.pv, made(k - U))
                    act.wait_ge(m.den, made(k - U))
                    act.activation(ee[:, q].rearrange("p a e -> p (a e)"), ex[:, q].rearrange("p a e -> p (a e)"), ACT.Exp).then_inc(m.ee, 1)
                    act.wait_ge(m.xz, made(k))
                    act.wait_ge(m.gx, made(k - U))
                    act.activation(th[:, q], psZ[:, 0:CH], ACT.Tanh, bias=w.gate_bh[:, l:l + 1], scale=0.5).then_inc(m.th, 1)
                pipeline(act, ECHUNK, U, [(0, step)])

            @block.vector
            def _(dve):
                dve.memset(mx[:, U - 1, CH:CH + 1], 0.0)
                dve.memset(den[:, U - 1, CH - 1:CH], 0.0)
                dve.memset(num[:, U - 1, CH - 1:CH], 0.0).then_inc(m.init, 1)
                dve.wait_ge(m.init, made(0))

                def step(k, q, r):
                    p = 1 - q
                    dve.wait_ge(in_loaded[q], 64 * r + 64)
                    dve.tensor_tensor(cont[:, q], win[:, q, 1:CH + 2], win[:, q, 0:CH + 1], ALU.is_equal).then_inc(m.cont, 1)
                    dve.wait_ge(m.cont, made(k))
                    dve.tensor_scalar(apart[:, q], cont[:, q, 0:CH], -1.0, BIG, ALU.add, ALU.mult).then_inc(m.apart, 1)
                    dve.wait_ge(m.mx, made(k - 1))
                    dve.tensor_copy(mx[:, q, 0:1], mx[:, p, CH:CH + 1]).then_inc(m.mx0, 1)
                    dve.wait_ge(m.qs, made(k))
                    dve.wait_ge(m.score, made(k - U))
                    dve.scalar_tensor_tensor(out=prod[:, q], in0=psK[:, 0:CH], scalar=w.bk[:, l:l + 1], in1=qs[:, q],
                                             op0=ALU.add, op1=ALU.mult).then_inc(m.prod, 1)
                    dve.wait_ge(m.score, made(k))
                    dve.wait_ge(m.apart, made(k))
                    dve.wait_ge(m.mx0, made(k))
                    dve.tensor_tensor_scan(mx[:, q, 1:CH + 1], apart[:, q], psA[:, 0:CH], mx[:, q, 0:1], ALU.add, ALU.max).then_inc(m.mx, 1)
                    dve.wait_ge(m.mx, made(k))
                    dve.wait_ge(m.ee, made(k - U))
                    dve.tensor_tensor(ex[:, q, 0], mx[:, q, 0:CH], mx[:, q, 1:CH + 1], ALU.subtract)
                    dve.tensor_tensor(ex[:, q, 1], psA[:, 0:CH], mx[:, q, 1:CH + 1], ALU.subtract).then_inc(m.ex, 1)
                    dve.wait_ge(m.ee, made(k))
                    dve.scalar_tensor_tensor(out=keep[:, q], in0=ee[:, q, 0], scalar=1.0, in1=cont[:, q, 0:CH],
                                             op0=ALU.min, op1=ALU.mult).then_inc(m.keep, 1)
                    dve.scalar_tensor_tensor(out=pv[:, q], in0=psV[:, 0:CH], scalar=w.bv[:, l:l + 1], in1=ee[:, q, 1],
                                             op0=ALU.add, op1=ALU.mult).then_inc(m.pv, 1)
                    dve.wait_ge(m.keep, made(k))
                    dve.wait_ge(m.den, made(k - 1))
                    dve.tensor_tensor_scan(den[:, q], keep[:, q], ee[:, q, 1], den[:, p, CH - 1:CH], ALU.mult, ALU.add).then_inc(m.den, 1)
                    dve.wait_ge(m.pv, made(k))
                    dve.wait_ge(m.num, made(k - 1))
                    dve.tensor_tensor_scan(num[:, q], keep[:, q], pv[:, q], num[:, p, CH - 1:CH], ALU.mult, ALU.add).then_inc(m.num, 1)
                    dve.wait_ge(m.den, made(k))
                    dve.reciprocal(rden[:, q], den[:, q]).then_inc(m.rden, 1)
                    dve.wait_ge(m.rden, made(k))
                    dve.wait_ge(m.num, made(k))
                    dve.wait_ge(m.xz, made(k - U))
                    dve.tensor_tensor(o[:, q], num[:, q], rden[:, q], ALU.mult).then_inc(m.o, 1)
                    dve.wait_ge(m.xz, made(k))
                    dve.wait_ge(m.o, made(k))
                    dve.scalar_tensor_tensor(out=dx[:, q], in0=psX[:, 0:CH], scalar=w.bskip[:, l:l + 1], in1=o[:, q],
                                             op0=ALU.add, op1=ALU.subtract).then_inc(m.dx, 1)
                    dve.wait_ge(m.th, made(k))
                    dve.wait_ge(m.dx, made(k))
                    dve.scalar_tensor_tensor(out=gx[:, q], in0=th[:, q], scalar=1.0, in1=dx[:, q], op0=ALU.add, op1=ALU.mult).then_inc(m.gx, 1)
                    dve.wait_ge(m.gx, made(k))
                    dve.scalar_tensor_tensor(out=y[:, q], in0=gx[:, q], scalar=0.5, in1=o[:, q], op0=ALU.mult, op1=ALU.add).then_inc(m.y, 1)
                    dve.wait_ge(m.y, made(k))
                    dve.wait_ge(yn_stored[q], 16 * r + 16)
                    dve.scalar_tensor_tensor(out=yn[:, q], in0=cont[:, q, 1:CH + 1], scalar=-1.0, in1=y[:, q], op0=ALU.add, op1=ALU.mult).then_inc(m.yn, 1)
                    dve.wait_ge(m.yn, made(k))
                    dve.bn_stats(w.ends[:, bass.ds(k * 6, 6)], yn[:, q]).then_inc(m.ystats, 1)

                pipeline(dve, ECHUNK, U, [(0, step)])


def edge_update(nc, a, w, scratch, l):
    U = 2
    with phase(nc, f"upd{l}") as ph:
        yn, hd, yw = (ph.sb(n, [128, U, CH]) for n in ("yn", "hd", "yw"))
        xd = ph.sb("xd", [TILE, U, TILES, D])
        win = ph.sb("win", [128, U, CH + 2], I32)
        cont = ph.sb("cont", [128, U, CH])
        yb, act1, hn = (ph.sb(n, [128, U, CH]) for n in ("yb", "act1", "hn"))
        actw, hw, sig, yw2, ywn = (ph.sb(n, [128, U, CH]) for n in ("actw", "hw", "sig", "yw2", "ywn"))
        rows = ph.sb("rows", [TILE, U, TILES, D])
        psR = [ph.ps(f"psR{s}") for s in range(U)]
        psX = [ph.ps(f"psX{s}") for s in range(U)]
        psZ = [ph.ps(f"psZ{s}") for s in range(U)]
        in_loaded = ph.loaded("in_loaded", U)
        hn_stored, rows_stored = ph.stored("hn_stored", U), ph.stored("rows_stored", U)
        names = "cont yb bn hn turned rows bnw hw xz sig yw2 ywn ywstats init"
        m = Group(**{n: ph.stage(n + "_made") for n in names.split()})
        table = scratch.h2 if l == 0 else scratch.x1
        last_of_slot = m.ywstats if l == 0 else m.rows
        col = lambda k: (ECHUNK - 1) * CH - k * CH
        with nc.Block() as block:
            @block.sync
            def _(sp):
                ph.start(sp)

                def load(k, q, r):
                    hold(sp, ph.seen, last_of_slot, made(k - U))
                    hold(sp, ph.seen, m.hn, made(k - U))
                    sp.dma_start(yn[:, q], cols_of(scratch.ydT, col(k))).then_inc(in_loaded[q], 16)
                    sp.dma_start(hd[:, q], cols_of(scratch.hdT, col(k))).then_inc(in_loaded[q], 16)
                    sp.dma_start(win[:, q], edge_window(scratch, col(k))).then_inc(in_loaded[q], 16)
                    if l == 0:
                        sp.dma_start(yw[:, q], cols_of(scratch.ywT, col(k))).then_inc(in_loaded[q], 16)
                    else:
                        sp.dma_start(flat(xd, q), rows_of(scratch.xd, col(k))).then_inc(in_loaded[q], 16)

                def store(k, q, r):
                    hold(sp, ph.seen, m.hn, made(k))
                    sp.dma_start(cols_of(scratch.hdT, col(k)), hn[:, q]).then_inc(hn_stored[q], 16)
                    hold(sp, ph.seen, m.rows, made(k))
                    move_rows(sp, rows_of(table, NODES + (ECHUNK - 1) * CH - k * CH), flat(rows, q), rows_stored[q])

                pipeline(sp, ECHUNK, U, [(0, load), (1, store)])
                for q in range(U):
                    sp.wait_ge(hn_stored[q], 16 + 16 * len(range(q, ECHUNK, U)))
                    sp.wait_ge(rows_stored[q], 16 + 32 * len(range(q, ECHUNK, U)))

            @block.vector
            def _(dve):
                dve.memset(yb[:, U - 1, 0:1], 0.0).then_inc(m.init, 1)
                dve.wait_ge(m.init, made(0))

                def spread(k, q, r):
                    dve.wait_ge(in_loaded[q], 64 * r + 64)
                    dve.tensor_tensor(cont[:, q], win[:, q, 2:CH + 2], win[:, q, 1:CH + 1], ALU.is_equal).then_inc(m.cont, 1)
                    dve.wait_ge(m.cont, made(k))
                    dve.wait_ge(m.yb, made(k - 1))
                    dve.wait_ge(m.bn, made(k - U))
                    dve.tensor_tensor_scan(yb[:, q, ::-1], cont[:, q, ::-1], yn[:, q, ::-1], yb[:, 1 - q, 0:1],
                                           ALU.mult, ALU.subtract).then_inc(m.yb, 1)

                def make_h(k, q, r):
                    dve.wait_ge(m.bn, made(k))
                    dve.wait_ge(hn_stored[q], 16 * r + 16)
                    dve.wait_ge(m.turned, made(k - U))
                    dve.tensor_tensor(hn[:, q], act1[:, q], hd[:, q], ALU.add).then_inc(m.hn, 1)
                    if l == 0:
                        dve.wait_ge(m.bnw, made(k))
                        dve.wait_ge(m.xz, made(k - U))
                        dve.tensor_tensor(hw[:, q], actw[:, q], hd[:, q], ALU.add).then_inc(m.hw, 1)
                    else:
                        dve.wait_ge(m.turned, made(k))
                        dve.wait_ge(rows_stored[q], 32 * r + 16)
                        dve.tensor_tensor(flat(rows, q), psR[q][0:TILE], flat(xd, q), ALU.add).then_inc(m.rows, 1)

                def make_y(k, q, r):
                    dve.wait_ge(m.sig, made(k))
                    dve.scalar_tensor_tensor(out=yw2[:, q], in0=psX[q][:, 0:CH], scalar=w.bskip[:, 1:2],
                                             in1=sig[:, q], op0=ALU.add, op1=ALU.mult).then_inc(m.yw2, 1)
                    dve.wait_ge(m.yw2, made(k))
                    dve.scalar_tensor_tensor(out=ywn[:, q], in0=cont[:, q], scalar=-1.0, in1=yw2[:, q], op0=ALU.add, op1=ALU.mult).then_inc(m.ywn, 1)
                    dve.wait_ge(m.ywn, made(k))
                    dve.bn_stats(w.wends[:, bass.ds(k * 6, 6)], ywn[:, q]).then_inc(m.ywstats, 1)

                pipeline(dve, ECHUNK, U, [(0, spread), (0, make_h)] + [(0, make_y)] * (l == 0))

            @block.scalar
            def _(act):
                def bn(k, q, r):
                    act.wait_ge(m.yb, made(k))
                    act.wait_ge(m.hn, made(k - U))
                    act.activation(act1[:, q], yb[:, q], ACT.Relu, bias=w.bn[:, 1:2], scale=w.bn[:, 0:1]).then_inc(m.bn, 1)
                    if l == 0:
                        act.wait_ge(m.hw, made(k - U))
                        act.activation(actw[:, q], yw[:, q], ACT.Relu, bias=w.bn[:, 1:2], scale=w.bn[:, 0:1]).then_inc(m.bnw, 1)
                        act.wait_ge(m.xz, made(k))
                        act.wait_ge(m.yw2, made(k - U))
                        act.activation(sig[:, q], psZ[q][:, 0:CH], ACT.Sigmoid, bias=w.gate_b[:, 1:2]).then_inc(m.sig, 1)
                        act.wait_ge(m.turned, made(k))
                        act.wait_ge(rows_stored[q], 32 * r + 16)
                        act.copy(flat(rows, q), psR[q][0:TILE]).then_inc(m.rows, 1)
                pipeline(act, ECHUNK, U, [(0, bn)])

            @block.tensor
            def _(pe):
                def turn(k, q, r):
                    pe.wait_ge(m.hn, made(k))
                    pe.wait_ge(m.rows, made(k - U))
                    to_rows(pe, psR[q], hn[:, q], w.ident, True, m.turned)
                    if l == 0:
                        pe.wait_ge(m.hw, made(k))
                        pe.wait_ge(m.yw2, made(k - U))
                        pe.matmul(psZ[q][:, 0:CH], w.gate_h[:, 1], hw[:, q], start=True, stop=True)
                        pe.matmul(psX[q][:, 0:CH], w.Wskip[:, 1], hw[:, q], start=True, stop=True).then_inc(m.xz, 1)
                pipeline(pe, ECHUNK, U, [(0, turn)])


def edge_sources(nc, a, w, scratch):
    U = 2
    with phase(nc, "esrc") as ph:
        si = ph.sb("si", [TILE, U, TILES], I32)
        rows = ph.sb("rows", [TILE, U, TILES, D])
        hs = ph.sb("hs", [128, U, CH])
        psT = [ph.ps(f"psT{s}") for s in range(U)]
        idx_loaded = ph.loaded("idx_loaded", U)
        moved, stored = ph.loaded("moved", U), ph.stored("stored", U)
        m = Group(xT=ph.stage("xT_made"), hs=ph.stage("hs_made"))
        per = 16 * TILES
        with nc.Block() as block:
            @block.sync
            def _(sp):
                ph.start(sp)

                def load(k, q, r):
                    hold(sp, ph.seen, m.xT, made(k - U))
                    sp.dma_start(si[:, q], index_slot(scratch.src_row, k * CH)).then_inc(idx_loaded[q], 16)

                def store(k, q, r):
                    hold(sp, ph.seen, m.hs, made(k))
                    sp.dma_start(cols_of(scratch.hsT, k * CH), hs[:, q]).then_inc(stored[q], 16)

                pipeline(sp, ECHUNK, U, [(0, load), (1, store)])
                for q in range(U):
                    sp.wait_ge(stored[q], 16 + 16 * len(range(q, ECHUNK, U)))

            @block.gpsimd
            def _(pool):
                def fetch(k, q, r):
                    pool.wait_ge(idx_loaded[q], 16 * r + 16)
                    pool.wait_ge(m.xT, made(k - U))
                    gather(pool, ph.seen, rows[:, q], scratch.h2, si[:, q], moved[q])
                pipeline(pool, ECHUNK, U, [(0, fetch)])

            @block.tensor
            def _(pe):
                def turn(k, q, r):
                    pe.wait_ge(moved[q], per * r + per)
                    pe.wait_ge(m.hs, made(k - U))
                    to_T(pe, psT[q], rows[:, q], w.ident, m.xT)
                pipeline(pe, ECHUNK, U, [(0, turn)])

            @block.scalar
            def _(act):
                def copy(k, q, r):
                    act.wait_ge(m.xT, made(k))
                    act.wait_ge(stored[q], 16 * r + 16)
                    act.activation(by_edge(hs[:, q]), by_tile(psT[q]), ACT.Identity).then_inc(m.hs, 1)
                pipeline(act, ECHUNK, U, [(0, copy)])


def edge_last(nc, a, w, scratch, out):
    U = 2
    N2 = 2 * TILES
    with phase(nc, "elast") as ph:
        si, ei, ends = (ph.sb(n, [TILE, U, TILES], I32) for n in ("si", "ei", "ends"))
        x = ph.sb("x", [TILE, U, N2, D])
        xb = ph.sb("xb", [TILE, U, TILES, D])
        ea = ph.sb("ea", [TILE, U, TILES, D])
        xn = ph.sb("xn", [TILE, U, N2, D])
        st = ph.sb("st", [TILE, U, N2, 6])
        mv = ph.sb("mv", [TILE, U, N2, 2])
        ve = ph.sb("ve", [TILE, U, N2])
        rstd = ph.sb("rstd", [TILE, U, N2])
        g = ph.sb("g", [128, U, 3, CH])
        win = ph.sb("win", [128, U, CH + 2], I32)
        ones, cont = ph.sb("ones", [128, CH]), ph.sb("cont", [128, U, CH])
        hid, hid2 = ph.sb("hid", [128, 2, CH]), ph.sb("hid2", [128, 2, CH])
        msg, tot, cnt = (ph.sb(n, [128, U, CH]) for n in ("msg", "tot", "cnt"))
        rcnt, mean = ph.sb("rcnt", [128, CH]), ph.sb("mean", [128, U, CH])
        o = ph.sb("o", [TILE, U, TILES, D])
        psT = [ph.ps(f"psT{s}") for s in range(3)]
        psH = [ph.ps(f"psH{s}") for s in range(2)]
        psM, psO = ph.ps("psM"), ph.ps("psO")
        idx_loaded, in_loaded, x_loaded = (ph.loaded(n, U) for n in ("idx_loaded", "in_loaded", "x_loaded"))
        moved, placed = ph.loaded("moved", U), ph.loaded("placed", U)
        names = "ends xb stats aggr_seen aggr eps rstd xn xT g cont hid0 hid1 hidden psm msg tot cnt rcnt mean hidden2 hid20 hid21 o_ps o init"
        m = Group(**{n: ph.stage(n + "_made") for n in names.split()})
        per = 16 * TILES
        with nc.Block() as block:
            @block.sync
            def _(sp):
                ph.start(sp)

                def load(k, q, r):
                    hold(sp, ph.seen, m.ends, made(k - U))
                    sp.dma_start(si[:, q], index_slot(scratch.src_row, k * CH)).then_inc(idx_loaded[q], 16)
                    sp.dma_start(ei[:, q], index_slot(scratch.end_index, k * CH)).then_inc(idx_loaded[q], 16)
                    hold(sp, ph.seen, m.o, made(k - U))
                    sp.dma_start(x[:, q, 0:TILES].rearrange("p j f -> p (j f)"), rows_of(scratch.x1, NODES + k * CH)).then_inc(x_loaded[q], 16)
                    sp.dma_start(flat(ea, q), rows_of(a["edge_attr_128"], k * CH)).then_inc(in_loaded[q], 16)
                    sp.dma_start(win[:, q], edge_window(scratch, k * CH)).then_inc(in_loaded[q], 16)
                pipeline(sp, ECHUNK, U, [(0, load)])

            @block.gpsimd
            def _(pool):
                pool.memset(ones[:], 1.0).then_inc(m.init, 1)

                def fetch(k, q, r):
                    pool.wait_ge(idx_loaded[q], 32 * r + 32)
                    pool.wait_ge(m.xn, made(k - U))
                    gather(pool, ph.seen, x[:, q, TILES:N2], scratch.x1, si[:, q], moved[q])

                def make_rstd(k, q, r):
                    pool.wait_ge(m.aggr, made(k))
                    pool.wait_ge(m.xn, made(k - U))
                    pool.tensor_tensor(ve[:, q], mv[:, q, :, 1], w.eps[0:TILE, 0:N2], ALU.add).then_inc(m.eps, 1)
                    pool.wait_ge(m.eps, made(k))
                    pool.tensor_tensor(rstd[:, q], ve[:, q], w.power[0:TILE, 0:N2], ALU.pow).then_inc(m.rstd, 1)

                def add_bias(k, q, r):
                    pool.wait_ge(x_loaded[q], 16 * r + 16)
                    pool.wait_ge(m.o, made(k - U))
                    pool.tensor_tensor(xb[:, q], x[:, q, 0:TILES], w.b2b[:].rearrange("p (o f) -> p o f", o=1).to_broadcast([TILE, TILES, D]), ALU.add).then_inc(m.xb, 1)

                def place(k, q, r):
                    if not (isinstance(r, int) and r == 0):
                        pool.wait_ge(placed[q], per * r)
                    pool.sem_inc(ph.seen, 1)
                    pool.tensor_copy(ends[:, q], ei[:, q]).then_inc(m.ends, 1)
                    pool.wait_ge(m.ends, made(k))
                    pool.wait_ge(m.o, made(k))
                    scatter_ends(pool, ph.seen, out, o[:, q], ends[:, q], placed[q])

                pipeline(pool, ECHUNK, U, [(0, fetch), (0, make_rstd), (0, add_bias), (1, place)], peel=U)
                for q in range(U):
                    pool.wait_ge(placed[q], per * len(range(q, ECHUNK, U)))

            @block.vector
            def _(dve):
                dve.memset(tot[:, U - 1, CH - 1:CH], 0.0)
                dve.memset(cnt[:, U - 1, CH - 1:CH], 0.0).then_inc(m.init, 1)
                dve.wait_ge(m.init, made(1))

                def norm(k, q, r):
                    dve.wait_ge(moved[q], per * r + per)
                    dve.wait_ge(x_loaded[q], 16 * r + 16)
                    dve.wait_ge(m.aggr, made(k - U))
                    norm_stats(dve, x[:, q], st[:, q], m.stats)
                    dve.wait_ge(m.stats, made(k))
                    dve.wait_ge(m.xn, made(k - U))
                    norm_aggr(dve, st[:, q], mv[:, q], m.aggr_seen, m.aggr)
                    dve.wait_ge(in_loaded[q], 32 * r + 32)
                    dve.tensor_tensor(cont[:, q], win[:, q, 1:CH + 1], win[:, q, 0:CH], ALU.is_equal).then_inc(m.cont, 1)
                    dve.wait_ge(m.cont, made(k))
                    dve.wait_ge(m.cnt, made(k - 1))
                    dve.tensor_tensor_scan(cnt[:, q], cont[:, q], ones[:], cnt[:, 1 - q, CH - 1:CH], ALU.mult, ALU.add).then_inc(m.cnt, 1)
                    dve.wait_ge(m.cnt, made(k))
                    dve.wait_ge(m.mean, made(k - 1))
                    dve.reciprocal(rcnt[:], cnt[:, q]).then_inc(m.rcnt, 1)
                    dve.wait_ge(m.rstd, made(k))
                    dve.wait_ge(m.xT, made(k - U))
                    norm_apply(dve, xn[:, q], x[:, q], mv[:, q], rstd[:, q], m.xn)

                def finish(k, q, r):
                    dve.wait_ge(m.hidden, made(k))
                    dve.wait_ge(m.psm, made(k - 1))
                    dve.tensor_scalar(hid[:, 1], psH[1][:, 0:CH], w.b1a[:, 1:2], 0.0, ALU.add, ALU.max).then_inc(m.hid1, 1)
                    dve.wait_ge(m.msg, made(k))
                    dve.wait_ge(m.tot, made(k - 1))
                    dve.tensor_tensor_scan(tot[:, q], cont[:, q], msg[:, q], tot[:, 1 - q, CH - 1:CH], ALU.mult, ALU.add).then_inc(m.tot, 1)
                    dve.wait_ge(m.tot, made(k))
                    dve.wait_ge(m.rcnt, made(k))
                    dve.wait_ge(m.hidden2, made(k - U))
                    dve.tensor_tensor(mean[:, q], tot[:, q], rcnt[:], ALU.mult).then_inc(m.mean, 1)
                    dve.wait_ge(m.hidden2, made(k))
                    dve.wait_ge(m.o_ps, made(k - 1))
                    dve.tensor_scalar(hid2[:, 1], psH[1][:, 0:CH], w.b2u[:, 1:2], 0.0, ALU.add, ALU.max).then_inc(m.hid21, 1)
                    dve.wait_ge(m.o_ps, made(k))
                    dve.wait_ge(m.xb, made(k))
                    if not (isinstance(r, int) and r == 0):
                        dve.wait_ge(placed[q], per * r)
                    dve.tensor_tensor(flat(o, q), psO[0:TILE], flat(xb, q), ALU.add).then_inc(m.o, 1)

                pipeline(dve, ECHUNK, U, [(0, norm), (0, finish)], peel=U)

            @block.tensor
            def _(pe):
                def step(k, q, r):
                    pe.wait_ge(m.xn, made(k))
                    pe.wait_ge(in_loaded[q], 32 * r + 32)
                    pe.wait_ge(m.g, made(k - 1))
                    for j in range(TILES):
                        for s, src in enumerate((xn[:, q, j], xn[:, q, TILES + j], ea[:, q, j])):
                            last = pe.transpose(psT[s][:, j * TILE:(j + 1) * TILE], src, w.ident[0:TILE, 0:TILE])
                    last.then_inc(m.xT, 1)
                    pe.wait_ge(m.g, made(k))
                    pe.wait_ge(m.hid20, made(k - 1))
                    pe.wait_ge(m.hid21, made(k - 1))
                    for h in range(2):
                        pe.matmul(psH[h][:, 0:CH], w.W1a[:, 0, h * 128:(h + 1) * 128], g[:, q, 1], start=True, stop=False)
                        last = pe.matmul(psH[h][:, 0:CH], w.W1a[:, 1, h * 128:(h + 1) * 128], g[:, q, 2], start=False, stop=True)
                    last.then_inc(m.hidden, 1)
                    pe.wait_ge(m.hid0, made(k))
                    pe.wait_ge(m.hid1, made(k))
                    pe.wait_ge(m.msg, made(k - 1))
                    pe.matmul(psM[:, 0:CH], w.W1b[:, 0], hid[:, 0], start=True, stop=False)
                    pe.matmul(psM[:, 0:CH], w.W1b[:, 1], hid[:, 1], start=False, stop=True).then_inc(m.psm, 1)
                    pe.wait_ge(m.mean, made(k))
                    for h in range(2):
                        pe.matmul(psH[h][:, 0:CH], w.W2a[:, 0, h * 128:(h + 1) * 128], g[:, q, 0], start=True, stop=False)
                        last = pe.matmul(psH[h][:, 0:CH], w.W2a[:, 1, h * 128:(h + 1) * 128], mean[:, q], start=False, stop=True)
                    last.then_inc(m.hidden2, 1)
                    pe.wait_ge(m.hid20, made(k))
                    pe.wait_ge(m.hid21, made(k))
                    pe.wait_ge(m.o, made(k - 1))
                    for j in range(TILES):
                        for h in range(2):
                            last = pe.matmul(psO[0:TILE, j * D:(j + 1) * D], tile_cols(hid2[:, h], j, True), w.W2b[:, h],
                                             start=(h == 0), stop=(h == 1))
                    last.then_inc(m.o_ps, 1)
                pipeline(pe, ECHUNK, U, [(0, step)])

            @block.scalar
            def _(act):
                def step(k, q, r):
                    act.wait_ge(m.xT, made(k))
                    act.wait_ge(m.hidden2, made(k - U))
                    act.activation(by_edge(g[:, q, 0]), by_tile(psT[0]), ACT.Relu)
                    act.activation(by_edge(g[:, q, 1]), by_tile(psT[1]), ACT.Relu)
                    act.activation(by_edge(g[:, q, 2]), by_tile(psT[2]), ACT.Identity).then_inc(m.g, 1)
                    act.wait_ge(m.hidden, made(k))
                    act.wait_ge(m.psm, made(k - 1))
                    act.activation(hid[:, 0], psH[0][:, 0:CH], ACT.Relu, bias=w.b1a[:, 0:1]).then_inc(m.hid0, 1)
                    act.wait_ge(m.psm, made(k))
                    act.wait_ge(m.tot, made(k - U))
                    act.activation(msg[:, q], psM[:, 0:CH], ACT.Identity, bias=w.b1b[:, 0:1]).then_inc(m.msg, 1)
                    act.wait_ge(m.hidden2, made(k))
                    act.wait_ge(m.o_ps, made(k - 1))
                    act.activation(hid2[:, 0], psH[0][:, 0:CH], ACT.Relu, bias=w.b2u[:, 0:1]).then_inc(m.hid20, 1)
                pipeline(act, ECHUNK, U, [(0, step)])


def program(nc, a, out):
    dram = lambda n, s, d=F32: nc.dram_tensor(n, s, d, kind="Internal").ap()
    scratch = Group(
        dst_pad=dram("dst_pad", (1, EDGES + 2), I32), end_index=dram("end_index", (EDGES,), I32),
        node_map=dram("node_map", (NODES, MAPW), I32), edge_row=dram("edge_row", (EDGES, MAPW), I32),
        src_row=dram("src_row", (EDGES,), I32),
        hT=dram("hT", (128, NODES)), yT=dram("yT", (128, NODES)),
        h2=dram("h2_rows", (NODES + EDGES, D)), x1=dram("x1_rows", (NODES + EDGES, D)),
        xd=dram("xd_rows", (EDGES, D)), x1d=dram("x1d_rows", (EDGES, D)),
        hdT=dram("hdT", (128, EDGES)), hsT=dram("hsT", (128, EDGES)), ydT=dram("ydT", (128, EDGES)),
        ywT=dram("ywT", (128, EDGES)))
    with ExitStack() as ctx:
        sb = lambda n, s, d=F32: ctx.enter_context(nc.sbuf_tensor(n, s, d))
        L = LAYERS
        w = Group(
            W_in=sb("W_in", [128, D]), Wq=sb("Wq", [128, L, D]), Wk=sb("Wk", [128, L, D]), Wv=sb("Wv", [128, L, D]),
            Wskip=sb("Wskip", [128, L, D]), We=sb("We", [1, L, D]), gate_h=sb("gate_h", [128, L, D]),
            gate_out=sb("gate_out", [128, L, D]), heads=sb("heads", [128, D]), ident=sb("ident", [128, 128]),
            W1a=sb("W1a", [128, 2, 256]), W1b=sb("W1b", [128, 2, D]), W2a=sb("W2a", [128, 2, 256]),
            W2b=sb("W2b", [128, 2, D]), b_in=sb("b_in", [128, 1]), bq=sb("bq", [128, L]), bk=sb("bk", [128, L]),
            bv=sb("bv", [128, L]), bskip=sb("bskip", [128, L]), gamma=sb("gamma", [128, L]), beta=sb("beta", [128, L]),
            gate_b=sb("gate_b", [128, L]), gate_bh=sb("gate_bh", [128, L]), b1a=sb("b1a", [128, 2]),
            b1b=sb("b1b", [128, 1]), b2u=sb("b2u", [128, 2]), b2b=sb("b2b", [TILE, D]),
            power=sb("power", [128, 2 * TILES]), eps=sb("eps", [128, 2 * TILES]),
            ystats=sb("ystats", [128, 6 * NCHUNK]), ends=sb("ends", [128, 6 * ECHUNK]), wends=sb("wends", [128, 6 * ECHUNK]),
            bn=sb("bn", [128, 2]))
        prepare(nc, a, w, scratch)
        edge_first(nc, a, w, scratch)
        map_sources(nc, a, scratch)
        attention(nc, a, w, scratch, 0)
        dense_first(nc, a, w, scratch)
        batch_norm_params(nc, w, 0)
        edge_update(nc, a, w, scratch, 0)
        dense_second(nc, a, w, scratch)
        edge_sources(nc, a, w, scratch)
        attention(nc, a, w, scratch, 1)
        batch_norm_params(nc, w, 1)
        edge_update(nc, a, w, scratch, 1)
        dense_last(nc, a, w, scratch, out)
        edge_last(nc, a, w, scratch, out)


_INS = ['x', 'src', 'dst', 'edge_attr_128', 'edge_weight1', 'L0_gnn_W_in', 'L0_gnn_b_in', 'L0_gnn_Wq', 'L0_gnn_bq',
        'L0_gnn_Wk', 'L0_gnn_bk', 'L0_gnn_Wv', 'L0_gnn_bv', 'L0_gnn_We', 'L0_gnn_Wskip', 'L0_gnn_bskip',
        'L0_gnn_Wbeta', 'L0_gnn_bn_gamma', 'L0_gnn_bn_beta', 'L1_gnn_u', 'L1_gnn_W1a', 'L1_gnn_b1a', 'L1_gnn_W1b',
        'L1_gnn_b1b', 'L1_gnn_W2a', 'L1_gnn_b2a', 'L1_gnn_W2b', 'L1_gnn_b2b']


def kernel(**inputs):
    import numpy as _np
    import concourse.bacc as _bacc
    from concourse import mybir as _mybir
    from concourse.bass_utils import run_bass_kernel_spmd as _run

    nc = _bacc.Bacc("TRN2", target_bir_lowering=False, num_devices=1)
    arrays, args = {}, {}
    for name in _INS:
        v = _np.ascontiguousarray(inputs[name])
        arrays[f"in_{name}"] = v
        args[name] = nc.dram_tensor(f"in_{name}", v.shape, _mybir.dt.from_np(v.dtype), kind="ExternalInput").ap()
    out = nc.dram_tensor("out", (NODES, D), F32, kind="ExternalOutput").ap()
    program(nc, args, out)
    return _run(nc, [arrays], core_ids=[0]).results[0]["out"]
```

```python
from collections import namedtuple
from contextlib import ExitStack, contextmanager

import concourse.bass as bass
from concourse import mybir

ALU = mybir.AluOpType
ACT = mybir.ActivationFunctionType
F32 = mybir.dt.float32
I32 = mybir.dt.int32

NODES, EDGES, D, HEADS, LAYERS = 50000, 12500, 128, 4, 2
HD = D // HEADS
TILE, TILES = 125, 4
CH = TILE * TILES
NCHUNK, ECHUNK = NODES // CH, EDGES // CH
SPLIT = 112
EPS = 1e-5
BIG = 3.0e38
MAPW = 16
NOWHERE = 1 << 20
AHEAD = 16


def Group(**named):
    return namedtuple("Group", named)(**named)


def made(k):
    return k + AHEAD + 1


def pipeline(eng, n, unroll, stages, peel=0):
    head = max(lag for lag, _ in stages) + peel
    turns = (n - head) // unroll

    def peeled(t):
        for lag, stage in stages:
            if 0 <= t - lag < n:
                stage(t - lag, (t - lag) % unroll, (t - lag) // unroll)

    for t in range(head):
        peeled(t)
    with eng.Fori(0, turns) as i:
        for s in range(unroll):
            for lag, stage in stages:
                d = head + s - lag
                stage(unroll * i + d, d % unroll, i + d // unroll)
    for t in range(head + unroll * turns, n + head - peel):
        peeled(t)


@contextmanager
def phase(nc, name):
    sems, begin = [], []

    def sem(n, at=0):
        sems.append(nc.alloc_semaphore(f"{name}_{n}"))
        if at:
            begin.append((sems[-1], at))
        return sems[-1]

    def start(eng):
        for s, at in begin:
            eng.sem_inc(s, at)

    with ExitStack() as ctx:
        yield Group(
            sb=lambda n, s, d=F32: ctx.enter_context(nc.sbuf_tensor(f"{name}_{n}", s, d)),
            ps=lambda n, s=(128, 512): ctx.enter_context(nc.psum_tensor(f"{name}_{n}", list(s), F32)),
            stage=lambda n: sem(n, AHEAD),
            count=lambda n: sem(n),
            loaded=lambda n, u: [sem(f"{n}{s}") for s in range(u)],
            stored=lambda n, u: [sem(f"{n}{s}", 16) for s in range(u)],
            seen=sem("sp_seen"), start=start)
        nc.all_engine_barrier()
        nc.clear_and_free_semaphores(sems)
        nc.all_engine_barrier()


def hold(sp, seen, sem, value):
    sp.wait_ge(sem, value)
    sp.sem_inc(seen, 1)



def rows_of(table, row0):
    return table[bass.ds(row0, CH), :].rearrange("(p j) f -> p (j f)", j=TILES)


def cols_of(table, col0):
    return table[:, bass.ds(col0, CH)]


def move_rows(eng, out, in_, sem, n=16):
    eng.dma_start(out[0:SPLIT], in_[0:SPLIT]).then_inc(sem, n)
    eng.dma_start(out[SPLIT:TILE], in_[SPLIT:TILE]).then_inc(sem, n)


def flat(buf, q):
    return buf[:, q].rearrange("p j f -> p (j f)")


def tile_cols(t, j, ordered):
    return t[:, j:CH:TILES] if ordered else t[:, j * TILE:(j + 1) * TILE]


def by_tile(ps):
    return ps[:, 0:CH].rearrange("f (j p) -> f j p", j=TILES)


def in_order(t, ordered):
    return t.rearrange("f (p j) -> f j p", j=TILES) if ordered else t.rearrange("f (j p) -> f j p", j=TILES)



def prepare(nc, a, w, scratch):
    with phase(nc, "prep") as ph, nc.Block() as block:
        loaded, ones_made, pool_made = ph.count("loaded"), ph.count("ones_made"), ph.count("pool_made")
        dve_made, pe_made, act_made, written = (ph.count(n) for n in ("dve_made", "pe_made", "act_made", "written"))
        beta3 = ph.sb("beta3", [128, LAYERS, 3])
        wskipT = ph.sb("wskipT", [128, LAYERS, D])
        gate_x = ph.sb("gate_x", [128, LAYERS, D])
        gate_cols = ph.sb("gate_cols", [128, LAYERS, 2])
        ucol = ph.sb("ucol", [128, 1])
        b2a = ph.sb("b2a", [128, 2])
        w2u = ph.sb("w2u", [128, 256])
        ones = ph.sb("ones", [128, D])
        dsti = ph.sb("dsti", [TILE, ECHUNK, TILES], I32)
        nxt = ph.sb("nxt", [TILE, ECHUNK, TILES], I32)
        f1 = ph.sb("f1", [TILE, ECHUNK * TILES])
        f2 = ph.sb("f2", [TILE, ECHUNK * TILES])
        endi = ph.sb("endi", [TILE, ECHUNK, TILES], I32)
        ident_map = ph.sb("ident_map", [TILE, NODES // TILE, MAPW], I32)
        edge_rows = ph.sb("edge_rows", [TILE, ECHUNK, TILES, MAPW], I32)
        minus1 = ph.sb("minus1", [1, 2], I32)
        ps = ph.ps("small")
        psg = ph.ps("gate")
        n_loads = []

        @block.sync
        def _(sp):
            def load(dst, src):
                sp.dma_start(dst, src).then_inc(loaded, 16)
                n_loads.append(1)
            load(w.W_in[:], a["L0_gnn_W_in"])
            for l in range(LAYERS):
                load(w.Wq[:, l], a["L0_gnn_Wq"][l])
                load(w.Wk[:, l], a["L0_gnn_Wk"][l])
                load(w.Wv[:, l], a["L0_gnn_Wv"][l])
                load(w.Wskip[:, l], a["L0_gnn_Wskip"][l])
            load(w.W1a[:], a["L1_gnn_W1a"].rearrange("(b k) m -> k b m", k=128))
            load(w.W1b[:], a["L1_gnn_W1b"].rearrange("(b k) m -> k b m", k=128))
            load(w.W2a[:], a["L1_gnn_W2a"][0:256].rearrange("(b k) m -> k b m", k=128))
            load(w2u[:], a["L1_gnn_W2a"][256:384])
            load(w.W2b[:], a["L1_gnn_W2b"].rearrange("(b k) m -> k b m", k=128))
            load(w.We[:], a["L0_gnn_We"].rearrange("l o f -> o l f"))
            load(w.b2b[:], a["L1_gnn_b2b"].rearrange("(o f) -> o f", o=1).to_broadcast([TILE, D]))
            with nc.allow_non_contiguous_dma(reason="one word a partition"):
                load(w.b_in[:], a["L0_gnn_b_in"].rearrange("(f o) -> f o", o=1))
                for name, t in (("bq", w.bq), ("bk", w.bk), ("bv", w.bv), ("bskip", w.bskip),
                                ("bn_gamma", w.gamma), ("bn_beta", w.beta)):
                    load(t[:], a["L0_gnn_" + name].rearrange("l f -> f l"))
                load(beta3[:], a["L0_gnn_Wbeta"].rearrange("l (t f) o -> f l (t o)", t=3))
                load(ucol[:], a["L1_gnn_u"][0:1].rearrange("o f -> f o"))
                load(b2a[:], a["L1_gnn_b2a"].rearrange("(h f) -> f h", h=2))
                load(w.b1a[:], a["L1_gnn_b1a"].rearrange("(h f) -> f h", h=2))
                load(w.b1b[:], a["L1_gnn_b1b"].rearrange("(f o) -> f o", o=1))
            load(dsti[:], a["dst"].rearrange("(c p j) -> p c j", p=TILE, j=TILES))
            sp.wait_ge(pool_made, 1)
            c_last = ECHUNK - 1
            head = a["dst"][1:1 + c_last * CH]
            load(nxt[:, 0:c_last], head.rearrange("(c p j) -> p c j", p=TILE, j=TILES))
            tail = a["dst"][1 + c_last * CH:1 + c_last * CH + (TILE - 1) * TILES]
            load(nxt[0:TILE - 1, c_last], tail.rearrange("(p j) -> p j", j=TILES))
            load(nxt[TILE - 1:TILE, c_last, 0:TILES - 1], a["dst"][EDGES - TILES + 1:EDGES].rearrange("(o j) -> o j", o=1))
            sp.wait_ge(pool_made, 2)
            sp.dma_start(scratch.dst_pad[:, 0:1], minus1[:, 0:1]).then_inc(written, 16)
            sp.dma_start(scratch.dst_pad[:, EDGES + 1:EDGES + 2], minus1[:, 1:2]).then_inc(written, 16)
            sp.dma_start(scratch.dst_pad[:, 1:EDGES + 1], a["dst"].rearrange("(o e) -> o e", o=1)).then_inc(written, 16)
            sp.wait_ge(pool_made, 4)
            sp.dma_start(scratch.node_map.rearrange("(p n) w -> p (n w)", p=TILE), ident_map[:].rearrange("p n w -> p (n w)")).then_inc(written, 16)
            for c in range(ECHUNK):
                sp.dma_start(scratch.edge_row[c * CH:(c + 1) * CH].rearrange("(p j) w -> p (j w)", j=TILES),
                             edge_rows[:, c].rearrange("p j w -> p (j w)")).then_inc(written, 16)
            sp.wait_ge(dve_made, 99)
            sp.dma_start(scratch.end_index.rearrange("(c p j) -> p c j", p=TILE, j=TILES), endi[:]).then_inc(written, 16)
            sp.wait_ge(written, 16 * (5 + ECHUNK))

        all_loaded = 16 * len(n_loads)

        @block.gpsimd
        def _(pool):
            pool.memset(nxt[:], -1).then_inc(pool_made, 1)
            pool.memset(minus1[:], -1).then_inc(pool_made, 1)
            pool.iota(ident_map[:], [[1, NODES // TILE], [0, MAPW]], base=0, channel_multiplier=NODES // TILE).then_inc(pool_made, 1)
            pool.iota(edge_rows[:], [[CH, ECHUNK], [1, TILES], [0, MAPW]], base=NODES, channel_multiplier=TILES).then_inc(pool_made, 1)
            pool.memset(ones[:], 1.0).then_inc(ones_made, 1)
            pool.memset(w.ident[:], 0.0).then_inc(ones_made, 1)
            pool.memset(w.heads[:], 0.0).then_inc(ones_made, 1)
            pool.memset(w.power[:], -0.5).then_inc(ones_made, 1)
            pool.memset(w.eps[:], EPS).then_inc(ones_made, 1)
            pool.memset(w.two[:], 2.0).then_inc(ones_made, 1)
            pool.wait_ge(ones_made, 6)
            pool.affine_select(out=w.ident[:], in_=w.ident[:], compare_op=ALU.not_equal, fill=1.0, base=0,
                               pattern=[[-1, 128]], channel_multiplier=1).then_inc(ones_made, 1)

        @block.vector
        def _(dve):
            n = 0

            def after(ins):
                nonlocal n
                n += 1
                ins.then_inc(dve_made, 1)
                dve.wait_ge(dve_made, n)

            dve.wait_ge(loaded, all_loaded)
            dve.wait_ge(ones_made, 7)
            for h in range(HEADS):
                dve.memset(w.heads[h * HD:(h + 1) * HD, h * HD:(h + 1) * HD], float(HD) ** -0.5)
            for l in range(LAYERS):
                after(dve.tensor_tensor(gate_cols[:, l, 0:1], beta3[:, l, 0:1], beta3[:, l, 2:3], ALU.add))
                after(dve.tensor_tensor(gate_cols[:, l, 1:2], beta3[:, l, 1:2], beta3[:, l, 2:3], ALU.subtract))
                after(dve.tensor_scalar(w.gate_out[:, l], ones[:], gate_cols[:, l, 0:1], None, ALU.mult))
                after(dve.tensor_scalar(gate_x[:, l], ones[:], gate_cols[:, l, 1:2], None, ALU.mult))
            dve.wait_ge(pe_made, 1)
            after(dve.tensor_copy(wskipT[:].rearrange("p l f -> p (l f)"), ps[:, 0:LAYERS * D]))
            dve.wait_ge(pe_made, 2)
            after(dve.tensor_copy(w.gate_h[:].rearrange("p l f -> p (l f)"), psg[:, 0:LAYERS * D]))
            after(dve.tensor_copy(w.gate_b[:], psg[:, LAYERS * D:LAYERS * D + LAYERS]))
            after(dve.tensor_scalar(w.gate_bh[:], w.gate_b[:], 0.5, None, ALU.mult))
            after(dve.tensor_tensor(w.b2u[:], psg[:, 300:302], b2a[:], ALU.add))
            d, e = dsti[:].rearrange("p c j -> p (c j)"), nxt[:].rearrange("p c j -> p (c j)")
            after(dve.tensor_tensor(f1[:], d, e, ALU.not_equal))
            after(dve.scalar_tensor_tensor(out=f2[:], in0=d, scalar=float(-NOWHERE), in1=f1[:], op0=ALU.add, op1=ALU.mult))
            after(dve.tensor_scalar(endi[:].rearrange("p c j -> p (c j)"), f2[:], float(NOWHERE), None, ALU.add))
            dve.sem_inc(dve_made, 99 - n)

        @block.tensor
        def _(pe):
            pe.wait_ge(loaded, all_loaded)
            pe.wait_ge(ones_made, 7)
            for l in range(LAYERS):
                last = pe.transpose(ps[:, l * D:(l + 1) * D], w.Wskip[:, l], w.ident[:])
            last.then_inc(pe_made, 1)
            pe.wait_ge(dve_made, 4 * LAYERS + 1)
            for l in range(LAYERS):
                pe.matmul(psg[:, l * D:(l + 1) * D], wskipT[:, l], gate_x[:, l], start=True, stop=True)
                pe.matmul(psg[:, LAYERS * D + l:LAYERS * D + l + 1], gate_x[:, l], w.bskip[:, l:l + 1], start=True, stop=True)
            for h in range(2):
                last = pe.matmul(psg[:, 300 + h:301 + h], w2u[:, h * 128:(h + 1) * 128], ucol[:], start=True, stop=True)
            last.then_inc(pe_made, 1)



def norm_stats(dve, x, st, stats_made):
    for j in range(x.shape[1]):
        last = dve.bn_stats(st[:, j], x[:, j])
    last.then_inc(stats_made, 1)


def norm_aggr(dve, st, mv, stats_seen, aggr_made):
    dve.sem_inc(stats_seen, 1)
    for j in range(st.shape[1]):
        last = dve.bn_aggr(mv[:, j], st[:, j])
    last.then_inc(aggr_made, 1)


def norm_bias(dve, nb, mv, rstd, sem):
    dve.scalar_tensor_tensor(out=nb, in0=mv[:, :, 0], scalar=-1.0, in1=rstd, op0=ALU.mult, op1=ALU.mult).then_inc(sem, 1)


def norm_relu(act, xn, x, rstd, nb, sem):
    for j in range(x.shape[1]):
        last = act.activation(xn[:, j], x[:, j], ACT.Relu, bias=nb[:, j:j + 1], scale=rstd[:, j:j + 1])
    last.then_inc(sem, 1)


def to_T(pe, ps, rows, ident, sem):
    for j in range(TILES):
        last = pe.transpose(ps[:, j * TILE:(j + 1) * TILE], rows[:, j], ident[0:TILE, 0:TILE])
    last.then_inc(sem, 1)


def to_rows(pe, ps, t, ident, ordered, sem):
    for j in range(TILES):
        last = pe.transpose(ps[0:TILE, j * D:(j + 1) * D], tile_cols(t, j, ordered), ident[:])
    last.then_inc(sem, 1)


def dense_first(nc, a, w, scratch):
    U = 4
    with phase(nc, "first") as ph:
        x = ph.sb("x", [TILE, U, TILES, D])
        xn = ph.sb("xn", [TILE, 2, TILES, D])
        st = ph.sb("st", [TILE, 2, TILES, 6])
        mv = ph.sb("mv", [TILE, 2, TILES, 2])
        ve = ph.sb("ve", [TILE, 2, TILES])
        rstd = ph.sb("rstd", [TILE, 2, TILES])
        nb = ph.sb("nb", [TILE, 2, TILES])
        h0 = ph.sb("h0", [128, 2, CH])
        h1 = ph.sb("h1", [128, U, CH])
        sig = ph.sb("sig", [128, 2, CH])
        y = ph.sb("y", [128, U, CH])
        psT = [ph.ps(f"psT{s}") for s in range(2)]
        psW = [ph.ps(f"psW{s}") for s in range(2)]
        psX = [ph.ps(f"psX{s}") for s in range(2)]
        psZ = [ph.ps(f"psZ{s}") for s in range(2)]
        x_loaded = ph.loaded("x_loaded", U)
        h1_stored, y_stored = ph.stored("h1_stored", U), ph.stored("y_stored", U)
        names = "stats seen aggr eps rstd nb xn xT h0 w_in h1 xz sig y ystats".split()
        m = Group(**{n: ph.stage(n + "_made") for n in names})
        with nc.Block() as block:
            @block.sync
            def _(sp):
                ph.start(sp)

                def load(k, q, r):
                    hold(sp, ph.seen, m.xn, made(k - U))
                    move_rows(sp, flat(x, q), rows_of(a["x"], k * CH), x_loaded[q])

                def store_h(k, q, r):
                    hold(sp, ph.seen, m.h1, made(k))
                    sp.dma_start(cols_of(scratch.hT, k * CH), h1[:, q]).then_inc(h1_stored[q], 16)

                def store_y(k, q, r):
                    hold(sp, ph.seen, m.y, made(k))
                    sp.dma_start(cols_of(scratch.yT, k * CH), y[:, q]).then_inc(y_stored[q], 16)

                pipeline(sp, NCHUNK, U, [(0, load), (7, store_h), (9, store_y)])
                for q in range(U):
                    sp.wait_ge(h1_stored[q], 16 + 16 * (NCHUNK // U))
                    sp.wait_ge(y_stored[q], 16 + 16 * (NCHUNK // U))

            @block.vector
            def _(dve):
                def stats(k, q, r):
                    dve.wait_ge(x_loaded[q], 32 * r + 32)
                    dve.wait_ge(m.aggr, made(k - 2))
                    norm_stats(dve, x[:, q], st[:, q % 2], m.stats)

                def aggr(k, q, r):
                    dve.wait_ge(m.stats, made(k))
                    dve.wait_ge(m.xn, made(k - 2))
                    norm_aggr(dve, st[:, q % 2], mv[:, q % 2], m.seen, m.aggr)

                def bias(k, q, r):
                    dve.wait_ge(m.rstd, made(k))
                    dve.wait_ge(m.xn, made(k - 2))
                    norm_bias(dve, nb[:, q % 2], mv[:, q % 2], rstd[:, q % 2], m.nb)

                def make_h1(k, q, r):
                    dve.wait_ge(m.w_in, made(k))
                    dve.wait_ge(m.xz, made(k - U))
                    dve.wait_ge(h1_stored[q], 16 * r + 16)
                    dve.tensor_scalar(h1[:, q], psW[q % 2][:, 0:CH], w.b_in[:, 0:1], 0.0, ALU.add, ALU.max).then_inc(m.h1, 1)

                def make_y(k, q, r):
                    dve.wait_ge(m.sig, made(k))
                    dve.wait_ge(m.ystats, made(k - U))
                    dve.wait_ge(y_stored[q], 16 * r + 16)
                    dve.scalar_tensor_tensor(out=y[:, q], in0=psX[q % 2][:, 0:CH], scalar=w.bskip[:, 0:1],
                                             in1=sig[:, q % 2], op0=ALU.add, op1=ALU.mult).then_inc(m.y, 1)

                def ystats(k, q, r):
                    dve.wait_ge(m.y, made(k))
                    dve.bn_stats(w.ystats[:, bass.ds(k * 6, 6)], y[:, q]).then_inc(m.ystats, 1)

                pipeline(dve, NCHUNK, U, [(1, bias), (0, stats), (4, make_h1), (0, aggr), (6, make_y), (7, ystats)])

            @block.gpsimd
            def _(pool):
                def make_rstd(k, q, r):
                    pool.wait_ge(m.aggr, made(k))
                    pool.wait_ge(m.xn, made(k - 2))
                    pool.tensor_tensor(ve[:, q % 2], mv[:, q % 2, :, 1], w.eps[0:TILE, 0:TILES], ALU.add).then_inc(m.eps, 1)
                    pool.wait_ge(m.eps, made(k))
                    pool.tensor_tensor(rstd[:, q % 2], ve[:, q % 2], w.power[0:TILE, 0:TILES], ALU.pow).then_inc(m.rstd, 1)
                pipeline(pool, NCHUNK, U, [(0, make_rstd)])

            @block.tensor
            def _(pe):
                def turn(k, q, r):
                    pe.wait_ge(m.xn, made(k))
                    pe.wait_ge(m.h0, made(k - 2))
                    to_T(pe, psT[q % 2], xn[:, q % 2], w.ident, m.xT)

                def first(k, q, r):
                    pe.wait_ge(m.h0, made(k))
                    pe.wait_ge(m.h1, made(k - 2))
                    pe.matmul(psW[q % 2][:, 0:CH], w.W_in[:], h0[:, q % 2], start=True, stop=True).then_inc(m.w_in, 1)

                def skip(k, q, r):
                    pe.wait_ge(m.h1, made(k))
                    pe.wait_ge(m.y, made(k - 2))
                    pe.matmul(psZ[q % 2][:, 0:CH], w.gate_h[:, 0], h1[:, q], start=True, stop=True)
                    pe.matmul(psX[q % 2][:, 0:CH], w.Wskip[:, 0], h1[:, q], start=True, stop=True).then_inc(m.xz, 1)

                pipeline(pe, NCHUNK, U, [(0, turn), (1, first), (3, skip)])

            @block.scalar
            def _(act):
                def make_xn(k, q, r):
                    act.wait_ge(m.nb, made(k))
                    act.wait_ge(m.xT, made(k - 2))
                    norm_relu(act, xn[:, q % 2], x[:, q], rstd[:, q % 2], nb[:, q % 2], m.xn)

                def make_h0(k, q, r):
                    act.wait_ge(m.xT, made(k))
                    act.wait_ge(m.w_in, made(k - 2))
                    act.activation(h0[:, q % 2], psT[q % 2][:, 0:CH], ACT.Identity).then_inc(m.h0, 1)

                def make_sig(k, q, r):
                    act.wait_ge(m.xz, made(k))
                    act.wait_ge(m.y, made(k - 2))
                    act.activation(sig[:, q % 2], psZ[q % 2][:, 0:CH], ACT.Sigmoid, bias=w.gate_b[:, 0:1]).then_inc(m.sig, 1)

                pipeline(act, NCHUNK, U, [(0, make_xn), (1, make_h0), (4, make_sig)])


def batch_norm_params(nc, w, l):
    with phase(nc, f"bn{l}") as ph, nc.Block() as block:
        done, pool_done = ph.count("dve_done"), ph.count("pool_done")
        agg = ph.sb("agg", [128, 3, 2])
        sq = ph.sb("sq", [128, 3])
        tmp = ph.sb("tmp", [128, 8])
        rs = ph.sb("rs", [128, 4])
        ratio = EDGES / NODES

        @block.vector
        def _(dve):
            n = 0

            def after(ins):
                nonlocal n
                n += 1
                ins.then_inc(done, 1)
                dve.wait_ge(done, n)
            after(dve.bn_aggr(agg[:, 0], w.ystats[:]))
            after(dve.bn_aggr(agg[:, 1], w.wends[:]))
            after(dve.bn_aggr(agg[:, 2], w.ends[:]))
            after(dve.tensor_tensor(sq[:], agg[:, :, 0], agg[:, :, 0], ALU.mult))
            after(dve.tensor_tensor(sq[:], sq[:], agg[:, :, 1], ALU.add))
            after(dve.tensor_tensor(tmp[:, 0:1], agg[:, 1, 0:1], agg[:, 2, 0:1], ALU.subtract))
            after(dve.scalar_tensor_tensor(out=tmp[:, 1:2], in0=tmp[:, 0:1], scalar=ratio, in1=agg[:, 0, 0:1], op0=ALU.mult, op1=ALU.add))
            after(dve.tensor_tensor(tmp[:, 2:3], sq[:, 2:3], sq[:, 1:2], ALU.subtract))
            after(dve.scalar_tensor_tensor(out=tmp[:, 3:4], in0=tmp[:, 2:3], scalar=ratio, in1=sq[:, 0:1], op0=ALU.mult, op1=ALU.add))
            after(dve.tensor_tensor(tmp[:, 4:5], tmp[:, 1:2], tmp[:, 1:2], ALU.mult))
            after(dve.tensor_tensor(tmp[:, 5:6], tmp[:, 3:4], tmp[:, 4:5], ALU.subtract))
            after(dve.tensor_scalar(rs[:, 0:1], tmp[:, 5:6], 0.0, EPS, ALU.max, ALU.add))
            dve.wait_ge(pool_done, 1)
            after(dve.tensor_tensor(w.bn[:, 0:1], w.gamma[:, l:l + 1], rs[:, 1:2], ALU.mult))
            after(dve.tensor_tensor(tmp[:, 6:7], tmp[:, 1:2], w.bn[:, 0:1], ALU.mult))
            after(dve.tensor_tensor(w.bn[:, 1:2], w.beta[:, l:l + 1], tmp[:, 6:7], ALU.subtract))

        @block.gpsimd
        def _(pool):
            pool.wait_ge(done, 12)
            pool.tensor_tensor(rs[:, 1:2], rs[:, 0:1], w.power[:, 0:1], ALU.pow).then_inc(pool_done, 1)


def dense_second(nc, a, w, scratch):
    U = 4
    with phase(nc, "second") as ph:
        yin = ph.sb("yin", [128, U, CH])
        hin = ph.sb("hin", [128, U, CH])
        act1 = ph.sb("act1", [128, 2, CH])
        h2 = ph.sb("h2", [128, U, CH])
        rows = ph.sb("rows", [TILE, U, TILES, D])
        sig = ph.sb("sig", [128, 2, CH])
        y = ph.sb("y", [128, U, CH])
        psR = [ph.ps(f"psR{s}") for s in range(2)]
        psX = [ph.ps(f"psX{s}") for s in range(2)]
        psZ = [ph.ps(f"psZ{s}") for s in range(2)]
        y_loaded, h_loaded = ph.loaded("y_loaded", U), ph.loaded("h_loaded", U)
        rows_stored, rows_stored2, y_stored = (ph.stored(n, U) for n in ("rows_stored", "rows_stored2", "y_stored"))
        m = Group(**{n: ph.stage(n + "_made") for n in "bn h2 turned rows xz sig y ystats".split()})
        with nc.Block() as block:
            @block.sync
            def _(sp):
                ph.start(sp)

                def load(k, q, r):
                    hold(sp, ph.seen, m.bn, made(k - U))
                    sp.dma_start(yin[:, q], cols_of(scratch.yT, k * CH)).then_inc(y_loaded[q], 16)
                    hold(sp, ph.seen, m.h2, made(k - U))
                    sp.dma_start(hin[:, q], cols_of(scratch.hT, k * CH)).then_inc(h_loaded[q], 16)

                def store_rows(k, q, r):
                    hold(sp, ph.seen, m.rows, made(k))
                    dst = rows_of(scratch.h2, k * CH)
                    sp.dma_start(dst[0:SPLIT], flat(rows, q)[0:SPLIT]).then_inc(rows_stored[q], 16)
                    sp.dma_start(dst[SPLIT:TILE], flat(rows, q)[SPLIT:TILE]).then_inc(rows_stored2[q], 16)

                def store_y(k, q, r):
                    hold(sp, ph.seen, m.y, made(k))
                    sp.dma_start(cols_of(scratch.yT, k * CH), y[:, q]).then_inc(y_stored[q], 16)

                pipeline(sp, NCHUNK, U, [(0, load), (6, store_rows), (7, store_y)])
                for sems in (rows_stored, rows_stored2, y_stored):
                    for q in range(U):
                        sp.wait_ge(sems[q], 16 + 16 * (NCHUNK // U))

            @block.scalar
            def _(act):
                def bn(k, q, r):
                    act.wait_ge(y_loaded[q], 16 * r + 16)
                    act.wait_ge(m.h2, made(k - 2))
                    act.activation(act1[:, q % 2], yin[:, q], ACT.Relu, bias=w.bn[:, 1:2], scale=w.bn[:, 0:1]).then_inc(m.bn, 1)

                def make_rows(k, q, r):
                    act.wait_ge(m.turned, made(k))
                    act.wait_ge(rows_stored[q], 16 * r + 16)
                    act.wait_ge(rows_stored2[q], 16 * r + 16)
                    act.copy(flat(rows, q), psR[q % 2][0:TILE]).then_inc(m.rows, 1)

                def make_sig(k, q, r):
                    act.wait_ge(m.xz, made(k))
                    act.wait_ge(m.y, made(k - 2))
                    act.activation(sig[:, q % 2], psZ[q % 2][:, 0:CH], ACT.Sigmoid, bias=w.gate_b[:, 1:2]).then_inc(m.sig, 1)

                pipeline(act, NCHUNK, U, [(3, make_sig), (0, bn), (3, make_rows)])

            @block.vector
            def _(dve):
                def make_h2(k, q, r):
                    dve.wait_ge(m.bn, made(k))
                    dve.wait_ge(h_loaded[q], 16 * r + 16)
                    dve.wait_ge(m.xz, made(k - U))
                    dve.tensor_tensor(h2[:, q], act1[:, q % 2], hin[:, q], ALU.add).then_inc(m.h2, 1)

                def make_y(k, q, r):
                    dve.wait_ge(m.sig, made(k))
                    dve.wait_ge(m.ystats, made(k - U))
                    dve.wait_ge(y_stored[q], 16 * r + 16)
                    dve.scalar_tensor_tensor(out=y[:, q], in0=psX[q % 2][:, 0:CH], scalar=w.bskip[:, 1:2],
                                             in1=sig[:, q % 2], op0=ALU.add, op1=ALU.mult).then_inc(m.y, 1)

                def ystats(k, q, r):
                    dve.wait_ge(m.y, made(k))
                    dve.bn_stats(w.ystats[:, bass.ds(k * 6, 6)], y[:, q]).then_inc(m.ystats, 1)

                pipeline(dve, NCHUNK, U, [(1, make_h2), (4, make_y), (5, ystats)])

            @block.tensor
            def _(pe):
                def turn(k, q, r):
                    pe.wait_ge(m.rows, made(k - 2))
                    to_rows(pe, psR[q % 2], h2[:, q], w.ident, False, m.turned)

                def skip(k, q, r):
                    pe.wait_ge(m.h2, made(k))
                    pe.wait_ge(m.y, made(k - 2))
                    pe.matmul(psZ[q % 2][:, 0:CH], w.gate_h[:, 1], h2[:, q], start=True, stop=True)
                    pe.matmul(psX[q % 2][:, 0:CH], w.Wskip[:, 1], h2[:, q], start=True, stop=True).then_inc(m.xz, 1)

                pipeline(pe, NCHUNK, U, [(2, skip), (2, turn)])


def dense_last(nc, a, w, scratch, out):
    U = 8
    with phase(nc, "last") as ph:
        yin = ph.sb("yin", [128, 4, CH])
        hin, xin, xh = (ph.sb(n, [TILE, 4, TILES, D]) for n in ("hin", "xin", "xh"))
        act1 = ph.sb("act1", [128, 2, CH])
        x1 = ph.sb("x1", [TILE, 8, TILES, D])
        x1b = ph.sb("x1b", [TILE, 8, TILES, D])
        xn = ph.sb("xn", [TILE, 2, TILES, D])
        st = ph.sb("st", [TILE, 4, TILES, 6])
        mv = ph.sb("mv", [TILE, 4, TILES, 2])
        ve = ph.sb("ve", [TILE, 4, TILES])
        rstd = ph.sb("rstd", [TILE, 4, TILES])
        nb = ph.sb("nb", [TILE, 4, TILES])
        g = ph.sb("g", [128, 2, CH])
        hid = ph.sb("hid", [128, 2, 2, CH])
        o = ph.sb("o", [TILE, 4, TILES, D])
        psR, psT = ([ph.ps(f"{n}{s}") for s in range(2)] for n in ("psR", "psT"))
        psH = [ph.ps(f"psH{h}") for h in range(2)]
        psO = [ph.ps(f"psO{s}") for s in range(2)]
        y_loaded, x_loaded = ph.loaded("y_loaded", 4), ph.loaded("x_loaded", 4)
        x1_stored, x1_stored2 = ph.stored("x1_stored", 8), ph.stored("x1_stored2", 8)
        o_stored, o_stored2 = ph.stored("o_stored", 4), ph.stored("o_stored2", 4)
        names = "bn xh turned x1 x1b stats seen aggr eps rstd nb xn xT g hidden hid0 hid1 o_ps o"
        m = Group(**{n: ph.stage(n + "_made") for n in names.split()})
        with nc.Block() as block:
            @block.sync
            def _(sp):
                ph.start(sp)

                def load(k, q, r):
                    q4, r4 = q % 4, 2 * r + q // 4
                    hold(sp, ph.seen, m.bn, made(k - 4))
                    sp.dma_start(yin[:, q4], cols_of(scratch.yT, k * CH)).then_inc(y_loaded[q4], 16)
                    hold(sp, ph.seen, m.xh, made(k - 4))
                    move_rows(sp, flat(hin, q4), rows_of(scratch.h2, k * CH), x_loaded[q4])
                    move_rows(sp, flat(xin, q4), rows_of(a["x"], k * CH), x_loaded[q4])

                def store_x1(k, q, r):
                    hold(sp, ph.seen, m.x1, made(k))
                    dst = rows_of(scratch.x1, k * CH)
                    sp.dma_start(dst[0:SPLIT], flat(x1, q)[0:SPLIT]).then_inc(x1_stored[q], 16)
                    sp.dma_start(dst[SPLIT:TILE], flat(x1, q)[SPLIT:TILE]).then_inc(x1_stored2[q], 16)

                def store_o(k, q, r):
                    q4 = q % 4
                    hold(sp, ph.seen, m.o, made(k))
                    dst = rows_of(out, k * CH)
                    sp.dma_start(dst[0:SPLIT], flat(o, q4)[0:SPLIT]).then_inc(o_stored[q4], 16)
                    sp.dma_start(dst[SPLIT:TILE], flat(o, q4)[SPLIT:TILE]).then_inc(o_stored2[q4], 16)

                pipeline(sp, NCHUNK, U, [(0, load), (7, store_x1), (15, store_o)])
                for q in range(8):
                    for sems in (x1_stored, x1_stored2):
                        sp.wait_ge(sems[q], 16 + 16 * len(range(q, NCHUNK, 8)))
                for q in range(4):
                    for sems in (o_stored, o_stored2):
                        sp.wait_ge(sems[q], 16 + 16 * len(range(q, NCHUNK, 4)))

            @block.scalar
            def _(act):
                def bn(k, q, r):
                    q4, r4 = q % 4, 2 * r + q // 4
                    act.wait_ge(y_loaded[q4], 16 * r4 + 16)
                    act.wait_ge(m.turned, made(k - 2))
                    act.activation(act1[:, q % 2], yin[:, q4], ACT.Relu, bias=w.bn[:, 1:2], scale=w.bn[:, 0:1]).then_inc(m.bn, 1)

                def make_xn(k, q, r):
                    act.wait_ge(m.nb, made(k))
                    act.wait_ge(m.xT, made(k - 2))
                    norm_relu(act, xn[:, q % 2], x1[:, q], rstd[:, q % 4], nb[:, q % 4], m.xn)

                def make_g(k, q, r):
                    act.wait_ge(m.xT, made(k))
                    act.wait_ge(m.hidden, made(k - 2))
                    act.activation(g[:, q % 2], psT[q % 2][:, 0:CH], ACT.Identity).then_inc(m.g, 1)

                def make_hid0(k, q, r):
                    act.wait_ge(m.hidden, made(k))
                    act.wait_ge(m.o_ps, made(k - 2))
                    act.activation(hid[:, q % 2, 0], psH[0][:, 0:CH], ACT.Relu, bias=w.b2u[:, 0:1]).then_inc(m.hid0, 1)

                pipeline(act, NCHUNK, U, [(9, make_hid0), (5, make_xn), (0, bn), (7, make_g)])

            @block.gpsimd
            def _(pool):
                def add_h2(k, q, r):
                    q4, r4 = q % 4, 2 * r + q // 4
                    pool.wait_ge(x_loaded[q4], 64 * r4 + 64)
                    pool.wait_ge(m.x1, made(k - 4))
                    pool.tensor_tensor(xh[:, q4], xin[:, q4], hin[:, q4], ALU.add).then_inc(m.xh, 1)

                def make_rstd(k, q, r):
                    pool.wait_ge(m.aggr, made(k))
                    pool.wait_ge(m.xn, made(k - 4))
                    pool.tensor_tensor(ve[:, q % 4], mv[:, q % 4, :, 1], w.eps[0:TILE, 0:TILES], ALU.add).then_inc(m.eps, 1)
                    pool.wait_ge(m.eps, made(k))
                    pool.tensor_tensor(rstd[:, q % 4], ve[:, q % 4], w.power[0:TILE, 0:TILES], ALU.pow).then_inc(m.rstd, 1)

                def add_bias(k, q, r):
                    pool.wait_ge(m.x1, made(k))
                    pool.wait_ge(m.o, made(k - 8))
                    pool.tensor_tensor(x1b[:, q], x1[:, q], w.b2b[:].rearrange("p (o f) -> p o f", o=1).to_broadcast([TILE, TILES, D]), ALU.add).then_inc(m.x1b, 1)

                pipeline(pool, NCHUNK, U, [(0, add_h2), (3, make_rstd), (5, add_bias)])

            @block.vector
            def _(dve):
                def make_x1(k, q, r):
                    q4 = q % 4
                    dve.wait_ge(m.turned, made(k))
                    dve.wait_ge(m.xh, made(k))
                    dve.wait_ge(x1_stored[q], 16 * r + 16)
                    dve.wait_ge(x1_stored2[q], 16 * r + 16)
                    dve.wait_ge(m.x1b, made(k - 8))
                    dve.tensor_tensor(flat(x1, q), psR[q % 2][0:TILE], flat(xh, q4), ALU.add).then_inc(m.x1, 1)

                def stats(k, q, r):
                    dve.wait_ge(m.x1, made(k))
                    dve.wait_ge(m.aggr, made(k - 4))
                    norm_stats(dve, x1[:, q], st[:, q % 4], m.stats)

                def aggr(k, q, r):
                    dve.wait_ge(m.stats, made(k))
                    dve.wait_ge(m.xn, made(k - 4))
                    norm_aggr(dve, st[:, q % 4], mv[:, q % 4], m.seen, m.aggr)

                def bias(k, q, r):
                    dve.wait_ge(m.rstd, made(k))
                    dve.wait_ge(m.xn, made(k - 4))
                    norm_bias(dve, nb[:, q % 4], mv[:, q % 4], rstd[:, q % 4], m.nb)

                def make_hid1(k, q, r):
                    dve.wait_ge(m.hidden, made(k))
                    dve.wait_ge(m.o_ps, made(k - 2))
                    dve.tensor_scalar(hid[:, q % 2, 1], psH[1][:, 0:CH], w.b2u[:, 1:2], 0.0, ALU.add, ALU.max).then_inc(m.hid1, 1)

                def make_o(k, q, r):
                    q4, r4 = q % 4, 2 * r + q // 4
                    dve.wait_ge(m.o_ps, made(k))
                    dve.wait_ge(m.x1b, made(k))
                    dve.wait_ge(o_stored[q4], 16 * r4 + 16)
                    dve.wait_ge(o_stored2[q4], 16 * r4 + 16)
                    dve.tensor_tensor(flat(o, q4), psO[q % 2][0:TILE], flat(x1b, q), ALU.add).then_inc(m.o, 1)

                pipeline(dve, NCHUNK, U, [(9, make_hid1), (4, bias), (2, make_x1), (11, make_o), (2, stats), (2, aggr)])

            @block.tensor
            def _(pe):
                def turn(k, q, r):
                    pe.wait_ge(m.bn, made(k))
                    pe.wait_ge(m.x1, made(k - 2))
                    to_rows(pe, psR[q % 2], act1[:, q % 2], w.ident, False, m.turned)

                def turn_back(k, q, r):
                    pe.wait_ge(m.xn, made(k))
                    pe.wait_ge(m.g, made(k - 2))
                    to_T(pe, psT[q % 2], xn[:, q % 2], w.ident, m.xT)

                def hidden(k, q, r):
                    pe.wait_ge(m.g, made(k))
                    pe.wait_ge(m.hid0, made(k - 1))
                    pe.wait_ge(m.hid1, made(k - 1))
                    for h in range(2):
                        last = pe.matmul(psH[h][:, 0:CH], w.W2a[:, 0, h * 128:(h + 1) * 128], g[:, q % 2], start=True, stop=True)
                    last.then_inc(m.hidden, 1)

                def output(k, q, r):
                    pe.wait_ge(m.hid0, made(k))
                    pe.wait_ge(m.hid1, made(k))
                    pe.wait_ge(m.o, made(k - 2))
                    for j in range(TILES):
                        for h in range(2):
                            last = pe.matmul(psO[q % 2][0:TILE, j * D:(j + 1) * D], tile_cols(hid[:, q % 2, h], j, False), w.W2b[:, h],
                                             start=(h == 0), stop=(h == 1))
                    last.then_inc(m.o_ps, 1)

                pipeline(pe, NCHUNK, U, [(1, turn), (8, hidden), (6, turn_back), (10, output)])

def by_edge(t):
    return t.rearrange("f (p j) -> f j p", j=TILES)


def edge_window(scratch, col0):
    return scratch.dst_pad[0:1, bass.ds(col0, CH + 2)].to_broadcast([128, CH + 2])


def index_slot(table, e0):
    return table[bass.ds(e0, CH)].rearrange("(p j) -> p j", j=TILES)


def gather(pool, seen, rows, table, index, sem):
    pool.sem_inc(seen, 1)
    for j in range(TILES):
        pool.indirect_dma_start(rows[:, j], None, table, bass.IndirectOffsetOnAxis(index[:, j:j + 1], 0),
                                bounds_check=table.shape[0] - 1, oob_is_err=False).then_inc(sem, 16)


def scatter_ends(pool, seen, table, rows, index, sem):
    pool.sem_inc(seen, 1)
    for j in range(TILES):
        pool.indirect_dma_start(table, bass.IndirectOffsetOnAxis(index[:, j:j + 1], 0), rows[:, j], None,
                                bounds_check=table.shape[0] - 1, oob_is_err=False).then_inc(sem, 16)


def edge_first(nc, a, w, scratch):
    U = 4
    N2 = 2 * TILES
    with phase(nc, "efirst") as ph:
        di, si, ei = (ph.sb(n, [TILE, U, TILES], I32) for n in ("di", "si", "ei"))
        er = ph.sb("er", [TILE, U, TILES, MAPW], I32)
        x = ph.sb("x", [TILE, U, N2, D])
        xn = ph.sb("xn", [TILE, 2, N2, D])
        st = ph.sb("st", [TILE, U, N2, 6])
        mv = ph.sb("mv", [TILE, U, N2, 2])
        ve = ph.sb("ve", [TILE, U, N2])
        rstd = ph.sb("rstd", [TILE, U, N2])
        nb = ph.sb("nb", [TILE, U, N2])
        h0 = ph.sb("h0", [128, 2, 2, CH])
        h1 = ph.sb("h1", [128, U, 2, CH])
        win = ph.sb("win", [128, U, CH + 2], I32)
        cont = ph.sb("cont", [128, 2, CH])
        begun = ph.sb("begun", [128, CH])
        ones = ph.sb("ones", [128, CH])
        cnt, rcnt = ph.sb("cnt", [128, U, CH]), ph.sb("rcnt", [128, U, CH])
        rcnt_stored = ph.stored("rcnt_stored", U)
        sig = ph.sb("sig", [128, CH])
        yw = ph.sb("yw", [128, U, CH])
        ywn = ph.sb("ywn", [128, CH])
        psT = [ph.ps(f"psT{s}") for s in range(2)]
        psW = [ph.ps(f"psW{s}") for s in range(2)]
        psX, psZ = ph.ps("psX"), ph.ps("psZ")
        idx_loaded, win_loaded = ph.loaded("idx_loaded", U), ph.loaded("win_loaded", U)
        moved = ph.loaded("moved", U)
        xd_stored, hd_stored, hs_stored, yw_stored = (ph.stored(n, U) for n in ("xd_stored", "hd_stored", "hs_stored", "yw_stored"))
        names = "stats aggr_seen aggr eps rstd nb xn xT h0 w_in h1d h1s xz sig yw cont begun cnt rcnt ywn ywstats init"
        m = Group(**{n: ph.stage(n + "_made") for n in names.split()})
        per = 16 * 3 * TILES
        with nc.Block() as block:
            @block.sync
            def _(sp):
                ph.start(sp)

                def load(k, q, r):
                    hold(sp, ph.seen, m.stats, made(k - U))
                    sp.dma_start(di[:, q], index_slot(a["dst"], k * CH)).then_inc(idx_loaded[q], 16)
                    sp.dma_start(si[:, q], index_slot(a["src"], k * CH)).then_inc(idx_loaded[q], 16)
                    sp.dma_start(ei[:, q], index_slot(scratch.end_index, k * CH)).then_inc(idx_loaded[q], 16)
                    sp.dma_start(er[:, q].rearrange("p j w -> p (j w)"), scratch.edge_row[bass.ds(k * CH, CH), :].rearrange(
                        "(p j) w -> p (j w)", j=TILES)).then_inc(idx_loaded[q], 16)

                def load_window(k, q, r):
                    hold(sp, ph.seen, m.begun, made(k - U))
                    sp.dma_start(win[:, q], edge_window(scratch, k * CH)).then_inc(win_loaded[q], 16)

                def store_x(k, q, r):
                    hold(sp, ph.seen, moved[q], per * r + per)
                    move_rows(sp, rows_of(scratch.xd, k * CH), x[:, q, 0:TILES].rearrange("p j f -> p (j f)"), xd_stored[q])

                def store_h(k, q, r):
                    hold(sp, ph.seen, m.h1d, made(k))
                    sp.dma_start(cols_of(scratch.hdT, k * CH), h1[:, q, 0]).then_inc(hd_stored[q], 16)
                    hold(sp, ph.seen, m.h1s, made(k))
                    sp.dma_start(cols_of(scratch.hsT, k * CH), h1[:, q, 1]).then_inc(hs_stored[q], 16)

                def store_y(k, q, r):
                    hold(sp, ph.seen, m.yw, made(k))
                    sp.dma_start(cols_of(scratch.ywT, k * CH), yw[:, q]).then_inc(yw_stored[q], 16)

                def store_rcnt(k, q, r):
                    hold(sp, ph.seen, m.rcnt, made(k))
                    sp.dma_start(cols_of(scratch.rcntT, k * CH), rcnt[:, q]).then_inc(rcnt_stored[q], 16)

                pipeline(sp, ECHUNK, U, [(0, load), (2, load_window), (2, store_x), (5, store_h), (5, store_rcnt), (5, store_y)])
                for q in range(U):
                    n = len(range(q, ECHUNK, U))
                    sp.wait_ge(moved[q], per * n)
                    sp.wait_ge(xd_stored[q], 16 + 32 * n)
                    for sems in (hd_stored, hs_stored, yw_stored, rcnt_stored):
                        sp.wait_ge(sems[q], 16 + 16 * n)

            @block.gpsimd
            def _(pool):
                def fetch(k, q, r):
                    pool.wait_ge(idx_loaded[q], 64 * r + 64)
                    pool.wait_ge(m.xn, made(k - U))
                    pool.wait_ge(xd_stored[q], 32 * r + 16)
                    gather(pool, ph.seen, x[:, q, 0:TILES], a["x"], di[:, q], moved[q])
                    gather(pool, ph.seen, x[:, q, TILES:N2], a["x"], si[:, q], moved[q])
                    scatter_ends(pool, ph.seen, scratch.node_map, er[:, q], ei[:, q], moved[q])

                def make_rstd(k, q, r):
                    pool.wait_ge(m.aggr, made(k))
                    pool.wait_ge(m.xn, made(k - U))
                    pool.tensor_tensor(ve[:, q], mv[:, q, :, 1], w.eps[0:TILE, 0:N2], ALU.add).then_inc(m.eps, 1)
                    pool.wait_ge(m.eps, made(k))
                    pool.tensor_tensor(rstd[:, q], ve[:, q], w.power[0:TILE, 0:N2], ALU.pow).then_inc(m.rstd, 1)

                pipeline(pool, ECHUNK, U, [(2, make_rstd), (0, fetch)])

            @block.vector
            def _(dve):
                dve.memset(ones[:], 1.0)
                dve.memset(cnt[:, U - 1, CH - 1:CH], 0.0).then_inc(m.init, 1)
                dve.wait_ge(m.init, made(0))

                def stats(k, q, r):
                    dve.wait_ge(moved[q], per * r + per)
                    dve.wait_ge(m.aggr, made(k - U))
                    norm_stats(dve, x[:, q], st[:, q], m.stats)

                def aggr(k, q, r):
                    dve.wait_ge(m.stats, made(k))
                    dve.wait_ge(m.xn, made(k - U))
                    norm_aggr(dve, st[:, q], mv[:, q], m.aggr_seen, m.aggr)

                def bias(k, q, r):
                    dve.wait_ge(m.rstd, made(k))
                    dve.wait_ge(m.xn, made(k - U))
                    norm_bias(dve, nb[:, q], mv[:, q], rstd[:, q], m.nb)

                def make_h1(k, q, r):
                    dve.wait_ge(m.w_in, made(k))
                    dve.wait_ge(m.xz, made(k - U))
                    dve.wait_ge(hd_stored[q], 16 * r + 16)
                    dve.wait_ge(hs_stored[q], 16 * r + 16)
                    dve.tensor_scalar(h1[:, q, 0], psW[0][:, 0:CH], w.b_in[:, 0:1], 0.0, ALU.add, ALU.max).then_inc(m.h1d, 1)
                    dve.tensor_scalar(h1[:, q, 1], psW[1][:, 0:CH], w.b_in[:, 0:1], 0.0, ALU.add, ALU.max).then_inc(m.h1s, 1)

                def make_cont(k, q, r):
                    dve.wait_ge(win_loaded[q], 16 * r + 16)
                    dve.wait_ge(m.ywn, made(k - 2))
                    dve.tensor_tensor(cont[:, q % 2], win[:, q, 2:CH + 2], win[:, q, 1:CH + 1], ALU.is_equal).then_inc(m.cont, 1)

                def count(k, q, r):
                    dve.wait_ge(m.cnt, made(k - 1))
                    dve.tensor_tensor(begun[:], win[:, q, 1:CH + 1], win[:, q, 0:CH], ALU.is_equal).then_inc(m.begun, 1)
                    dve.wait_ge(m.begun, made(k))
                    dve.tensor_tensor_scan(cnt[:, q], begun[:], ones[:], cnt[:, (q - 1) % U, CH - 1:CH], ALU.mult, ALU.add).then_inc(m.cnt, 1)
                    dve.wait_ge(m.cnt, made(k))
                    dve.wait_ge(rcnt_stored[q], 16 * r + 16)
                    dve.reciprocal(rcnt[:, q], cnt[:, q]).then_inc(m.rcnt, 1)

                def make_yw(k, q, r):
                    dve.wait_ge(m.sig, made(k))
                    dve.wait_ge(yw_stored[q], 16 * r + 16)
                    dve.scalar_tensor_tensor(out=yw[:, q], in0=psX[:, 0:CH], scalar=w.bskip[:, 0:1],
                                             in1=sig[:], op0=ALU.add, op1=ALU.mult).then_inc(m.yw, 1)
                    dve.wait_ge(m.yw, made(k))
                    dve.wait_ge(m.cont, made(k))
                    dve.wait_ge(m.ywstats, made(k - 1))
                    dve.scalar_tensor_tensor(out=ywn[:], in0=cont[:, q % 2], scalar=-1.0, in1=yw[:, q], op0=ALU.add, op1=ALU.mult).then_inc(m.ywn, 1)
                    dve.wait_ge(m.ywn, made(k))
                    dve.bn_stats(w.wends[:, bass.ds(k * 6, 6)], ywn[:]).then_inc(m.ywstats, 1)

                pipeline(dve, ECHUNK, U, [(0, stats), (0, aggr), (2, bias), (3, make_h1), (3, make_cont), (3, count), (3, make_yw)])

            @block.tensor
            def _(pe):
                def turn(k, q, r):
                    pe.wait_ge(m.xn, made(k))
                    pe.wait_ge(m.h0, made(k - 1))
                    for j in range(N2):
                        last = pe.transpose(psT[j // TILES][:, (j % TILES) * TILE:(j % TILES + 1) * TILE], xn[:, q % 2, j], w.ident[0:TILE, 0:TILE])
                    last.then_inc(m.xT, 1)

                def first(k, q, r):
                    pe.wait_ge(m.h0, made(k))
                    pe.wait_ge(m.h1s, made(k - 1))
                    for s in range(2):
                        last = pe.matmul(psW[s][:, 0:CH], w.W_in[:], h0[:, q % 2, s], start=True, stop=True)
                    last.then_inc(m.w_in, 1)

                def skip(k, q, r):
                    pe.wait_ge(m.h1d, made(k))
                    pe.wait_ge(m.yw, made(k - 1))
                    pe.matmul(psZ[:, 0:CH], w.gate_h[:, 0], h1[:, q, 0], start=True, stop=True)
                    pe.matmul(psX[:, 0:CH], w.Wskip[:, 0], h1[:, q, 0], start=True, stop=True).then_inc(m.xz, 1)

                pipeline(pe, ECHUNK, U, [(0, turn), (0, first), (0, skip)])

            @block.scalar
            def _(act):
                def make_xn(k, q, r):
                    act.wait_ge(m.nb, made(k))
                    act.wait_ge(m.xT, made(k - 2))
                    norm_relu(act, xn[:, q % 2], x[:, q], rstd[:, q], nb[:, q], m.xn)

                def make_h0(k, q, r):
                    act.wait_ge(m.xT, made(k))
                    act.wait_ge(m.w_in, made(k - 2))
                    act.activation(by_edge(h0[:, q % 2, 0]), by_tile(psT[0]), ACT.Identity)
                    act.activation(by_edge(h0[:, q % 2, 1]), by_tile(psT[1]), ACT.Identity).then_inc(m.h0, 1)

                def make_sig(k, q, r):
                    act.wait_ge(m.xz, made(k))
                    act.wait_ge(m.yw, made(k - 1))
                    act.activation(sig[:], psZ[:, 0:CH], ACT.Sigmoid, bias=w.gate_b[:, 0:1]).then_inc(m.sig, 1)

                pipeline(act, ECHUNK, U, [(0, make_xn), (0, make_h0), (0, make_sig)])


def attention(nc, a, w, scratch, l):
    U = 6
    D0 = 2 * l
    with phase(nc, f"att{l}") as ph:
        hd, hs = ph.sb("hd", [128, U, CH]), ph.sb("hs", [128, U, CH])
        ew = ph.sb("ew", [1, U, CH])
        win = ph.sb("win", [128, U, CH + 2], I32)
        qs, prod = ph.sb("qs", [128, 2, CH]), ph.sb("prod", [128, 2, CH])
        cont, apart = ph.sb("cont", [128, U, CH + 1]), ph.sb("apart", [128, 2, CH])
        mx = ph.sb("mx", [128, 2, CH + 1])
        ex, ee = ph.sb("ex", [128, 2, 2, CH]), ph.sb("ee", [128, 2, 2, CH])
        keep, pv = ph.sb("keep", [128, 2, CH]), ph.sb("pv", [128, 2, CH])
        den, num, lden, rden, dr, left, o0 = (ph.sb(n, [128, 2, CH]) for n in ("den", "num", "lden", "rden", "dr", "left", "o0"))
        o, th, dx, gx, y = (ph.sb(n, [128, 2, CH]) for n in ("o", "th", "dx", "gx", "y"))
        yn = ph.sb("yn", [128, U, CH])
        psQ, psK, psA, psX, psZ = (ph.ps(n) for n in ("psQ", "psK", "psA", "psX", "psZ"))
        psV = [ph.ps(f"psV{s}") for s in range(2)]
        in_loaded = ph.loaded("in_loaded", U)
        si = ph.sb("si", [TILE, U, TILES], I32)
        idx_loaded, moved = ph.loaded("idx_loaded", U), ph.loaded("moved", U)
        if l == 0:
            entry = ph.sb("entry", [TILE, U, TILES, MAPW], I32)
            sr = ph.sb("sr", [TILE, U, TILES], I32)
            sr_stored = ph.stored("sr_stored", U)
        else:
            rows = ph.sb("rows", [TILE, U, TILES, D])
            psT = ph.ps("psT")
        yn_stored = ph.stored("yn_stored", U)
        names = "sr xT hs qk v qs prod score cont apart mx0 mx ex ee keep pv den num lden seed dr left o0 o xz gated th dx gx y yn ystats init"
        m = Group(**{n: ph.stage(n + "_made") for n in names.split()})
        loads = 64 if l == 0 else 48
        fetched = m.xT if l else m.sr
        with nc.Block() as block:
            @block.sync
            def _(sp):
                ph.start(sp)

                def load_index(k, q, r):
                    hold(sp, ph.seen, fetched, made(k - U))
                    sp.dma_start(si[:, q], index_slot(scratch.src_row if l else a["src"], k * CH)).then_inc(idx_loaded[q], 16)

                def store_row(k, q, r):
                    hold(sp, ph.seen, m.sr, made(k))
                    sp.dma_start(index_slot(scratch.src_row, k * CH), sr[:, q]).then_inc(sr_stored[q], 16)

                def load(k, q, r):
                    hold(sp, ph.seen, m.gated, made(k - U))
                    sp.dma_start(hd[:, q], cols_of(scratch.hdT, k * CH)).then_inc(in_loaded[q], 16)
                    if l == 0:
                        sp.dma_start(hs[:, q], cols_of(scratch.hsT, k * CH)).then_inc(in_loaded[q], 16)
                    sp.dma_start(ew[:, q], a["edge_weight1"][bass.ds(k * CH, CH), :].rearrange("e o -> o e")).then_inc(in_loaded[q], 16)
                    hold(sp, ph.seen, m.cont, made(k - U))
                    sp.dma_start(win[:, q], edge_window(scratch, k * CH)).then_inc(in_loaded[q], 16)

                def store(k, q, r):
                    hold(sp, ph.seen, m.yn, made(k))
                    sp.dma_start(cols_of(scratch.ydT, k * CH), yn[:, q]).then_inc(yn_stored[q], 16)

                pipeline(sp, ECHUNK, U, [(0, load_index), (D0, load), (D0 + 7, store)] + [(5, store_row)] * (1 - l))
                for q in range(U):
                    sp.wait_ge(yn_stored[q], 16 + 16 * len(range(q, ECHUNK, U)))
                    if l == 0:
                        sp.wait_ge(sr_stored[q], 16 + 16 * len(range(q, ECHUNK, U)))

            @block.tensor
            def _(pe):
                def turn(k, q, r):
                    pe.wait_ge(moved[q], 16 * TILES * (r + 1))
                    pe.wait_ge(m.hs, made(k - 1))
                    to_T(pe, psT, rows[:, q], w.ident, m.xT)

                def query_key(k, q, r):
                    pe.wait_ge(in_loaded[q], loads * r + loads)
                    if l == 1:
                        pe.wait_ge(m.hs, made(k))
                    pe.wait_ge(m.qs, made(k - 1))
                    pe.wait_ge(m.prod, made(k - 1))
                    pe.matmul(psQ[:, 0:CH], w.Wq[:, l], hd[:, q], start=True, stop=True)
                    pe.matmul(psK[:, 0:CH], w.Wk[:, l], hs[:, q], start=True, stop=False)
                    pe.matmul(psK[:, 0:CH], w.We[:, l], ew[:, q], start=False, stop=True).then_inc(m.qk, 1)

                def value(k, q, r):
                    pe.wait_ge(m.pv, made(k - 2))
                    pe.matmul(psV[q % 2][:, 0:CH], w.Wv[:, l], hs[:, q], start=True, stop=False)
                    pe.matmul(psV[q % 2][:, 0:CH], w.We[:, l], ew[:, q], start=False, stop=True).then_inc(m.v, 1)

                def score(k, q, r):
                    pe.wait_ge(m.prod, made(k))
                    pe.wait_ge(m.ex, made(k - 1))
                    pe.matmul(psA[:, 0:CH], w.heads[:], prod[:, q % 2], start=True, stop=True).then_inc(m.score, 1)

                def skip(k, q, r):
                    pe.wait_ge(m.dx, made(k - 1))
                    pe.wait_ge(m.th, made(k - 1))
                    pe.matmul(psX[:, 0:CH], w.Wskip[:, l], hd[:, q], start=True, stop=True)
                    pe.matmul(psZ[:, 0:CH], w.gate_h[:, l], hd[:, q], start=True, stop=False).then_inc(m.xz, 1)

                def gate(k, q, r):
                    pe.wait_ge(m.o, made(k))
                    pe.matmul(psZ[:, 0:CH], w.gate_out[:, l], o[:, q % 2], start=False, stop=True).then_inc(m.gated, 1)

                pipeline(pe, ECHUNK, U, [(1, turn)] * l + [(D0 + 2, score), (D0 + 2, value), (D0, query_key), (D0 + 5, skip), (D0 + 5, gate)])

            @block.gpsimd
            def _(pool):
                def fetch(k, q, r):
                    pool.wait_ge(idx_loaded[q], 16 * r + 16)
                    pool.wait_ge(fetched, made(k - U))
                    if l == 0:
                        gather(pool, ph.seen, entry[:, q], scratch.node_map, si[:, q], moved[q])
                    else:
                        gather(pool, ph.seen, rows[:, q], scratch.h2, si[:, q], moved[q])

                def overshoot(k, q, r):
                    s = q % 2
                    pool.wait_ge(m.seed, made(k))
                    pool.wait_ge(m.left, made(k - 2))
                    pool.tensor_tensor(dr[:, s], den[:, s], rden[:, s], ALU.mult).then_inc(m.dr, 1)
                    pool.wait_ge(m.gated, made(k - 2))
                    pool.wait_ge(m.y, made(k - 2))
                    pool.wait_ge(m.num, made(k))
                    pool.tensor_tensor(o0[:, s], num[:, s], rden[:, s], ALU.mult).then_inc(m.o0, 1)

                def divide(k, q, r):
                    s = q % 2
                    pool.wait_ge(m.left, made(k))
                    pool.wait_ge(m.o0, made(k))
                    pool.tensor_tensor(o[:, s], o0[:, s], left[:, s], ALU.mult).then_inc(m.o, 1)

                pipeline(pool, ECHUNK, U, [(0, fetch), (D0 + 4, overshoot), (D0 + 4, divide)])

            @block.scalar
            def _(act):
                def source(k, q, r):
                    act.wait_ge(m.xT, made(k))
                    act.wait_ge(m.v, made(k - U))
                    act.activation(by_edge(hs[:, q]), by_tile(psT), ACT.Identity).then_inc(m.hs, 1)

                def query(k, q, r):
                    act.wait_ge(m.qk, made(k))
                    act.wait_ge(m.prod, made(k - 2))
                    act.activation(qs[:, q % 2], psQ[:, 0:CH], ACT.Identity, bias=w.bq[:, l:l + 1]).then_inc(m.qs, 1)

                def exps(k, q, r):
                    act.wait_ge(m.ex, made(k))
                    act.wait_ge(m.num, made(k - 2))
                    act.activation(ee[:, q % 2].rearrange("p a e -> p (a e)"), ex[:, q % 2].rearrange("p a e -> p (a e)"), ACT.Exp).then_inc(m.ee, 1)

                def gate(k, q, r):
                    act.wait_ge(m.gated, made(k))
                    act.wait_ge(m.gx, made(k - 2))
                    act.activation(th[:, q % 2], psZ[:, 0:CH], ACT.Tanh, bias=w.gate_bh[:, l:l + 1], scale=0.5).then_inc(m.th, 1)

                def guess(k, q, r):
                    s = q % 2
                    act.wait_ge(m.den, made(k))
                    act.wait_ge(m.seed, made(k - 2))
                    act.activation(lden[:, s], den[:, s], ACT.Ln).then_inc(m.lden, 1)
                    act.wait_ge(m.lden, made(k))
                    act.wait_ge(m.o0, made(k - 2))
                    act.activation(rden[:, s], lden[:, s], ACT.Exp, scale=-1.0).then_inc(m.seed, 1)

                def correct(k, q, r):
                    act.wait_ge(m.dr, made(k))
                    act.wait_ge(m.o, made(k - 2))
                    act.activation(left[:, q % 2], dr[:, q % 2], ACT.Identity, bias=w.two[:], scale=-1.0).then_inc(m.left, 1)

                pipeline(act, ECHUNK, U, [(1, source)] * l + [(D0 + 6, gate), (D0 + 1, query), (D0 + 3, exps), (D0 + 4, guess), (D0 + 4, correct)])

            @block.vector
            def _(dve):
                dve.memset(mx[:, 1, CH:CH + 1], 0.0)
                dve.memset(den[:, 1, CH - 1:CH], 0.0)
                dve.memset(num[:, 1, CH - 1:CH], 0.0).then_inc(m.init, 1)
                dve.wait_ge(m.init, made(0))

                def take_row(k, q, r):
                    dve.wait_ge(moved[q], 16 * TILES * (r + 1))
                    dve.wait_ge(sr_stored[q], 16 * r + 16)
                    dve.tensor_copy(sr[:, q], entry[:, q, :, 0]).then_inc(m.sr, 1)

                def product(k, q, r):
                    s = q % 2
                    dve.wait_ge(in_loaded[q], loads * r + loads)
                    dve.tensor_tensor(cont[:, q], win[:, q, 1:CH + 2], win[:, q, 0:CH + 1], ALU.is_equal).then_inc(m.cont, 1)
                    dve.wait_ge(m.cont, made(k))
                    dve.tensor_scalar(apart[:, s], cont[:, q, 0:CH], -1.0, BIG, ALU.add, ALU.mult).then_inc(m.apart, 1)
                    dve.wait_ge(m.qs, made(k))
                    dve.wait_ge(m.score, made(k - 2))
                    dve.scalar_tensor_tensor(out=prod[:, s], in0=psK[:, 0:CH], scalar=w.bk[:, l:l + 1], in1=qs[:, s],
                                             op0=ALU.add, op1=ALU.mult).then_inc(m.prod, 1)

                def maximum(k, q, r):
                    s, p = q % 2, 1 - q % 2
                    dve.wait_ge(m.mx, made(k - 1))
                    dve.tensor_copy(mx[:, s, 0:1], mx[:, p, CH:CH + 1]).then_inc(m.mx0, 1)
                    dve.wait_ge(m.score, made(k))
                    dve.wait_ge(m.apart, made(k))
                    dve.wait_ge(m.mx0, made(k))
                    dve.tensor_tensor_scan(mx[:, s, 1:CH + 1], apart[:, s], psA[:, 0:CH], mx[:, s, 0:1], ALU.add, ALU.max).then_inc(m.mx, 1)
                    dve.wait_ge(m.mx, made(k))
                    dve.wait_ge(m.ee, made(k - 2))
                    dve.tensor_tensor(ex[:, s, 1], psA[:, 0:CH], mx[:, s, 1:CH + 1], ALU.subtract)
                    dve.tensor_tensor(ex[:, s, 0], mx[:, s, 0:CH], mx[:, s, 1:CH + 1], ALU.subtract).then_inc(m.ex, 1)

                def sums(k, q, r):
                    s, p = q % 2, 1 - q % 2
                    dve.wait_ge(m.ee, made(k))
                    dve.wait_ge(m.v, made(k))
                    dve.scalar_tensor_tensor(out=keep[:, s], in0=ee[:, s, 0], scalar=1.0, in1=cont[:, q, 0:CH],
                                             op0=ALU.min, op1=ALU.mult).then_inc(m.keep, 1)
                    dve.scalar_tensor_tensor(out=pv[:, s], in0=psV[s][:, 0:CH], scalar=w.bv[:, l:l + 1], in1=ee[:, s, 1],
                                             op0=ALU.add, op1=ALU.mult).then_inc(m.pv, 1)
                    dve.wait_ge(m.keep, made(k))
                    dve.wait_ge(m.den, made(k - 1))
                    dve.wait_ge(m.dr, made(k - 2))
                    dve.tensor_tensor_scan(den[:, s], keep[:, s], ee[:, s, 1], den[:, p, CH - 1:CH], ALU.mult, ALU.add).then_inc(m.den, 1)
                    dve.wait_ge(m.pv, made(k))
                    dve.wait_ge(m.num, made(k - 1))
                    dve.wait_ge(m.o0, made(k - 2))
                    dve.tensor_tensor_scan(num[:, s], keep[:, s], pv[:, s], num[:, p, CH - 1:CH], ALU.mult, ALU.add).then_inc(m.num, 1)

                def combine(k, q, r):
                    s = q % 2
                    dve.wait_ge(m.xz, made(k))
                    dve.wait_ge(m.o, made(k))
                    dve.scalar_tensor_tensor(out=dx[:, s], in0=psX[:, 0:CH], scalar=w.bskip[:, l:l + 1], in1=o[:, s],
                                             op0=ALU.add, op1=ALU.subtract).then_inc(m.dx, 1)
                    dve.wait_ge(m.th, made(k))
                    dve.wait_ge(m.dx, made(k))
                    dve.scalar_tensor_tensor(out=gx[:, s], in0=th[:, s], scalar=1.0, in1=dx[:, s], op0=ALU.add, op1=ALU.mult).then_inc(m.gx, 1)
                    dve.wait_ge(m.gx, made(k))
                    dve.scalar_tensor_tensor(out=y[:, s], in0=gx[:, s], scalar=0.5, in1=o[:, s], op0=ALU.mult, op1=ALU.add).then_inc(m.y, 1)
                    dve.wait_ge(m.y, made(k))
                    dve.wait_ge(yn_stored[q], 16 * r + 16)
                    dve.wait_ge(m.ystats, made(k - U))
                    dve.scalar_tensor_tensor(out=yn[:, q], in0=cont[:, q, 1:CH + 1], scalar=-1.0, in1=y[:, s], op0=ALU.add, op1=ALU.mult).then_inc(m.yn, 1)
                    dve.wait_ge(m.yn, made(k))
                    dve.bn_stats(w.ends[:, bass.ds(k * 6, 6)], yn[:, q]).then_inc(m.ystats, 1)

                pipeline(dve, ECHUNK, U, [(D0 + 1, product), (D0 + 6, combine), (D0 + 2, maximum), (D0 + 3, sums)] + [(2, take_row)] * (1 - l))


def edge_update(nc, a, w, scratch, l):
    U = 6
    with phase(nc, f"upd{l}") as ph:
        yn, hd, yw = (ph.sb(n, [128, U, CH]) for n in ("yn", "hd", "yw"))
        xd = ph.sb("xd", [TILE, U, TILES, D])
        win = ph.sb("win", [128, U, CH + 2], I32)
        cont = ph.sb("cont", [128, U, CH])
        yb, act1, actw, sig, yw2, ywn = (ph.sb(n, [128, 2, CH]) for n in ("yb", "act1", "actw", "sig", "yw2", "ywn"))
        hn, hw = ph.sb("hn", [128, U, CH]), ph.sb("hw", [128, U, CH])
        rows = ph.sb("rows", [TILE, U, TILES, D])
        psR = [ph.ps(f"psR{s}") for s in range(2)]
        psX = [ph.ps(f"psX{s}") for s in range(2)]
        psZ = [ph.ps(f"psZ{s}") for s in range(2)]
        in_loaded = ph.loaded("in_loaded", U)
        hn_stored, rows_stored = ph.stored("hn_stored", U), ph.stored("rows_stored", U)
        names = "cont yb bn hn turned rows bnw hw xz sig yw2 ywn ywstats init"
        m = Group(**{n: ph.stage(n + "_made") for n in names.split()})
        table = scratch.h2 if l == 0 else scratch.x1
        last_of_slot = m.hw if l == 0 else m.rows
        col = lambda k: (ECHUNK - 1) * CH - k * CH
        with nc.Block() as block:
            @block.sync
            def _(sp):
                ph.start(sp)

                def load(k, q, r):
                    hold(sp, ph.seen, last_of_slot, made(k - U))
                    hold(sp, ph.seen, m.hn, made(k - U))
                    sp.dma_start(yn[:, q], cols_of(scratch.ydT, col(k))).then_inc(in_loaded[q], 16)
                    sp.dma_start(hd[:, q], cols_of(scratch.hdT, col(k))).then_inc(in_loaded[q], 16)
                    sp.dma_start(win[:, q], edge_window(scratch, col(k))).then_inc(in_loaded[q], 16)
                    if l == 0:
                        sp.dma_start(yw[:, q], cols_of(scratch.ywT, col(k))).then_inc(in_loaded[q], 16)
                    else:
                        sp.dma_start(flat(xd, q), rows_of(scratch.xd, col(k))).then_inc(in_loaded[q], 16)

                def store(k, q, r):
                    hold(sp, ph.seen, m.hn, made(k))
                    sp.dma_start(cols_of(scratch.hdT, col(k)), hn[:, q]).then_inc(hn_stored[q], 16)
                    hold(sp, ph.seen, m.rows, made(k))
                    move_rows(sp, rows_of(table, NODES + (ECHUNK - 1) * CH - k * CH), flat(rows, q), rows_stored[q])

                pipeline(sp, ECHUNK, U, [(0, load), (5, store)])
                for q in range(U):
                    sp.wait_ge(hn_stored[q], 16 + 16 * len(range(q, ECHUNK, U)))
                    sp.wait_ge(rows_stored[q], 16 + 32 * len(range(q, ECHUNK, U)))

            @block.vector
            def _(dve):
                dve.memset(yb[:, 1, 0:1], 0.0).then_inc(m.init, 1)
                dve.wait_ge(m.init, made(0))

                def spread(k, q, r):
                    dve.wait_ge(in_loaded[q], 64 * r + 64)
                    dve.tensor_tensor(cont[:, q], win[:, q, 2:CH + 2], win[:, q, 1:CH + 1], ALU.is_equal).then_inc(m.cont, 1)
                    dve.wait_ge(m.cont, made(k))
                    dve.wait_ge(m.yb, made(k - 1))
                    dve.wait_ge(m.bn, made(k - 2))
                    dve.tensor_tensor_scan(yb[:, q % 2, ::-1], cont[:, q, ::-1], yn[:, q, ::-1], yb[:, 1 - q % 2, 0:1],
                                           ALU.mult, ALU.subtract).then_inc(m.yb, 1)

                def make_h(k, q, r):
                    dve.wait_ge(m.bn, made(k))
                    dve.wait_ge(hn_stored[q], 16 * r + 16)
                    dve.wait_ge(m.turned, made(k - U))
                    dve.tensor_tensor(hn[:, q], act1[:, q % 2], hd[:, q], ALU.add).then_inc(m.hn, 1)
                    if l == 0:
                        dve.wait_ge(m.bnw, made(k))
                        dve.wait_ge(m.xz, made(k - U))
                        dve.tensor_tensor(hw[:, q], actw[:, q % 2], hd[:, q], ALU.add).then_inc(m.hw, 1)

                def make_rows(k, q, r):
                    dve.wait_ge(m.turned, made(k))
                    dve.wait_ge(rows_stored[q], 32 * r + 16)
                    dve.tensor_tensor(flat(rows, q), psR[q % 2][0:TILE], flat(xd, q), ALU.add).then_inc(m.rows, 1)

                def make_y(k, q, r):
                    dve.wait_ge(m.sig, made(k))
                    dve.scalar_tensor_tensor(out=yw2[:, q % 2], in0=psX[q % 2][:, 0:CH], scalar=w.bskip[:, 1:2],
                                             in1=sig[:, q % 2], op0=ALU.add, op1=ALU.mult).then_inc(m.yw2, 1)
                    dve.wait_ge(m.yw2, made(k))
                    dve.scalar_tensor_tensor(out=ywn[:, q % 2], in0=cont[:, q], scalar=-1.0, in1=yw2[:, q % 2], op0=ALU.add, op1=ALU.mult).then_inc(m.ywn, 1)
                    dve.wait_ge(m.ywn, made(k))
                    dve.bn_stats(w.wends[:, bass.ds(k * 6, 6)], ywn[:, q % 2]).then_inc(m.ywstats, 1)

                pipeline(dve, ECHUNK, U, [(0, spread), (2, make_h), (5, make_y) if l == 0 else (4, make_rows)])

            @block.scalar
            def _(act):
                def bn(k, q, r):
                    act.wait_ge(m.yb, made(k))
                    act.wait_ge(m.hn, made(k - 2))
                    act.activation(act1[:, q % 2], yb[:, q % 2], ACT.Relu, bias=w.bn[:, 1:2], scale=w.bn[:, 0:1]).then_inc(m.bn, 1)
                    if l == 0:
                        act.wait_ge(m.hw, made(k - 2))
                        act.activation(actw[:, q % 2], yw[:, q], ACT.Relu, bias=w.bn[:, 1:2], scale=w.bn[:, 0:1]).then_inc(m.bnw, 1)

                def make_sig(k, q, r):
                    act.wait_ge(m.xz, made(k))
                    act.wait_ge(m.yw2, made(k - 2))
                    act.activation(sig[:, q % 2], psZ[q % 2][:, 0:CH], ACT.Sigmoid, bias=w.gate_b[:, 1:2]).then_inc(m.sig, 1)
                    act.wait_ge(m.turned, made(k))
                    act.wait_ge(rows_stored[q], 32 * r + 16)
                    act.copy(flat(rows, q), psR[q % 2][0:TILE]).then_inc(m.rows, 1)

                pipeline(act, ECHUNK, U, [(4, make_sig), (1, bn)] if l == 0 else [(1, bn)])

            @block.tensor
            def _(pe):
                def turn(k, q, r):
                    pe.wait_ge(m.hn, made(k))
                    pe.wait_ge(m.rows, made(k - 2))
                    to_rows(pe, psR[q % 2], hn[:, q], w.ident, True, m.turned)
                    if l == 0:
                        pe.wait_ge(m.hw, made(k))
                        pe.wait_ge(m.yw2, made(k - 2))
                        pe.matmul(psZ[q % 2][:, 0:CH], w.gate_h[:, 1], hw[:, q], start=True, stop=True)
                        pe.matmul(psX[q % 2][:, 0:CH], w.Wskip[:, 1], hw[:, q], start=True, stop=True).then_inc(m.xz, 1)
                pipeline(pe, ECHUNK, U, [(3, turn)])


def edge_last(nc, a, w, scratch, out):
    U = 4
    N2 = 2 * TILES
    with phase(nc, "elast") as ph:
        si, ends = (ph.sb(n, [TILE, U, TILES], I32) for n in ("si", "ends"))
        x = ph.sb("x", [TILE, U, N2, D])
        xb = ph.sb("xb", [TILE, U, TILES, D])
        ea = ph.sb("ea", [TILE, U, TILES, D])
        xn = ph.sb("xn", [TILE, 2, N2, D])
        st = ph.sb("st", [TILE, U, N2, 6])
        mv = ph.sb("mv", [TILE, U, N2, 2])
        ve = ph.sb("ve", [TILE, U, N2])
        rstd, nb = ph.sb("rstd", [TILE, U, N2]), ph.sb("nb", [TILE, U, N2])
        g = ph.sb("g", [128, U, 2, CH])
        eT = ph.sb("eT", [128, 2, CH])
        win = ph.sb("win", [128, U, CH + 2], I32)
        cont = ph.sb("cont", [128, 2, CH])
        hid, hid2 = ph.sb("hid", [128, 2, 2, CH]), ph.sb("hid2", [128, 2, 2, CH])
        msg, tot = (ph.sb(n, [128, 2, CH]) for n in ("msg", "tot"))
        rcnt = ph.sb("rcnt", [128, U, CH])
        mean = ph.sb("mean", [128, 2, CH])
        o = ph.sb("o", [TILE, U, TILES, D])
        psT = [ph.ps(f"psT{s}") for s in range(2)]
        psH = [ph.ps(f"psH{s}") for s in range(2)]
        psG = [ph.ps(f"psG{s}") for s in range(2)]
        psM, psO = ph.ps("psM"), ph.ps("psO")
        idx_loaded, ends_loaded, x_loaded, ea_loaded, run_loaded = (
            ph.loaded(n, U) for n in ("idx_loaded", "ends_loaded", "x_loaded", "ea_loaded", "run_loaded"))
        moved, placed = ph.loaded("moved", U), ph.loaded("placed", U)
        names = ("xb stats aggr_seen aggr eps rstd nb xn xT g eaT eT cont hid0 hid1 hidden psm msg tot mean "
                 "hidden2 hid20 hid21 o_ps o init")
        m = Group(**{n: ph.stage(n + "_made") for n in names.split()})
        per = 16 * TILES
        with nc.Block() as block:
            @block.sync
            def _(sp):
                ph.start(sp)

                def load(k, q, r):
                    hold(sp, ph.seen, m.stats, made(k - U))
                    sp.dma_start(si[:, q], index_slot(scratch.src_row, k * CH)).then_inc(idx_loaded[q], 16)
                    hold(sp, ph.seen, m.xb, made(k - U))
                    hold(sp, ph.seen, m.xn, made(k - U))
                    sp.dma_start(x[:, q, 0:TILES].rearrange("p j f -> p (j f)"), rows_of(scratch.x1, NODES + k * CH)).then_inc(x_loaded[q], 16)

                def load_attr(k, q, r):
                    hold(sp, ph.seen, m.eaT, made(k - U))
                    sp.dma_start(flat(ea, q), rows_of(a["edge_attr_128"], k * CH)).then_inc(ea_loaded[q], 16)

                def load_run(k, q, r):
                    hold(sp, ph.seen, m.mean, made(k - U))
                    sp.dma_start(rcnt[:, q], cols_of(scratch.rcntT, k * CH)).then_inc(run_loaded[q], 16)
                    sp.dma_start(win[:, q], edge_window(scratch, k * CH)).then_inc(run_loaded[q], 16)

                def load_ends(k, q, r):
                    if not (isinstance(r, int) and r == 0):
                        hold(sp, ph.seen, placed[q], per * r)
                    sp.dma_start(ends[:, q], index_slot(scratch.end_index, k * CH)).then_inc(ends_loaded[q], 16)

                pipeline(sp, ECHUNK, U, [(0, load), (1, load_attr), (2, load_run), (5, load_ends)], peel=U)

            @block.gpsimd
            def _(pool):
                def fetch(k, q, r):
                    pool.wait_ge(idx_loaded[q], 16 * r + 16)
                    pool.wait_ge(m.xn, made(k - U))
                    gather(pool, ph.seen, x[:, q, TILES:N2], scratch.x1, si[:, q], moved[q])

                def make_rstd(k, q, r):
                    s = q
                    pool.wait_ge(m.aggr, made(k))
                    pool.wait_ge(m.xn, made(k - U))
                    pool.tensor_tensor(ve[:, s], mv[:, s, :, 1], w.eps[0:TILE, 0:N2], ALU.add).then_inc(m.eps, 1)
                    pool.wait_ge(m.eps, made(k))
                    pool.tensor_tensor(rstd[:, s], ve[:, s], w.power[0:TILE, 0:N2], ALU.pow).then_inc(m.rstd, 1)

                def add_bias(k, q, r):
                    pool.wait_ge(x_loaded[q], 16 * r + 16)
                    pool.wait_ge(m.o, made(k - U))
                    pool.tensor_tensor(xb[:, q], x[:, q, 0:TILES], w.b2b[:].rearrange("p (o f) -> p o f", o=1).to_broadcast([TILE, TILES, D]), ALU.add).then_inc(m.xb, 1)

                def place(k, q, r):
                    pool.wait_ge(ends_loaded[q], 16 * r + 16)
                    pool.wait_ge(m.o, made(k))
                    scatter_ends(pool, ph.seen, out, o[:, q], ends[:, q], placed[q])

                pipeline(pool, ECHUNK, U, [(2, make_rstd), (0, fetch), (3, add_bias), (7, place)], peel=U)
                for q in range(U):
                    pool.wait_ge(placed[q], per * len(range(q, ECHUNK, U)))

            @block.vector
            def _(dve):
                dve.memset(tot[:, 1, CH - 1:CH], 0.0).then_inc(m.init, 1)
                dve.wait_ge(m.init, made(0))

                def stats(k, q, r):
                    dve.wait_ge(moved[q], per * r + per)
                    dve.wait_ge(x_loaded[q], 16 * r + 16)
                    dve.wait_ge(m.aggr, made(k - U))
                    norm_stats(dve, x[:, q], st[:, q], m.stats)

                def aggr(k, q, r):
                    dve.wait_ge(m.stats, made(k))
                    dve.wait_ge(m.xn, made(k - U))
                    norm_aggr(dve, st[:, q], mv[:, q], m.aggr_seen, m.aggr)

                def bias(k, q, r):
                    dve.wait_ge(m.rstd, made(k))
                    dve.wait_ge(m.xn, made(k - U))
                    norm_bias(dve, nb[:, q], mv[:, q], rstd[:, q], m.nb)

                def half(k, q, r):
                    dve.wait_ge(m.hidden, made(k))
                    dve.wait_ge(m.psm, made(k - 2))
                    dve.tensor_scalar(hid[:, q % 2, 1], psH[1][:, 0:CH], w.b1a[:, 1:2], 0.0, ALU.add, ALU.max).then_inc(m.hid1, 1)

                def total(k, q, r):
                    s = q % 2
                    dve.wait_ge(run_loaded[q], 32 * r + 32)
                    dve.wait_ge(m.tot, made(k - 2))
                    dve.tensor_tensor(cont[:, s], win[:, q, 1:CH + 1], win[:, q, 0:CH], ALU.is_equal).then_inc(m.cont, 1)
                    dve.wait_ge(m.cont, made(k))
                    dve.wait_ge(m.msg, made(k))
                    dve.wait_ge(m.tot, made(k - 1))
                    dve.tensor_tensor_scan(tot[:, s], cont[:, s], msg[:, s], tot[:, 1 - s, CH - 1:CH], ALU.mult, ALU.add).then_inc(m.tot, 1)
                    dve.wait_ge(m.tot, made(k))
                    dve.wait_ge(m.hidden2, made(k - 2))
                    dve.tensor_tensor(mean[:, s], tot[:, s], rcnt[:, q], ALU.mult).then_inc(m.mean, 1)

                def half2(k, q, r):
                    dve.wait_ge(m.hidden2, made(k))
                    dve.wait_ge(m.o_ps, made(k - 2))
                    dve.tensor_scalar(hid2[:, q % 2, 1], psG[1][:, 0:CH], w.b2u[:, 1:2], 0.0, ALU.add, ALU.max).then_inc(m.hid21, 1)

                def output(k, q, r):
                    dve.wait_ge(m.o_ps, made(k))
                    dve.wait_ge(m.xb, made(k))
                    if not (isinstance(r, int) and r == 0):
                        dve.wait_ge(placed[q], per * r)
                    dve.tensor_tensor(flat(o, q), psO[0:TILE], flat(xb, q), ALU.add).then_inc(m.o, 1)

                pipeline(dve, ECHUNK, U, [(2, bias), (0, stats), (0, aggr), (6, output), (4, total), (5, half2), (3, half)], peel=U)

            @block.tensor
            def _(pe):
                def turn(k, q, r):
                    pe.wait_ge(m.xn, made(k))
                    pe.wait_ge(m.eT, made(k - 1))
                    for j in range(TILES):
                        for s in range(2):
                            last = pe.transpose(psT[s][:, j * TILE:(j + 1) * TILE], xn[:, q % 2, s * TILES + j], w.ident[0:TILE, 0:TILE])
                    last.then_inc(m.xT, 1)

                def message(k, q, r):
                    pe.wait_ge(m.hid0, made(k))
                    pe.wait_ge(m.hid1, made(k))
                    pe.wait_ge(m.msg, made(k - 1))
                    pe.matmul(psM[:, 0:CH], w.W1b[:, 0], hid[:, q % 2, 0], start=True, stop=False)
                    pe.matmul(psM[:, 0:CH], w.W1b[:, 1], hid[:, q % 2, 1], start=False, stop=True).then_inc(m.psm, 1)

                def output(k, q, r):
                    pe.wait_ge(m.hid20, made(k))
                    pe.wait_ge(m.hid21, made(k))
                    pe.wait_ge(m.o, made(k - 1))
                    for j in range(TILES):
                        for h in range(2):
                            last = pe.matmul(psO[0:TILE, j * D:(j + 1) * D], tile_cols(hid2[:, q % 2, h], j, True), w.W2b[:, h],
                                             start=(h == 0), stop=(h == 1))
                    last.then_inc(m.o_ps, 1)

                def turn_attr(k, q, r):
                    pe.wait_ge(ea_loaded[q], 16 * r + 16)
                    pe.wait_ge(m.g, made(k))
                    for j in range(TILES):
                        last = pe.transpose(psT[0][:, j * TILE:(j + 1) * TILE], ea[:, q, j], w.ident[0:TILE, 0:TILE])
                    last.then_inc(m.eaT, 1)

                def hidden(k, q, r):
                    pe.wait_ge(m.eT, made(k))
                    pe.wait_ge(m.hid0, made(k - 1))
                    pe.wait_ge(m.hid1, made(k - 1))
                    for h in range(2):
                        pe.matmul(psH[h][:, 0:CH], w.W1a[:, 0, h * 128:(h + 1) * 128], g[:, q, 1], start=True, stop=False)
                        last = pe.matmul(psH[h][:, 0:CH], w.W1a[:, 1, h * 128:(h + 1) * 128], eT[:, q % 2], start=False, stop=True)
                    last.then_inc(m.hidden, 1)

                def hidden2(k, q, r):
                    pe.wait_ge(m.mean, made(k))
                    pe.wait_ge(m.hid20, made(k - 1))
                    pe.wait_ge(m.hid21, made(k - 1))
                    for h in range(2):
                        pe.matmul(psG[h][:, 0:CH], w.W2a[:, 0, h * 128:(h + 1) * 128], g[:, q, 0], start=True, stop=False)
                        last = pe.matmul(psG[h][:, 0:CH], w.W2a[:, 1, h * 128:(h + 1) * 128], mean[:, q % 2], start=False, stop=True)
                    last.then_inc(m.hidden2, 1)

                pipeline(pe, ECHUNK, U, [(3, turn), (6, output), (4, message), (3, turn_attr), (5, hidden2), (3, hidden)])

            @block.scalar
            def _(act):
                def make_xn(k, q, r):
                    act.wait_ge(m.nb, made(k))
                    act.wait_ge(m.xT, made(k - 2))
                    norm_relu(act, xn[:, q % 2], x[:, q], rstd[:, q], nb[:, q], m.xn)

                def make_g(k, q, r):
                    act.wait_ge(m.xT, made(k))
                    act.wait_ge(m.hidden2, made(k - U))
                    act.activation(by_edge(g[:, q, 0]), by_tile(psT[0]), ACT.Identity)
                    act.activation(by_edge(g[:, q, 1]), by_tile(psT[1]), ACT.Identity).then_inc(m.g, 1)

                def make_msg(k, q, r):
                    act.wait_ge(m.psm, made(k))
                    act.wait_ge(m.tot, made(k - 2))
                    act.activation(msg[:, q % 2], psM[:, 0:CH], ACT.Identity, bias=w.b1b[:, 0:1]).then_inc(m.msg, 1)

                def make_eT(k, q, r):
                    act.wait_ge(m.eaT, made(k))
                    act.wait_ge(m.hidden, made(k - 2))
                    act.activation(by_edge(eT[:, q % 2]), by_tile(psT[0]), ACT.Identity).then_inc(m.eT, 1)

                def half(k, q, r):
                    act.wait_ge(m.hidden, made(k))
                    act.wait_ge(m.psm, made(k - 2))
                    act.activation(hid[:, q % 2, 0], psH[0][:, 0:CH], ACT.Relu, bias=w.b1a[:, 0:1]).then_inc(m.hid0, 1)

                def half2(k, q, r):
                    act.wait_ge(m.hidden2, made(k))
                    act.wait_ge(m.o_ps, made(k - 2))
                    act.activation(hid2[:, q % 2, 0], psG[0][:, 0:CH], ACT.Relu, bias=w.b2u[:, 0:1]).then_inc(m.hid20, 1)

                pipeline(act, ECHUNK, U, [(3, make_g), (2, make_xn), (4, make_msg), (3, make_eT), (5, half2), (3, half)])


def program(nc, a, out):
    dram = lambda n, s, d=F32: nc.dram_tensor(n, s, d, kind="Internal").ap()
    scratch = Group(
        dst_pad=dram("dst_pad", (1, EDGES + 2), I32), end_index=dram("end_index", (EDGES,), I32),
        node_map=dram("node_map", (NODES, MAPW), I32), edge_row=dram("edge_row", (EDGES, MAPW), I32),
        src_row=dram("src_row", (EDGES,), I32),
        hT=dram("hT", (128, NODES)), yT=dram("yT", (128, NODES)),
        h2=dram("h2_rows", (NODES + EDGES, D)), x1=dram("x1_rows", (NODES + EDGES, D)),
        xd=dram("xd_rows", (EDGES, D)), x1d=dram("x1d_rows", (EDGES, D)),
        hdT=dram("hdT", (128, EDGES)), hsT=dram("hsT", (128, EDGES)), ydT=dram("ydT", (128, EDGES)),
        ywT=dram("ywT", (128, EDGES)), rcntT=dram("rcntT", (128, EDGES)))
    with ExitStack() as ctx:
        sb = lambda n, s, d=F32: ctx.enter_context(nc.sbuf_tensor(n, s, d))
        L = LAYERS
        w = Group(
            W_in=sb("W_in", [128, D]), Wq=sb("Wq", [128, L, D]), Wk=sb("Wk", [128, L, D]), Wv=sb("Wv", [128, L, D]),
            Wskip=sb("Wskip", [128, L, D]), We=sb("We", [1, L, D]), gate_h=sb("gate_h", [128, L, D]),
            gate_out=sb("gate_out", [128, L, D]), heads=sb("heads", [128, D]), ident=sb("ident", [128, 128]),
            W1a=sb("W1a", [128, 2, 256]), W1b=sb("W1b", [128, 2, D]), W2a=sb("W2a", [128, 2, 256]),
            W2b=sb("W2b", [128, 2, D]), b_in=sb("b_in", [128, 1]), bq=sb("bq", [128, L]), bk=sb("bk", [128, L]),
            bv=sb("bv", [128, L]), bskip=sb("bskip", [128, L]), gamma=sb("gamma", [128, L]), beta=sb("beta", [128, L]),
            gate_b=sb("gate_b", [128, L]), gate_bh=sb("gate_bh", [128, L]), b1a=sb("b1a", [128, 2]),
            b1b=sb("b1b", [128, 1]), b2u=sb("b2u", [128, 2]), b2b=sb("b2b", [TILE, D]),
            power=sb("power", [128, 2 * TILES]), eps=sb("eps", [128, 2 * TILES]), two=sb("two", [128, 1]),
            ystats=sb("ystats", [128, 6 * NCHUNK]), ends=sb("ends", [128, 6 * ECHUNK]), wends=sb("wends", [128, 6 * ECHUNK]),
            bn=sb("bn", [128, 2]))
        prepare(nc, a, w, scratch)
        edge_first(nc, a, w, scratch)
        attention(nc, a, w, scratch, 0)
        dense_first(nc, a, w, scratch)
        batch_norm_params(nc, w, 0)
        edge_update(nc, a, w, scratch, 0)
        dense_second(nc, a, w, scratch)
        attention(nc, a, w, scratch, 1)
        batch_norm_params(nc, w, 1)
        edge_update(nc, a, w, scratch, 1)
        dense_last(nc, a, w, scratch, out)
        edge_last(nc, a, w, scratch, out)


_INS = ['x', 'src', 'dst', 'edge_attr_128', 'edge_weight1', 'L0_gnn_W_in', 'L0_gnn_b_in', 'L0_gnn_Wq', 'L0_gnn_bq',
        'L0_gnn_Wk', 'L0_gnn_bk', 'L0_gnn_Wv', 'L0_gnn_bv', 'L0_gnn_We', 'L0_gnn_Wskip', 'L0_gnn_bskip',
        'L0_gnn_Wbeta', 'L0_gnn_bn_gamma', 'L0_gnn_bn_beta', 'L1_gnn_u', 'L1_gnn_W1a', 'L1_gnn_b1a', 'L1_gnn_W1b',
        'L1_gnn_b1b', 'L1_gnn_W2a', 'L1_gnn_b2a', 'L1_gnn_W2b', 'L1_gnn_b2b']


def kernel(**inputs):
    import numpy as _np
    import concourse.bacc as _bacc
    from concourse import mybir as _mybir
    from concourse.bass_utils import run_bass_kernel_spmd as _run

    nc = _bacc.Bacc("TRN2", target_bir_lowering=False, num_devices=1)
    arrays, args = {}, {}
    for name in _INS:
        v = _np.ascontiguousarray(inputs[name])
        arrays[f"in_{name}"] = v
        args[name] = nc.dram_tensor(f"in_{name}", v.shape, _mybir.dt.from_np(v.dtype), kind="ExternalInput").ap()
    out = nc.dram_tensor("out", (NODES, D), F32, kind="ExternalOutput").ap()
    program(nc, args, out)
    return _run(nc, [arrays], core_ids=[0]).results[0]["out"]
```

```python
from collections import namedtuple
from contextlib import ExitStack, contextmanager

import concourse.bass as bass
from concourse import mybir

ALU = mybir.AluOpType
ACT = mybir.ActivationFunctionType
F32 = mybir.dt.float32
I32 = mybir.dt.int32

NODES, EDGES, D, HEADS, LAYERS = 50000, 12500, 128, 4, 2
HD = D // HEADS
TILE, TILES = 125, 4
CH = TILE * TILES
NCHUNK, ECHUNK = NODES // CH, EDGES // CH
SPLIT = 112
EPS = 1e-5
BIG = 3.0e38
MAPW = 16
NOWHERE = 1 << 20
AHEAD = 16


def Group(**named):
    return namedtuple("Group", named)(**named)


def made(k):
    return k + AHEAD + 1


def pipeline(eng, n, unroll, stages, peel=0):
    head = max(lag for lag, _ in stages) + peel
    turns = (n - head) // unroll

    def peeled(t):
        for lag, stage in stages:
            if 0 <= t - lag < n:
                stage(t - lag, (t - lag) % unroll, (t - lag) // unroll)

    for t in range(head):
        peeled(t)
    with eng.Fori(0, turns) as i:
        for s in range(unroll):
            for lag, stage in stages:
                d = head + s - lag
                stage(unroll * i + d, d % unroll, i + d // unroll)
    for t in range(head + unroll * turns, n + head - peel):
        peeled(t)


@contextmanager
def phase(nc, name):
    sems, begin = [], []

    def sem(n, at=0):
        sems.append(nc.alloc_semaphore(f"{name}_{n}"))
        if at:
            begin.append((sems[-1], at))
        return sems[-1]

    def start(eng):
        for s, at in begin:
            eng.sem_inc(s, at)

    with ExitStack() as ctx:
        yield Group(
            sb=lambda n, s, d=F32: ctx.enter_context(nc.sbuf_tensor(f"{name}_{n}", s, d)),
            ps=lambda n, s=(128, 512): ctx.enter_context(nc.psum_tensor(f"{name}_{n}", list(s), F32)),
            stage=lambda n: sem(n, AHEAD),
            count=lambda n: sem(n),
            loaded=lambda n, u: [sem(f"{n}{s}") for s in range(u)],
            stored=lambda n, u: [sem(f"{n}{s}", 16) for s in range(u)],
            seen=sem("sp_seen"), start=start)
        nc.all_engine_barrier()
        nc.clear_and_free_semaphores(sems)
        nc.all_engine_barrier()


def hold(sp, seen, sem, value):
    sp.wait_ge(sem, value)
    sp.sem_inc(seen, 1)



def rows_of(table, row0):
    return table[bass.ds(row0, CH), :].rearrange("(p j) f -> p (j f)", j=TILES)


def cols_of(table, col0, n=CH):
    return table[:, bass.ds(col0, n)]


def pair_rows(table, row0):
    return table[bass.ds(row0, 2 * CH), :].rearrange("(c p j) f -> p c (j f)", c=2, j=TILES)


def pair(buf, q):
    return buf[:, 2 * q:2 * q + 2].rearrange("p c j f -> p c (j f)")


def pair_cols(buf, q):
    return buf[:, 2 * q:2 * q + 2].rearrange("p c e -> p (c e)")


def move_rows(eng, out, in_, sem, n=16):
    eng.dma_start(out[0:SPLIT], in_[0:SPLIT]).then_inc(sem, n)
    eng.dma_start(out[SPLIT:TILE], in_[SPLIT:TILE]).then_inc(sem, n)


def flat(buf, q):
    return buf[:, q].rearrange("p j f -> p (j f)")


def tile_cols(t, j, ordered):
    return t[:, j:CH:TILES] if ordered else t[:, j * TILE:(j + 1) * TILE]


def by_tile(ps):
    return ps[:, 0:CH].rearrange("f (j p) -> f j p", j=TILES)


def in_order(t, ordered):
    return t.rearrange("f (p j) -> f j p", j=TILES) if ordered else t.rearrange("f (j p) -> f j p", j=TILES)



def prepare(nc, a, w, scratch):
    with phase(nc, "prep") as ph, nc.Block() as block:
        loaded, ones_made, pool_made = ph.count("loaded"), ph.count("ones_made"), ph.count("pool_made")
        dve_made, pe_made, act_made, written = (ph.count(n) for n in ("dve_made", "pe_made", "act_made", "written"))
        beta3 = ph.sb("beta3", [128, LAYERS, 3])
        wskipT = ph.sb("wskipT", [128, LAYERS, D])
        gate_x = ph.sb("gate_x", [128, LAYERS, D])
        gate_cols = ph.sb("gate_cols", [128, LAYERS, 2])
        ucol = ph.sb("ucol", [128, 1])
        b2a = ph.sb("b2a", [128, 2])
        w2u = ph.sb("w2u", [128, 256])
        ones = ph.sb("ones", [128, D])
        dsti = ph.sb("dsti", [TILE, ECHUNK, TILES], I32)
        nxt = ph.sb("nxt", [TILE, ECHUNK, TILES], I32)
        f1 = ph.sb("f1", [TILE, ECHUNK * TILES])
        f2 = ph.sb("f2", [TILE, ECHUNK * TILES])
        endi = ph.sb("endi", [TILE, ECHUNK, TILES], I32)
        ident_map = ph.sb("ident_map", [TILE, NODES // TILE, MAPW], I32)
        edge_rows = ph.sb("edge_rows", [TILE, ECHUNK, TILES, MAPW], I32)
        minus1 = ph.sb("minus1", [1, 2], I32)
        ps = ph.ps("small")
        psg = ph.ps("gate")
        n_loads = []

        @block.sync
        def _(sp):
            def load(dst, src):
                sp.dma_start(dst, src).then_inc(loaded, 16)
                n_loads.append(1)
            load(w.W_in[:], a["L0_gnn_W_in"])
            for l in range(LAYERS):
                load(w.Wq[:, l], a["L0_gnn_Wq"][l])
                load(w.Wk[:, l], a["L0_gnn_Wk"][l])
                load(w.Wv[:, l], a["L0_gnn_Wv"][l])
                load(w.Wskip[:, l], a["L0_gnn_Wskip"][l])
            load(w.W1a[:], a["L1_gnn_W1a"].rearrange("(b k) m -> k b m", k=128))
            load(w.W1b[:], a["L1_gnn_W1b"].rearrange("(b k) m -> k b m", k=128))
            load(w.W2a[:], a["L1_gnn_W2a"][0:256].rearrange("(b k) m -> k b m", k=128))
            load(w2u[:], a["L1_gnn_W2a"][256:384])
            load(w.W2b[:], a["L1_gnn_W2b"].rearrange("(b k) m -> k b m", k=128))
            load(w.We[:], a["L0_gnn_We"].rearrange("l o f -> o l f"))
            load(w.b2b[:], a["L1_gnn_b2b"].rearrange("(o f) -> o f", o=1).to_broadcast([TILE, D]))
            with nc.allow_non_contiguous_dma(reason="one word a partition"):
                load(w.b_in[:], a["L0_gnn_b_in"].rearrange("(f o) -> f o", o=1))
                for name, t in (("bq", w.bq), ("bk", w.bk), ("bv", w.bv), ("bskip", w.bskip),
                                ("bn_gamma", w.gamma), ("bn_beta", w.beta)):
                    load(t[:], a["L0_gnn_" + name].rearrange("l f -> f l"))
                load(beta3[:], a["L0_gnn_Wbeta"].rearrange("l (t f) o -> f l (t o)", t=3))
                load(ucol[:], a["L1_gnn_u"][0:1].rearrange("o f -> f o"))
                load(b2a[:], a["L1_gnn_b2a"].rearrange("(h f) -> f h", h=2))
                load(w.b1a[:], a["L1_gnn_b1a"].rearrange("(h f) -> f h", h=2))
                load(w.b1b[:], a["L1_gnn_b1b"].rearrange("(f o) -> f o", o=1))
            load(dsti[:], a["dst"].rearrange("(c p j) -> p c j", p=TILE, j=TILES))
            sp.wait_ge(pool_made, 1)
            c_last = ECHUNK - 1
            head = a["dst"][1:1 + c_last * CH]
            load(nxt[:, 0:c_last], head.rearrange("(c p j) -> p c j", p=TILE, j=TILES))
            tail = a["dst"][1 + c_last * CH:1 + c_last * CH + (TILE - 1) * TILES]
            load(nxt[0:TILE - 1, c_last], tail.rearrange("(p j) -> p j", j=TILES))
            load(nxt[TILE - 1:TILE, c_last, 0:TILES - 1], a["dst"][EDGES - TILES + 1:EDGES].rearrange("(o j) -> o j", o=1))
            sp.wait_ge(pool_made, 2)
            sp.dma_start(scratch.dst_pad[:, 0:1], minus1[:, 0:1]).then_inc(written, 16)
            sp.dma_start(scratch.dst_pad[:, EDGES + 1:EDGES + 2], minus1[:, 1:2]).then_inc(written, 16)
            sp.dma_start(scratch.dst_pad[:, 1:EDGES + 1], a["dst"].rearrange("(o e) -> o e", o=1)).then_inc(written, 16)
            sp.wait_ge(pool_made, 4)
            sp.dma_start(scratch.node_map.rearrange("(p n) w -> p (n w)", p=TILE), ident_map[:].rearrange("p n w -> p (n w)")).then_inc(written, 16)
            for c in range(ECHUNK):
                sp.dma_start(scratch.edge_row[c * CH:(c + 1) * CH].rearrange("(p j) w -> p (j w)", j=TILES),
                             edge_rows[:, c].rearrange("p j w -> p (j w)")).then_inc(written, 16)
            sp.wait_ge(dve_made, 99)
            sp.dma_start(scratch.end_index.rearrange("(c p j) -> p c j", p=TILE, j=TILES), endi[:]).then_inc(written, 16)
            sp.wait_ge(written, 16 * (5 + ECHUNK))

        all_loaded = 16 * len(n_loads)

        @block.gpsimd
        def _(pool):
            pool.memset(nxt[:], -1).then_inc(pool_made, 1)
            pool.memset(minus1[:], -1).then_inc(pool_made, 1)
            pool.iota(ident_map[:], [[1, NODES // TILE], [0, MAPW]], base=0, channel_multiplier=NODES // TILE).then_inc(pool_made, 1)
            pool.iota(edge_rows[:], [[CH, ECHUNK], [1, TILES], [0, MAPW]], base=NODES, channel_multiplier=TILES).then_inc(pool_made, 1)
            pool.memset(ones[:], 1.0).then_inc(ones_made, 1)
            pool.memset(w.ident[:], 0.0).then_inc(ones_made, 1)
            pool.memset(w.heads[:], 0.0).then_inc(ones_made, 1)
            pool.memset(w.power[:], -0.5).then_inc(ones_made, 1)
            pool.memset(w.eps[:], EPS).then_inc(ones_made, 1)
            pool.memset(w.two[:], 2.0).then_inc(ones_made, 1)
            pool.wait_ge(ones_made, 6)
            pool.affine_select(out=w.ident[:], in_=w.ident[:], compare_op=ALU.not_equal, fill=1.0, base=0,
                               pattern=[[-1, 128]], channel_multiplier=1).then_inc(ones_made, 1)

        @block.vector
        def _(dve):
            n = 0

            def after(ins):
                nonlocal n
                n += 1
                ins.then_inc(dve_made, 1)
                dve.wait_ge(dve_made, n)

            dve.wait_ge(loaded, all_loaded)
            dve.wait_ge(ones_made, 7)
            for h in range(HEADS):
                dve.memset(w.heads[h * HD:(h + 1) * HD, h * HD:(h + 1) * HD], float(HD) ** -0.5)
            for l in range(LAYERS):
                after(dve.tensor_tensor(gate_cols[:, l, 0:1], beta3[:, l, 0:1], beta3[:, l, 2:3], ALU.add))
                after(dve.tensor_tensor(gate_cols[:, l, 1:2], beta3[:, l, 1:2], beta3[:, l, 2:3], ALU.subtract))
                after(dve.tensor_scalar(w.gate_out[:, l], ones[:], gate_cols[:, l, 0:1], None, ALU.mult))
                after(dve.tensor_scalar(gate_x[:, l], ones[:], gate_cols[:, l, 1:2], None, ALU.mult))
            dve.wait_ge(pe_made, 1)
            after(dve.tensor_copy(wskipT[:].rearrange("p l f -> p (l f)"), ps[:, 0:LAYERS * D]))
            dve.wait_ge(pe_made, 2)
            after(dve.tensor_copy(w.gate_h[:].rearrange("p l f -> p (l f)"), psg[:, 0:LAYERS * D]))
            after(dve.tensor_copy(w.gate_b[:], psg[:, LAYERS * D:LAYERS * D + LAYERS]))
            after(dve.tensor_scalar(w.gate_bh[:], w.gate_b[:], 0.5, None, ALU.mult))
            after(dve.tensor_tensor(w.b2u[:], psg[:, 300:302], b2a[:], ALU.add))
            d, e = dsti[:].rearrange("p c j -> p (c j)"), nxt[:].rearrange("p c j -> p (c j)")
            after(dve.tensor_tensor(f1[:], d, e, ALU.not_equal))
            after(dve.scalar_tensor_tensor(out=f2[:], in0=d, scalar=float(-NOWHERE), in1=f1[:], op0=ALU.add, op1=ALU.mult))
            after(dve.tensor_scalar(endi[:].rearrange("p c j -> p (c j)"), f2[:], float(NOWHERE), None, ALU.add))
            dve.sem_inc(dve_made, 99 - n)

        @block.tensor
        def _(pe):
            pe.wait_ge(loaded, all_loaded)
            pe.wait_ge(ones_made, 7)
            for l in range(LAYERS):
                last = pe.transpose(ps[:, l * D:(l + 1) * D], w.Wskip[:, l], w.ident[:])
            last.then_inc(pe_made, 1)
            pe.wait_ge(dve_made, 4 * LAYERS + 1)
            for l in range(LAYERS):
                pe.matmul(psg[:, l * D:(l + 1) * D], wskipT[:, l], gate_x[:, l], start=True, stop=True)
                pe.matmul(psg[:, LAYERS * D + l:LAYERS * D + l + 1], gate_x[:, l], w.bskip[:, l:l + 1], start=True, stop=True)
            for h in range(2):
                last = pe.matmul(psg[:, 300 + h:301 + h], w2u[:, h * 128:(h + 1) * 128], ucol[:], start=True, stop=True)
            last.then_inc(pe_made, 1)



def norm_stats(dve, x, st, stats_made):
    for j in range(x.shape[1]):
        last = dve.bn_stats(st[:, j], x[:, j])
    last.then_inc(stats_made, 1)


def norm_aggr(dve, st, mv, stats_seen, aggr_made):
    dve.sem_inc(stats_seen, 1)
    for j in range(st.shape[1]):
        last = dve.bn_aggr(mv[:, j], st[:, j])
    last.then_inc(aggr_made, 1)


def norm_bias(dve, nb, mv, rstd, sem):
    dve.scalar_tensor_tensor(out=nb, in0=mv[:, :, 0], scalar=-1.0, in1=rstd, op0=ALU.mult, op1=ALU.mult).then_inc(sem, 1)


def norm_relu(act, xn, x, rstd, nb, sem):
    for j in range(x.shape[1]):
        last = act.activation(xn[:, j], x[:, j], ACT.Relu, bias=nb[:, j:j + 1], scale=rstd[:, j:j + 1])
    last.then_inc(sem, 1)


def to_T(pe, ps, rows, ident, sem):
    for j in range(TILES):
        last = pe.transpose(ps[:, j * TILE:(j + 1) * TILE], rows[:, j], ident[0:TILE, 0:TILE])
    last.then_inc(sem, 1)


def to_rows(pe, ps, t, ident, ordered, sem):
    for j in range(TILES):
        last = pe.transpose(ps[0:TILE, j * D:(j + 1) * D], tile_cols(t, j, ordered), ident[:])
    last.then_inc(sem, 1)


def first_layer_in(nc, a, w, scratch):
    U, DST, SRC = 6, 4, 5
    chunks = NCHUNK + 2 * ECHUNK
    with phase(nc, "first") as ph:
        index = ph.sb("index", [TILE, 2, TILES], I32)
        x = ph.sb("x", [TILE, U, TILES, D])
        xn = ph.sb("xn", [TILE, 2, TILES, D])
        st = ph.sb("st", [TILE, 2, TILES, 6])
        mv = ph.sb("mv", [TILE, U, TILES, 2])
        ve, rstd, nb = (ph.sb(n, [TILE, U, TILES]) for n in ("ve", "rstd", "nb"))
        h0, sig = ph.sb("h0", [128, 2, CH]), ph.sb("sig", [128, 2, CH])
        h1, y = ph.sb("h1", [128, U, CH]), ph.sb("y", [128, U, CH])
        win = ph.sb("win", [128, CH + 2], I32)
        cont, ywn = ph.sb("cont", [128, CH]), ph.sb("ywn", [128, CH])
        psT, psW, psX, psZ = ([ph.ps(f"{n}{s}") for s in range(2)] for n in ("psT", "psW", "psX", "psZ"))
        x_loaded = ph.loaded("x_loaded", U)
        index_loaded, win_loaded = ph.loaded("index_loaded", 2), ph.count("win_loaded")
        xd_stored = ph.stored("xd_stored", 1)[0]
        h1_stored, y_stored = ph.stored("h1_stored", U), ph.stored("y_stored", U)
        names = "stats seen aggr eps rstd nb xn xT h0 w_in h1 xz sig y ystats cont ywn"
        m = Group(**{n: ph.stage(n + "_made") for n in names.split()})
        x_full = lambda q: 32 if q < DST else 16 * TILES

        def chunk(q, r):
            return (4 * r + q) * CH if q < DST else r * CH

        def kept(q, r, back=0):
            q -= back
            if q < 0:
                q, r = q + U, r - 1
            return made(5 * r + min(q, DST))

        with nc.Block() as block:
            @block.sync
            def _(sp):
                ph.start(sp)

                def load(k, q, r):
                    if q < DST:
                        hold(sp, ph.seen, m.xn, made(k - U))
                        move_rows(sp, flat(x, q), rows_of(a["x"], chunk(q, r)), x_loaded[q])

                def load_index(end, r):
                    if not (isinstance(r, int) and r == 0):
                        hold(sp, ph.seen, x_loaded[DST + end], x_full(DST) * r)
                    sp.dma_start(index[:, end], index_slot(a["src" if end else "dst"], r * CH)).then_inc(index_loaded[end], 16)

                def load_dst(k, q, r):
                    if q == 0:
                        load_index(0, r)

                def load_src(k, q, r):
                    if q == 2:
                        load_index(1, r)

                def store_x(k, q, r):
                    if q == DST:
                        hold(sp, ph.seen, x_loaded[q], x_full(q) * (r + 1))
                        move_rows(sp, rows_of(scratch.xd, r * CH), flat(x, q), xd_stored)

                def load_window(k, q, r):
                    if q == DST:
                        hold(sp, ph.seen, m.ywn, made(r - 1))
                        sp.dma_start(win[:], edge_window(scratch, r * CH)).then_inc(win_loaded, 16)

                def store_h(k, q, r):
                    table = scratch.hT if q < DST else scratch.hdT if q == DST else scratch.hsT
                    hold(sp, ph.seen, m.h1, made(k))
                    sp.dma_start(cols_of(table, chunk(q, r)), h1[:, q]).then_inc(h1_stored[q], 16)

                def store_y(k, q, r):
                    if q != SRC:
                        hold(sp, ph.seen, m.y, kept(q, r))
                        sp.dma_start(cols_of(scratch.yT if q < DST else scratch.ywT, chunk(q, r)), y[:, q]).then_inc(y_stored[q], 16)

                load_index(0, 0)
                pipeline(sp, chunks, U, [(-1, load_dst), (0, load_src), (0, load), (2, store_x), (7, load_window), (9, store_h), (13, store_y)])
                sp.wait_ge(xd_stored, 16 + 32 * ECHUNK)
                for q in range(U):
                    sp.wait_ge(h1_stored[q], 16 + 16 * (chunks // U))
                    if q != SRC:
                        sp.wait_ge(y_stored[q], 16 + 16 * (chunks // U))

            @block.gpsimd
            def _(pool):
                def fetch(k, q, r):
                    if q < 2:
                        return
                    end, half = (q - 2) // 2, q % 2
                    to = DST + end
                    pool.wait_ge(index_loaded[end], 16 * r + 16)
                    pool.wait_ge(m.xn, made(k - q + to - U))
                    if end == 0:
                        pool.wait_ge(xd_stored, 32 * r + 16)
                    pool.sem_inc(ph.seen, 1)
                    for j in (2 * half, 2 * half + 1):
                        pool.indirect_dma_start(x[:, to, j], None, a["x"], bass.IndirectOffsetOnAxis(index[:, end, j:j + 1], 0),
                                                bounds_check=NODES - 1, oob_is_err=False).then_inc(x_loaded[to], 16)

                def make_rstd(k, q, r):
                    pool.wait_ge(m.aggr, made(k))
                    pool.wait_ge(m.xn, made(k - U))
                    pool.tensor_tensor(ve[:, q], mv[:, q, :, 1], w.eps[0:TILE, 0:TILES], ALU.add).then_inc(m.eps, 1)
                    pool.wait_ge(m.eps, made(k))
                    pool.tensor_tensor(rstd[:, q], ve[:, q], w.power[0:TILE, 0:TILES], ALU.pow).then_inc(m.rstd, 1)

                pipeline(pool, chunks, U, [(3, make_rstd), (0, fetch)])

            @block.vector
            def _(dve):
                def stats(k, q, r):
                    dve.wait_ge(x_loaded[q], x_full(q) * (r + 1))
                    dve.wait_ge(m.aggr, made(k - 2))
                    norm_stats(dve, x[:, q], st[:, q % 2], m.stats)

                def aggr(k, q, r):
                    dve.wait_ge(m.stats, made(k))
                    dve.wait_ge(m.xn, made(k - U))
                    norm_aggr(dve, st[:, q % 2], mv[:, q], m.seen, m.aggr)

                def bias(k, q, r):
                    dve.wait_ge(m.rstd, made(k))
                    dve.wait_ge(m.xn, made(k - U))
                    norm_bias(dve, nb[:, q], mv[:, q], rstd[:, q], m.nb)

                def make_h1(k, q, r):
                    dve.wait_ge(m.w_in, made(k))
                    if q != SRC:
                        dve.wait_ge(m.xz, kept(q, r, U))
                    dve.wait_ge(h1_stored[q], 16 * r + 16)
                    dve.tensor_scalar(h1[:, q], psW[q % 2][:, 0:CH], w.b_in[:, 0:1], 0.0, ALU.add, ALU.max).then_inc(m.h1, 1)

                def make_y(k, q, r):
                    if q == SRC:
                        return
                    dve.wait_ge(m.sig, kept(q, r))
                    dve.wait_ge(m.ystats, kept(q, r, U))
                    dve.wait_ge(y_stored[q], 16 * r + 16)
                    dve.scalar_tensor_tensor(out=y[:, q], in0=psX[q % 2][:, 0:CH], scalar=w.bskip[:, 0:1],
                                             in1=sig[:, q % 2], op0=ALU.add, op1=ALU.mult).then_inc(m.y, 1)

                def ystats(k, q, r):
                    if q == SRC:
                        return
                    if q < DST:
                        dve.wait_ge(m.y, kept(q, r))
                        dve.bn_stats(w.ystats[:, bass.ds((4 * r + q) * 6, 6)], y[:, q]).then_inc(m.ystats, 1)
                        return
                    dve.wait_ge(win_loaded, 16 * r + 16)
                    dve.wait_ge(m.ywn, made(r - 1))
                    dve.tensor_tensor(cont[:], win[:, 2:CH + 2], win[:, 1:CH + 1], ALU.is_equal).then_inc(m.cont, 1)
                    dve.wait_ge(m.cont, made(r))
                    dve.wait_ge(m.y, kept(q, r))
                    dve.wait_ge(m.ystats, kept(q, r, 1))
                    dve.scalar_tensor_tensor(out=ywn[:], in0=cont[:], scalar=-1.0, in1=y[:, q], op0=ALU.add, op1=ALU.mult).then_inc(m.ywn, 1)
                    dve.wait_ge(m.ywn, made(r))
                    dve.bn_stats(w.wends[:, bass.ds(r * 6, 6)], ywn[:]).then_inc(m.ystats, 1)

                pipeline(dve, chunks, U, [(4, bias), (8, make_h1), (2, stats), (11, make_y), (2, aggr), (12, ystats)])

            @block.tensor
            def _(pe):
                def turn(k, q, r):
                    pe.wait_ge(m.xn, made(k))
                    pe.wait_ge(m.h0, made(k - 2))
                    to_T(pe, psT[q % 2], xn[:, q % 2], w.ident, m.xT)

                def first(k, q, r):
                    pe.wait_ge(m.h0, made(k))
                    pe.wait_ge(m.h1, made(k - 2))
                    pe.matmul(psW[q % 2][:, 0:CH], w.W_in[:], h0[:, q % 2], start=True, stop=True).then_inc(m.w_in, 1)

                def skip(k, q, r):
                    if q == SRC:
                        return
                    pe.wait_ge(m.h1, made(k))
                    pe.wait_ge(m.y, kept(q, r, 2))
                    pe.matmul(psZ[q % 2][:, 0:CH], w.gate_h[:, 0], h1[:, q], start=True, stop=True)
                    pe.matmul(psX[q % 2][:, 0:CH], w.Wskip[:, 0], h1[:, q], start=True, stop=True).then_inc(m.xz, 1)

                pipeline(pe, chunks, U, [(5, turn), (7, first), (9, skip)])

            @block.scalar
            def _(act):
                def make_xn(k, q, r):
                    act.wait_ge(m.nb, made(k))
                    act.wait_ge(m.xT, made(k - 2))
                    norm_relu(act, xn[:, q % 2], x[:, q], rstd[:, q], nb[:, q], m.xn)

                def make_h0(k, q, r):
                    act.wait_ge(m.xT, made(k))
                    act.wait_ge(m.w_in, made(k - 2))
                    if q < DST:
                        act.activation(h0[:, q % 2], psT[q % 2][:, 0:CH], ACT.Identity).then_inc(m.h0, 1)
                    else:
                        act.activation(by_edge(h0[:, q % 2]), by_tile(psT[q % 2]), ACT.Identity).then_inc(m.h0, 1)

                def make_sig(k, q, r):
                    if q == SRC:
                        return
                    act.wait_ge(m.xz, kept(q, r))
                    act.wait_ge(m.y, kept(q, r, 2))
                    act.activation(sig[:, q % 2], psZ[q % 2][:, 0:CH], ACT.Sigmoid, bias=w.gate_b[:, 0:1]).then_inc(m.sig, 1)

                pipeline(act, chunks, U, [(6, make_h0), (4, make_xn), (10, make_sig)])


def batch_norm_params(nc, w, l):
    with phase(nc, f"bn{l}") as ph, nc.Block() as block:
        done, pool_done = ph.count("dve_done"), ph.count("pool_done")
        agg = ph.sb("agg", [128, 3, 2])
        sq = ph.sb("sq", [128, 3])
        tmp = ph.sb("tmp", [128, 8])
        rs = ph.sb("rs", [128, 4])
        ratio = EDGES / NODES

        @block.vector
        def _(dve):
            n = 0

            def after(ins):
                nonlocal n
                n += 1
                ins.then_inc(done, 1)
                dve.wait_ge(done, n)
            after(dve.bn_aggr(agg[:, 0], w.ystats[:]))
            after(dve.bn_aggr(agg[:, 1], w.wends[:]))
            after(dve.bn_aggr(agg[:, 2], w.ends[:]))
            after(dve.tensor_tensor(sq[:], agg[:, :, 0], agg[:, :, 0], ALU.mult))
            after(dve.tensor_tensor(sq[:], sq[:], agg[:, :, 1], ALU.add))
            after(dve.tensor_tensor(tmp[:, 0:1], agg[:, 1, 0:1], agg[:, 2, 0:1], ALU.subtract))
            after(dve.scalar_tensor_tensor(out=tmp[:, 1:2], in0=tmp[:, 0:1], scalar=ratio, in1=agg[:, 0, 0:1], op0=ALU.mult, op1=ALU.add))
            after(dve.tensor_tensor(tmp[:, 2:3], sq[:, 2:3], sq[:, 1:2], ALU.subtract))
            after(dve.scalar_tensor_tensor(out=tmp[:, 3:4], in0=tmp[:, 2:3], scalar=ratio, in1=sq[:, 0:1], op0=ALU.mult, op1=ALU.add))
            after(dve.tensor_tensor(tmp[:, 4:5], tmp[:, 1:2], tmp[:, 1:2], ALU.mult))
            after(dve.tensor_tensor(tmp[:, 5:6], tmp[:, 3:4], tmp[:, 4:5], ALU.subtract))
            after(dve.tensor_scalar(rs[:, 0:1], tmp[:, 5:6], 0.0, EPS, ALU.max, ALU.add))
            dve.wait_ge(pool_done, 1)
            after(dve.tensor_tensor(w.bn[:, 0:1], w.gamma[:, l:l + 1], rs[:, 1:2], ALU.mult))
            after(dve.tensor_tensor(tmp[:, 6:7], tmp[:, 1:2], w.bn[:, 0:1], ALU.mult))
            after(dve.tensor_tensor(w.bn[:, 1:2], w.beta[:, l:l + 1], tmp[:, 6:7], ALU.subtract))

        @block.gpsimd
        def _(pool):
            pool.wait_ge(done, 12)
            pool.tensor_tensor(rs[:, 1:2], rs[:, 0:1], w.power[:, 0:1], ALU.pow).then_inc(pool_done, 1)


def dense_second(nc, a, w, scratch):
    U = 8
    with phase(nc, "second") as ph:
        yin = ph.sb("yin", [128, U, CH])
        hin = ph.sb("hin", [128, U, CH])
        act1 = ph.sb("act1", [128, 2, CH])
        h2 = ph.sb("h2", [128, U, CH])
        rows = ph.sb("rows", [TILE, U, TILES, D])
        sig = ph.sb("sig", [128, 2, CH])
        y = ph.sb("y", [128, U, CH])
        psR = [ph.ps(f"psR{s}") for s in range(2)]
        psX = [ph.ps(f"psX{s}") for s in range(2)]
        psZ = [ph.ps(f"psZ{s}") for s in range(2)]
        y_loaded, h_loaded = ph.loaded("y_loaded", U // 2), ph.loaded("h_loaded", U // 2)
        rows_stored, rows_stored2, y_stored = (ph.stored(n, U // 2) for n in ("rows_stored", "rows_stored2", "y_stored"))
        src, src_row = ph.sb("src", [TILE, NCHUNK], I32), ph.sb("src_row", [TILE, NCHUNK], I32)
        si, entry = ph.sb("si", [TILE, U, 1], I32), ph.sb("entry", [TILE, U, MAPW], I32)
        src_loaded, src_stored, looked_up = ph.count("src_loaded"), ph.count("src_stored"), ph.loaded("looked_up", U)
        m = Group(**{n: ph.stage(n + "_made") for n in "si row bn h2 turned rows xz sig y ystats".split()})
        with nc.Block() as block:
            @block.sync
            def _(sp):
                ph.start(sp)
                sp.dma_start(src[:], a["src"].rearrange("(p t) -> p t", t=NCHUNK)).then_inc(src_loaded, 16)

                def load(t, q, r):
                    hold(sp, ph.seen, m.bn, made(2 * t + 1 - U))
                    sp.dma_start(pair_cols(yin, q), cols_of(scratch.yT, t * 2 * CH, 2 * CH)).then_inc(y_loaded[q], 16)
                    hold(sp, ph.seen, m.h2, made(2 * t + 1 - U))
                    sp.dma_start(pair_cols(hin, q), cols_of(scratch.hT, t * 2 * CH, 2 * CH)).then_inc(h_loaded[q], 16)

                def store_rows(t, q, r):
                    hold(sp, ph.seen, m.rows, made(2 * t + 1))
                    dst = pair_rows(scratch.h2, t * 2 * CH)
                    sp.dma_start(dst[0:SPLIT], pair(rows, q)[0:SPLIT]).then_inc(rows_stored[q], 16)
                    sp.dma_start(dst[SPLIT:TILE], pair(rows, q)[SPLIT:TILE]).then_inc(rows_stored2[q], 16)

                def store_y(t, q, r):
                    hold(sp, ph.seen, m.y, made(2 * t + 1))
                    sp.dma_start(cols_of(scratch.yT, t * 2 * CH, 2 * CH), pair_cols(y, q)).then_inc(y_stored[q], 16)

                pipeline(sp, NCHUNK // 2, U // 2, [(0, load), (5, store_rows), (6, store_y)])
                sp.wait_ge(m.row, made(NCHUNK - 1))
                sp.dma_start(scratch.src_row.rearrange("(p t) -> p t", t=NCHUNK), src_row[:]).then_inc(src_stored, 16)
                sp.wait_ge(src_stored, 16)
                for sems in (rows_stored, rows_stored2, y_stored):
                    for q in range(U // 2):
                        sp.wait_ge(sems[q], 16 + 16 * len(range(q, NCHUNK // 2, U // 2)))

            @block.scalar
            def _(act):
                def bn(k, q, r):
                    act.wait_ge(y_loaded[q // 2], 16 * r + 16)
                    act.wait_ge(m.h2, made(k - 2))
                    act.activation(act1[:, q % 2], yin[:, q], ACT.Relu, bias=w.bn[:, 1:2], scale=w.bn[:, 0:1]).then_inc(m.bn, 1)

                def make_rows(k, q, r):
                    act.wait_ge(m.turned, made(k))
                    act.wait_ge(rows_stored[q // 2], 16 * r + 16)
                    act.wait_ge(rows_stored2[q // 2], 16 * r + 16)
                    act.copy(flat(rows, q), psR[q % 2][0:TILE]).then_inc(m.rows, 1)

                def make_sig(k, q, r):
                    act.wait_ge(m.xz, made(k))
                    act.wait_ge(m.y, made(k - 2))
                    act.activation(sig[:, q % 2], psZ[q % 2][:, 0:CH], ACT.Sigmoid, bias=w.gate_b[:, 1:2]).then_inc(m.sig, 1)

                pipeline(act, NCHUNK, U, [(3, make_sig), (0, bn), (3, make_rows)])

            @block.gpsimd
            def _(pool):
                def look_up(k, q, r):
                    pool.wait_ge(m.si, made(k))
                    pool.wait_ge(m.row, made(k - U))
                    pool.sem_inc(ph.seen, 1)
                    pool.indirect_dma_start(entry[:, q], None, scratch.node_map, bass.IndirectOffsetOnAxis(si[:, q], 0),
                                            bounds_check=NODES - 1, oob_is_err=False).then_inc(looked_up[q], 16)

                pipeline(pool, NCHUNK, U, [(0, look_up)])

            @block.vector
            def _(dve):
                def take_index(k, q, r):
                    dve.wait_ge(m.row, made(k - U))
                    dve.tensor_copy(si[:, q], src[:, bass.ds(k, 1)]).then_inc(m.si, 1)

                def take_row(k, q, r):
                    dve.wait_ge(looked_up[q], 16 * r + 16)
                    dve.tensor_copy(src_row[:, bass.ds(k, 1)], entry[:, q, 0:1]).then_inc(m.row, 1)

                def make_h2(k, q, r):
                    dve.wait_ge(m.bn, made(k))
                    dve.wait_ge(h_loaded[q // 2], 16 * r + 16)
                    dve.wait_ge(m.xz, made(k - U))
                    dve.tensor_tensor(h2[:, q], act1[:, q % 2], hin[:, q], ALU.add).then_inc(m.h2, 1)

                def make_y(k, q, r):
                    dve.wait_ge(m.sig, made(k))
                    dve.wait_ge(m.ystats, made(k - U))
                    dve.wait_ge(y_stored[q // 2], 16 * r + 16)
                    dve.scalar_tensor_tensor(out=y[:, q], in0=psX[q % 2][:, 0:CH], scalar=w.bskip[:, 1:2],
                                             in1=sig[:, q % 2], op0=ALU.add, op1=ALU.mult).then_inc(m.y, 1)

                def ystats(k, q, r):
                    dve.wait_ge(m.y, made(k))
                    dve.bn_stats(w.ystats[:, bass.ds(k * 6, 6)], y[:, q]).then_inc(m.ystats, 1)

                dve.wait_ge(src_loaded, 16)
                pipeline(dve, NCHUNK, U, [(0, take_index), (3, take_row), (1, make_h2), (4, make_y), (5, ystats)])

            @block.tensor
            def _(pe):
                def turn(k, q, r):
                    pe.wait_ge(m.rows, made(k - 2))
                    to_rows(pe, psR[q % 2], h2[:, q], w.ident, False, m.turned)

                def skip(k, q, r):
                    pe.wait_ge(m.h2, made(k))
                    pe.wait_ge(m.y, made(k - 2))
                    pe.matmul(psZ[q % 2][:, 0:CH], w.gate_h[:, 1], h2[:, q], start=True, stop=True)
                    pe.matmul(psX[q % 2][:, 0:CH], w.Wskip[:, 1], h2[:, q], start=True, stop=True).then_inc(m.xz, 1)

                pipeline(pe, NCHUNK, U, [(2, skip), (2, turn)])


def dense_last(nc, a, w, scratch, out):
    U = 8
    with phase(nc, "last") as ph:
        yin = ph.sb("yin", [128, U, CH])
        hin, xin = (ph.sb(n, [TILE, U, TILES, D]) for n in ("hin", "xin"))
        xh = ph.sb("xh", [TILE, 4, TILES, D])
        act1 = ph.sb("act1", [128, 2, CH])
        x1 = ph.sb("x1", [TILE, U, TILES, D])
        x1b = ph.sb("x1b", [TILE, U, TILES, D])
        xn = ph.sb("xn", [TILE, 2, TILES, D])
        st = ph.sb("st", [TILE, 4, TILES, 6])
        mv = ph.sb("mv", [TILE, 4, TILES, 2])
        ve = ph.sb("ve", [TILE, 4, TILES])
        rstd = ph.sb("rstd", [TILE, 4, TILES])
        nb = ph.sb("nb", [TILE, 4, TILES])
        g = ph.sb("g", [128, 2, CH])
        hid = ph.sb("hid", [128, 4, 2, CH])
        o = ph.sb("o", [TILE, U, TILES, D])
        psR = [ph.ps(f"psR{s}") for s in range(2)]
        psT, psE = ph.ps("psT"), ph.ps("psE")
        psH = [ph.ps(f"psH{h}") for h in range(2)]
        psO = [ph.ps(f"psO{s}") for s in range(2)]
        y_loaded, x_loaded = ph.loaded("y_loaded", 4), ph.loaded("x_loaded", 4)
        x1_stored, x1_stored2 = ph.stored("x1_stored", 4), ph.stored("x1_stored2", 4)
        o_stored, o_stored2 = ph.stored("o_stored", 4), ph.stored("o_stored2", 4)
        names = "bn xh turned x1 x1b stats seen aggr eps rstd nb xn xT g hidden hid0 hid1 o_ps o"
        m = Group(**{n: ph.stage(n + "_made") for n in names.split()})
        eyn, ehd, econt, eyb, eact, eh3 = (ph.sb(n, [128, 2, CH]) for n in ("eyn", "ehd", "econt", "eyb", "eact", "eh3"))
        ewin = ph.sb("ewin", [128, 2, CH + 2], I32)
        exd, erows = ph.sb("exd", [TILE, 2, TILES, D]), ph.sb("erows", [TILE, 2, TILES, D])
        e_loaded, e_stored = ph.loaded("e_loaded", 2), ph.stored("e_stored", 2)
        e = Group(**{n: ph.stage(f"edge_{n}_made") for n in "cont yb bn h3 turned rows init".split()})
        e_col = lambda c: (ECHUNK - 1) * CH - c * CH

        def edges(stage, unit=4):
            def step(k, q, r):
                if q % unit == 0:
                    stage(2 * r + q // unit, q // unit, r)
            return step

        with nc.Block() as block:
            @block.sync
            def _(sp):
                ph.start(sp)

                def load(t, q, r):
                    hold(sp, ph.seen, m.bn, made(2 * t + 1 - U))
                    sp.dma_start(pair_cols(yin, q), cols_of(scratch.yT, t * 2 * CH, 2 * CH)).then_inc(y_loaded[q], 16)
                    hold(sp, ph.seen, m.xh, made(2 * t + 1 - U))
                    move_rows(sp, pair(hin, q), pair_rows(scratch.h2, t * 2 * CH), x_loaded[q])
                    move_rows(sp, pair(xin, q), pair_rows(a["x"], t * 2 * CH), x_loaded[q])

                def store_x1(t, q, r):
                    hold(sp, ph.seen, m.x1, made(2 * t + 1))
                    dst = pair_rows(scratch.x1, t * 2 * CH)
                    sp.dma_start(dst[0:SPLIT], pair(x1, q)[0:SPLIT]).then_inc(x1_stored[q], 16)
                    sp.dma_start(dst[SPLIT:TILE], pair(x1, q)[SPLIT:TILE]).then_inc(x1_stored2[q], 16)

                def store_o(t, q, r):
                    hold(sp, ph.seen, m.o, made(2 * t + 1))
                    dst = pair_rows(out, t * 2 * CH)
                    sp.dma_start(dst[0:SPLIT], pair(o, q)[0:SPLIT]).then_inc(o_stored[q], 16)
                    sp.dma_start(dst[SPLIT:TILE], pair(o, q)[SPLIT:TILE]).then_inc(o_stored2[q], 16)

                def load_edges(c, s, r):
                    hold(sp, ph.seen, e.rows, made(c - 2))
                    sp.dma_start(eyn[:, s], cols_of(scratch.ydT, e_col(c))).then_inc(e_loaded[s], 16)
                    sp.dma_start(ehd[:, s], cols_of(scratch.hdT, e_col(c))).then_inc(e_loaded[s], 16)
                    sp.dma_start(ewin[:, s], edge_window(scratch, e_col(c))).then_inc(e_loaded[s], 16)
                    sp.dma_start(flat(exd, s), rows_of(scratch.xd, e_col(c))).then_inc(e_loaded[s], 16)

                def store_edges(c, s, r):
                    hold(sp, ph.seen, e.rows, made(c))
                    move_rows(sp, rows_of(scratch.x1, NODES + (ECHUNK - 1) * CH - c * CH), flat(erows, s), e_stored[s])

                pipeline(sp, NCHUNK // 2, U // 2, [(0, load), (2, edges(load_edges, 2)), (4, store_x1), (6, edges(store_edges, 2)), (9, store_o)])
                for s in range(2):
                    sp.wait_ge(e_stored[s], 16 + 32 * len(range(s, ECHUNK, 2)))
                for q in range(U // 2):
                    for sems in (x1_stored, x1_stored2, o_stored, o_stored2):
                        sp.wait_ge(sems[q], 16 + 16 * len(range(q, NCHUNK // 2, U // 2)))

            @block.scalar
            def _(act):
                def bn(k, q, r):
                    act.wait_ge(y_loaded[q // 2], 16 * r + 16)
                    act.wait_ge(m.turned, made(k - 2))
                    act.activation(act1[:, q % 2], yin[:, q], ACT.Relu, bias=w.bn[:, 1:2], scale=w.bn[:, 0:1]).then_inc(m.bn, 1)

                def make_xn(k, q, r):
                    act.wait_ge(m.nb, made(k))
                    act.wait_ge(m.xT, made(k - 2))
                    norm_relu(act, xn[:, q % 2], x1[:, q], rstd[:, q % 4], nb[:, q % 4], m.xn)

                def make_g(k, q, r):
                    act.wait_ge(m.xT, made(k))
                    act.wait_ge(m.hidden, made(k - 2))
                    act.activation(g[:, q % 2], psT[:, 0:CH], ACT.Identity).then_inc(m.g, 1)

                def make_hid0(k, q, r):
                    act.wait_ge(m.hidden, made(k))
                    act.wait_ge(m.o_ps, made(k - 4))
                    act.activation(hid[:, q % 4, 0], psH[0][:, 0:CH], ACT.Relu, bias=w.b2u[:, 0:1]).then_inc(m.hid0, 1)

                def edges_bn(c, s, r):
                    act.wait_ge(e.yb, made(c))
                    act.wait_ge(e.h3, made(c - 2))
                    act.activation(eact[:, s], eyb[:, s], ACT.Relu, bias=w.bn[:, 1:2], scale=w.bn[:, 0:1]).then_inc(e.bn, 1)

                pipeline(act, NCHUNK, U, [(9, make_hid0), (7, make_g), (5, make_xn), (0, bn), (3, edges(edges_bn))])

            @block.gpsimd
            def _(pool):
                def add_h2(k, q, r):
                    pool.wait_ge(x_loaded[q // 2], 64 * r + 64)
                    pool.wait_ge(m.x1, made(k - 4))
                    pool.tensor_tensor(xh[:, q % 4], xin[:, q], hin[:, q], ALU.add).then_inc(m.xh, 1)

                def make_rstd(k, q, r):
                    pool.wait_ge(m.aggr, made(k))
                    pool.wait_ge(m.xn, made(k - 4))
                    pool.tensor_tensor(ve[:, q % 4], mv[:, q % 4, :, 1], w.eps[0:TILE, 0:TILES], ALU.add).then_inc(m.eps, 1)
                    pool.wait_ge(m.eps, made(k))
                    pool.tensor_tensor(rstd[:, q % 4], ve[:, q % 4], w.power[0:TILE, 0:TILES], ALU.pow).then_inc(m.rstd, 1)

                def add_bias(k, q, r):
                    pool.wait_ge(m.x1, made(k))
                    pool.wait_ge(m.o, made(k - 8))
                    pool.tensor_tensor(x1b[:, q], x1[:, q], w.b2b[:].rearrange("p (o f) -> p o f", o=1).to_broadcast([TILE, TILES, D]), ALU.add).then_inc(m.x1b, 1)

                pipeline(pool, NCHUNK, U, [(0, add_h2), (3, make_rstd), (5, add_bias)])

            @block.vector
            def _(dve):
                def make_x1(k, q, r):
                    dve.wait_ge(m.turned, made(k))
                    dve.wait_ge(m.xh, made(k))
                    dve.wait_ge(x1_stored[q // 2], 16 * r + 16)
                    dve.wait_ge(x1_stored2[q // 2], 16 * r + 16)
                    dve.wait_ge(m.x1b, made(k - 8))
                    dve.tensor_tensor(flat(x1, q), psR[q % 2][0:TILE], flat(xh, q % 4), ALU.add).then_inc(m.x1, 1)

                def stats(k, q, r):
                    dve.wait_ge(m.x1, made(k))
                    dve.wait_ge(m.aggr, made(k - 4))
                    norm_stats(dve, x1[:, q], st[:, q % 4], m.stats)

                def aggr(k, q, r):
                    dve.wait_ge(m.stats, made(k))
                    dve.wait_ge(m.xn, made(k - 4))
                    norm_aggr(dve, st[:, q % 4], mv[:, q % 4], m.seen, m.aggr)

                def bias(k, q, r):
                    dve.wait_ge(m.rstd, made(k))
                    dve.wait_ge(m.xn, made(k - 4))
                    norm_bias(dve, nb[:, q % 4], mv[:, q % 4], rstd[:, q % 4], m.nb)

                def make_hid1(k, q, r):
                    dve.wait_ge(m.hidden, made(k))
                    dve.wait_ge(m.o_ps, made(k - 4))
                    dve.tensor_scalar(hid[:, q % 4, 1], psH[1][:, 0:CH], w.b2u[:, 1:2], 0.0, ALU.add, ALU.max).then_inc(m.hid1, 1)

                def make_o(k, q, r):
                    dve.wait_ge(m.o_ps, made(k))
                    dve.wait_ge(m.x1b, made(k))
                    dve.wait_ge(o_stored[q // 2], 16 * r + 16)
                    dve.wait_ge(o_stored2[q // 2], 16 * r + 16)
                    dve.tensor_tensor(flat(o, q), psO[q % 2][0:TILE], flat(x1b, q), ALU.add).then_inc(m.o, 1)

                def spread(c, s, r):
                    dve.wait_ge(e_loaded[s], 64 * r + 64)
                    dve.tensor_tensor(econt[:, s], ewin[:, s, 2:CH + 2], ewin[:, s, 1:CH + 1], ALU.is_equal).then_inc(e.cont, 1)
                    dve.wait_ge(e.cont, made(c))
                    dve.wait_ge(e.yb, made(c - 1))
                    dve.wait_ge(e.bn, made(c - 2))
                    dve.tensor_tensor_scan(eyb[:, s, ::-1], econt[:, s, ::-1], eyn[:, s, ::-1], eyb[:, 1 - s, 0:1],
                                           ALU.mult, ALU.subtract).then_inc(e.yb, 1)

                def edges_h3(c, s, r):
                    dve.wait_ge(e.bn, made(c))
                    dve.wait_ge(e.turned, made(c - 2))
                    dve.tensor_tensor(eh3[:, s], eact[:, s], ehd[:, s], ALU.add).then_inc(e.h3, 1)

                def edges_rows(c, s, r):
                    dve.wait_ge(e.turned, made(c))
                    dve.wait_ge(e_stored[s], 32 * r + 16)
                    dve.tensor_tensor(flat(erows, s), psE[0:TILE], flat(exd, s), ALU.add).then_inc(e.rows, 1)

                dve.memset(eyb[:, 1, 0:1], 0.0).then_inc(e.init, 1)
                dve.wait_ge(e.init, made(0))
                pipeline(dve, NCHUNK, U, [(2, edges(spread)), (4, edges(edges_h3)), (6, edges(edges_rows)), (9, make_hid1), (4, bias), (2, make_x1), (11, make_o), (2, stats), (2, aggr)])

            @block.tensor
            def _(pe):
                def turn(k, q, r):
                    pe.wait_ge(m.bn, made(k))
                    pe.wait_ge(m.x1, made(k - 2))
                    to_rows(pe, psR[q % 2], act1[:, q % 2], w.ident, False, m.turned)

                def turn_back(k, q, r):
                    pe.wait_ge(m.xn, made(k))
                    pe.wait_ge(m.g, made(k - 1))
                    to_T(pe, psT, xn[:, q % 2], w.ident, m.xT)

                def hidden(k, q, r):
                    pe.wait_ge(m.g, made(k))
                    pe.wait_ge(m.hid0, made(k - 1))
                    pe.wait_ge(m.hid1, made(k - 1))
                    for h in range(2):
                        last = pe.matmul(psH[h][:, 0:CH], w.W2a[:, 0, h * 128:(h + 1) * 128], g[:, q % 2], start=True, stop=True)
                    last.then_inc(m.hidden, 1)

                def output(k, q, r):
                    pe.wait_ge(m.hid0, made(k))
                    pe.wait_ge(m.hid1, made(k))
                    pe.wait_ge(m.o, made(k - 2))
                    for j in range(TILES):
                        for h in range(2):
                            last = pe.matmul(psO[q % 2][0:TILE, j * D:(j + 1) * D], tile_cols(hid[:, q % 4, h], j, False), w.W2b[:, h],
                                             start=(h == 0), stop=(h == 1))
                    last.then_inc(m.o_ps, 1)

                def turn_edges(c, s, r):
                    pe.wait_ge(e.h3, made(c))
                    pe.wait_ge(e.rows, made(c - 1))
                    to_rows(pe, psE, eh3[:, s], w.ident, True, e.turned)

                pipeline(pe, NCHUNK, U, [(5, edges(turn_edges)), (1, turn), (8, hidden), (6, turn_back), (10, output)])

def by_edge(t):
    return t.rearrange("f (p j) -> f j p", j=TILES)


def edge_window(scratch, col0):
    return scratch.dst_pad[0:1, bass.ds(col0, CH + 2)].to_broadcast([128, CH + 2])


def index_slot(table, e0):
    return table[bass.ds(e0, CH)].rearrange("(p j) -> p j", j=TILES)


def gather(pool, seen, rows, table, index, sem):
    pool.sem_inc(seen, 1)
    for j in range(TILES):
        pool.indirect_dma_start(rows[:, j], None, table, bass.IndirectOffsetOnAxis(index[:, j:j + 1], 0),
                                bounds_check=table.shape[0] - 1, oob_is_err=False).then_inc(sem, 16)


def scatter_ends(pool, seen, table, rows, index, sem):
    pool.sem_inc(seen, 1)
    for j in range(TILES):
        pool.indirect_dma_start(table, bass.IndirectOffsetOnAxis(index[:, j:j + 1], 0), rows[:, j], None,
                                bounds_check=table.shape[0] - 1, oob_is_err=False).then_inc(sem, 16)


def attention(nc, a, w, scratch, l):
    U = 6
    D0 = 2 * l
    with phase(nc, f"att{l}") as ph:
        hd, hs = ph.sb("hd", [128, U, CH]), ph.sb("hs", [128, U, CH])
        ew = ph.sb("ew", [1, U, CH])
        win = ph.sb("win", [128, U, CH + 2], I32)
        qs, prod = ph.sb("qs", [128, 2, CH]), ph.sb("prod", [128, 2, CH])
        cont, apart = ph.sb("cont", [128, U, CH + 1]), ph.sb("apart", [128, 2, CH])
        mx = ph.sb("mx", [128, 2, CH + 1])
        ex, ee = ph.sb("ex", [128, 2, 2, CH]), ph.sb("ee", [128, 2, 2, CH])
        keep, pv = ph.sb("keep", [128, 2, CH]), ph.sb("pv", [128, 2, CH])
        den, num, lden, rden, dr, left, o0 = (ph.sb(n, [128, 2, CH]) for n in ("den", "num", "lden", "rden", "dr", "left", "o0"))
        o, th, dx, gx, y = (ph.sb(n, [128, 2, CH]) for n in ("o", "th", "dx", "gx", "y"))
        yn = ph.sb("yn", [128, U, CH])
        psQ, psK, psA, psX, psZ = (ph.ps(n) for n in ("psQ", "psK", "psA", "psX", "psZ"))
        psV = [ph.ps(f"psV{s}") for s in range(2)]
        in_loaded = ph.loaded("in_loaded", U)
        idx = ph.sb("idx", [TILE, U, TILES], I32)
        idx_loaded, moved = ph.loaded("idx_loaded", U), ph.loaded("moved", U)
        if l == 0:
            er = ph.sb("er", [TILE, U, TILES, MAPW], I32)
        else:
            rows = ph.sb("rows", [TILE, U, TILES, D])
            psT = ph.ps("psT")
        yn_stored = ph.stored("yn_stored", U)
        names = "scattered xT hs qk v qs prod score cont apart mx0 mx ex ee keep pv den num lden seed dr left o0 o xz gated th dx gx y yn ystats init"
        m = Group(**{n: ph.stage(n + "_made") for n in names.split()})
        loads = 64 if l == 0 else 48
        with nc.Block() as block:
            @block.sync
            def _(sp):
                ph.start(sp)

                def load_index(k, q, r):
                    hold(sp, ph.seen, m.xT if l else m.scattered, made(k - U))
                    sp.dma_start(idx[:, q], index_slot(scratch.src_row if l else scratch.end_index, k * CH)).then_inc(idx_loaded[q], 16)
                    if l == 0:
                        sp.dma_start(er[:, q].rearrange("p j w -> p (j w)"), scratch.edge_row[bass.ds(k * CH, CH), :].rearrange(
                            "(p j) w -> p (j w)", j=TILES)).then_inc(idx_loaded[q], 16)

                def load(k, q, r):
                    hold(sp, ph.seen, m.gated, made(k - U))
                    sp.dma_start(hd[:, q], cols_of(scratch.hdT, k * CH)).then_inc(in_loaded[q], 16)
                    if l == 0:
                        sp.dma_start(hs[:, q], cols_of(scratch.hsT, k * CH)).then_inc(in_loaded[q], 16)
                    sp.dma_start(ew[:, q], a["edge_weight1"][bass.ds(k * CH, CH), :].rearrange("e o -> o e")).then_inc(in_loaded[q], 16)
                    hold(sp, ph.seen, m.cont, made(k - U))
                    sp.dma_start(win[:, q], edge_window(scratch, k * CH)).then_inc(in_loaded[q], 16)

                def store(k, q, r):
                    hold(sp, ph.seen, m.yn, made(k))
                    sp.dma_start(cols_of(scratch.ydT, k * CH), yn[:, q]).then_inc(yn_stored[q], 16)

                pipeline(sp, ECHUNK, U, [(0, load_index), (D0, load), (D0 + 7, store)])
                for q in range(U):
                    sp.wait_ge(yn_stored[q], 16 + 16 * len(range(q, ECHUNK, U)))
                    sp.wait_ge(moved[q], 16 * TILES * len(range(q, ECHUNK, U)))

            @block.tensor
            def _(pe):
                def turn(k, q, r):
                    pe.wait_ge(moved[q], 16 * TILES * (r + 1))
                    pe.wait_ge(m.hs, made(k - 1))
                    to_T(pe, psT, rows[:, q], w.ident, m.xT)

                def query_key(k, q, r):
                    pe.wait_ge(in_loaded[q], loads * r + loads)
                    if l == 1:
                        pe.wait_ge(m.hs, made(k))
                    pe.wait_ge(m.qs, made(k - 1))
                    pe.wait_ge(m.prod, made(k - 1))
                    pe.matmul(psQ[:, 0:CH], w.Wq[:, l], hd[:, q], start=True, stop=True)
                    pe.matmul(psK[:, 0:CH], w.Wk[:, l], hs[:, q], start=True, stop=False)
                    pe.matmul(psK[:, 0:CH], w.We[:, l], ew[:, q], start=False, stop=True).then_inc(m.qk, 1)

                def value(k, q, r):
                    pe.wait_ge(m.pv, made(k - 2))
                    pe.matmul(psV[q % 2][:, 0:CH], w.Wv[:, l], hs[:, q], start=True, stop=False)
                    pe.matmul(psV[q % 2][:, 0:CH], w.We[:, l], ew[:, q], start=False, stop=True).then_inc(m.v, 1)

                def score(k, q, r):
                    pe.wait_ge(m.prod, made(k))
                    pe.wait_ge(m.ex, made(k - 1))
                    pe.matmul(psA[:, 0:CH], w.heads[:], prod[:, q % 2], start=True, stop=True).then_inc(m.score, 1)

                def skip(k, q, r):
                    pe.wait_ge(m.dx, made(k - 1))
                    pe.wait_ge(m.th, made(k - 1))
                    pe.matmul(psX[:, 0:CH], w.Wskip[:, l], hd[:, q], start=True, stop=True)
                    pe.matmul(psZ[:, 0:CH], w.gate_h[:, l], hd[:, q], start=True, stop=False).then_inc(m.xz, 1)

                def gate(k, q, r):
                    pe.wait_ge(m.o, made(k))
                    pe.matmul(psZ[:, 0:CH], w.gate_out[:, l], o[:, q % 2], start=False, stop=True).then_inc(m.gated, 1)

                pipeline(pe, ECHUNK, U, [(1, turn)] * l + [(D0 + 2, score), (D0 + 2, value), (D0, query_key), (D0 + 5, skip), (D0 + 5, gate)])

            @block.gpsimd
            def _(pool):
                def fetch(k, q, r):
                    pool.wait_ge(idx_loaded[q], 16 * r + 16)
                    pool.wait_ge(m.xT, made(k - U))
                    gather(pool, ph.seen, rows[:, q], scratch.h2, idx[:, q], moved[q])

                def scatter(k, q, r):
                    pool.wait_ge(idx_loaded[q], 32 * r + 32)
                    scatter_ends(pool, ph.seen, scratch.node_map, er[:, q], idx[:, q], moved[q])

                def scattered(k, q, r):
                    pool.wait_ge(moved[q], 16 * TILES * (r + 1))
                    pool.sem_inc(m.scattered, 1)

                def overshoot(k, q, r):
                    s = q % 2
                    pool.wait_ge(m.seed, made(k))
                    pool.wait_ge(m.left, made(k - 2))
                    pool.tensor_tensor(dr[:, s], den[:, s], rden[:, s], ALU.mult).then_inc(m.dr, 1)
                    pool.wait_ge(m.gated, made(k - 2))
                    pool.wait_ge(m.y, made(k - 2))
                    pool.wait_ge(m.num, made(k))
                    pool.tensor_tensor(o0[:, s], num[:, s], rden[:, s], ALU.mult).then_inc(m.o0, 1)

                def divide(k, q, r):
                    s = q % 2
                    pool.wait_ge(m.left, made(k))
                    pool.wait_ge(m.o0, made(k))
                    pool.tensor_tensor(o[:, s], o0[:, s], left[:, s], ALU.mult).then_inc(m.o, 1)

                pipeline(pool, ECHUNK, U, ([(0, fetch)] if l else [(0, scatter), (1, scattered)]) + [(D0 + 4, overshoot), (D0 + 4, divide)])

            @block.scalar
            def _(act):
                def source(k, q, r):
                    act.wait_ge(m.xT, made(k))
                    act.wait_ge(m.v, made(k - U))
                    act.activation(by_edge(hs[:, q]), by_tile(psT), ACT.Identity).then_inc(m.hs, 1)

                def query(k, q, r):
                    act.wait_ge(m.qk, made(k))
                    act.wait_ge(m.prod, made(k - 2))
                    act.activation(qs[:, q % 2], psQ[:, 0:CH], ACT.Identity, bias=w.bq[:, l:l + 1]).then_inc(m.qs, 1)

                def exps(k, q, r):
                    act.wait_ge(m.ex, made(k))
                    act.wait_ge(m.num, made(k - 2))
                    act.activation(ee[:, q % 2].rearrange("p a e -> p (a e)"), ex[:, q % 2].rearrange("p a e -> p (a e)"), ACT.Exp).then_inc(m.ee, 1)

                def gate(k, q, r):
                    act.wait_ge(m.gated, made(k))
                    act.wait_ge(m.gx, made(k - 2))
                    act.activation(th[:, q % 2], psZ[:, 0:CH], ACT.Tanh, bias=w.gate_bh[:, l:l + 1], scale=0.5).then_inc(m.th, 1)

                def guess(k, q, r):
                    s = q % 2
                    act.wait_ge(m.den, made(k))
                    act.wait_ge(m.seed, made(k - 2))
                    act.activation(lden[:, s], den[:, s], ACT.Ln).then_inc(m.lden, 1)
                    act.wait_ge(m.lden, made(k))
                    act.wait_ge(m.o0, made(k - 2))
                    act.activation(rden[:, s], lden[:, s], ACT.Exp, scale=-1.0).then_inc(m.seed, 1)

                def correct(k, q, r):
                    act.wait_ge(m.dr, made(k))
                    act.wait_ge(m.o, made(k - 2))
                    act.activation(left[:, q % 2], dr[:, q % 2], ACT.Identity, bias=w.two[:], scale=-1.0).then_inc(m.left, 1)

                pipeline(act, ECHUNK, U, [(1, source)] * l + [(D0 + 6, gate), (D0 + 1, query), (D0 + 3, exps), (D0 + 4, guess), (D0 + 4, correct)])

            @block.vector
            def _(dve):
                dve.memset(mx[:, 1, CH:CH + 1], 0.0)
                dve.memset(den[:, 1, CH - 1:CH], 0.0)
                dve.memset(num[:, 1, CH - 1:CH], 0.0).then_inc(m.init, 1)
                dve.wait_ge(m.init, made(0))

                def product(k, q, r):
                    s = q % 2
                    dve.wait_ge(in_loaded[q], loads * r + loads)
                    dve.tensor_tensor(cont[:, q], win[:, q, 1:CH + 2], win[:, q, 0:CH + 1], ALU.is_equal).then_inc(m.cont, 1)
                    dve.wait_ge(m.cont, made(k))
                    dve.tensor_scalar(apart[:, s], cont[:, q, 0:CH], -1.0, BIG, ALU.add, ALU.mult).then_inc(m.apart, 1)
                    dve.wait_ge(m.qs, made(k))
                    dve.wait_ge(m.score, made(k - 2))
                    dve.scalar_tensor_tensor(out=prod[:, s], in0=psK[:, 0:CH], scalar=w.bk[:, l:l + 1], in1=qs[:, s],
                                             op0=ALU.add, op1=ALU.mult).then_inc(m.prod, 1)

                def maximum(k, q, r):
                    s, p = q % 2, 1 - q % 2
                    dve.wait_ge(m.mx, made(k - 1))
                    dve.tensor_copy(mx[:, s, 0:1], mx[:, p, CH:CH + 1]).then_inc(m.mx0, 1)
                    dve.wait_ge(m.score, made(k))
                    dve.wait_ge(m.apart, made(k))
                    dve.wait_ge(m.mx0, made(k))
                    dve.tensor_tensor_scan(mx[:, s, 1:CH + 1], apart[:, s], psA[:, 0:CH], mx[:, s, 0:1], ALU.add, ALU.max).then_inc(m.mx, 1)
                    dve.wait_ge(m.mx, made(k))
                    dve.wait_ge(m.ee, made(k - 2))
                    dve.tensor_tensor(ex[:, s, 1], psA[:, 0:CH], mx[:, s, 1:CH + 1], ALU.subtract)
                    dve.tensor_tensor(ex[:, s, 0], mx[:, s, 0:CH], mx[:, s, 1:CH + 1], ALU.subtract).then_inc(m.ex, 1)

                def sums(k, q, r):
                    s, p = q % 2, 1 - q % 2
                    dve.wait_ge(m.ee, made(k))
                    dve.wait_ge(m.v, made(k))
                    dve.scalar_tensor_tensor(out=keep[:, s], in0=ee[:, s, 0], scalar=1.0, in1=cont[:, q, 0:CH],
                                             op0=ALU.min, op1=ALU.mult).then_inc(m.keep, 1)
                    dve.scalar_tensor_tensor(out=pv[:, s], in0=psV[s][:, 0:CH], scalar=w.bv[:, l:l + 1], in1=ee[:, s, 1],
                                             op0=ALU.add, op1=ALU.mult).then_inc(m.pv, 1)
                    dve.wait_ge(m.keep, made(k))
                    dve.wait_ge(m.den, made(k - 1))
                    dve.wait_ge(m.dr, made(k - 2))
                    dve.tensor_tensor_scan(den[:, s], keep[:, s], ee[:, s, 1], den[:, p, CH - 1:CH], ALU.mult, ALU.add).then_inc(m.den, 1)
                    dve.wait_ge(m.pv, made(k))
                    dve.wait_ge(m.num, made(k - 1))
                    dve.wait_ge(m.o0, made(k - 2))
                    dve.tensor_tensor_scan(num[:, s], keep[:, s], pv[:, s], num[:, p, CH - 1:CH], ALU.mult, ALU.add).then_inc(m.num, 1)

                def combine(k, q, r):
                    s = q % 2
                    dve.wait_ge(m.xz, made(k))
                    dve.wait_ge(m.o, made(k))
                    dve.scalar_tensor_tensor(out=dx[:, s], in0=psX[:, 0:CH], scalar=w.bskip[:, l:l + 1], in1=o[:, s],
                                             op0=ALU.add, op1=ALU.subtract).then_inc(m.dx, 1)
                    dve.wait_ge(m.th, made(k))
                    dve.wait_ge(m.dx, made(k))
                    dve.scalar_tensor_tensor(out=gx[:, s], in0=th[:, s], scalar=1.0, in1=dx[:, s], op0=ALU.add, op1=ALU.mult).then_inc(m.gx, 1)
                    dve.wait_ge(m.gx, made(k))
                    dve.scalar_tensor_tensor(out=y[:, s], in0=gx[:, s], scalar=0.5, in1=o[:, s], op0=ALU.mult, op1=ALU.add).then_inc(m.y, 1)
                    dve.wait_ge(m.y, made(k))
                    dve.wait_ge(yn_stored[q], 16 * r + 16)
                    dve.wait_ge(m.ystats, made(k - U))
                    dve.scalar_tensor_tensor(out=yn[:, q], in0=cont[:, q, 1:CH + 1], scalar=-1.0, in1=y[:, s], op0=ALU.add, op1=ALU.mult).then_inc(m.yn, 1)
                    dve.wait_ge(m.yn, made(k))
                    dve.bn_stats(w.ends[:, bass.ds(k * 6, 6)], yn[:, q]).then_inc(m.ystats, 1)

                pipeline(dve, ECHUNK, U, [(D0 + 1, product), (D0 + 6, combine), (D0 + 2, maximum), (D0 + 3, sums)])


def edge_update(nc, a, w, scratch, l):
    U = 6
    with phase(nc, f"upd{l}") as ph:
        yn, hd, yw = (ph.sb(n, [128, U, CH]) for n in ("yn", "hd", "yw"))
        xd = ph.sb("xd", [TILE, U, TILES, D])
        win = ph.sb("win", [128, U, CH + 2], I32)
        cont = ph.sb("cont", [128, U, CH])
        yb, act1, actw, sig, yw2, ywn = (ph.sb(n, [128, 2, CH]) for n in ("yb", "act1", "actw", "sig", "yw2", "ywn"))
        hn, hw = ph.sb("hn", [128, U, CH]), ph.sb("hw", [128, U, CH])
        rows = ph.sb("rows", [TILE, U, TILES, D])
        psR = [ph.ps(f"psR{s}") for s in range(2)]
        psX = [ph.ps(f"psX{s}") for s in range(2)]
        psZ = [ph.ps(f"psZ{s}") for s in range(2)]
        in_loaded = ph.loaded("in_loaded", U)
        hn_stored, rows_stored = ph.stored("hn_stored", U), ph.stored("rows_stored", U)
        names = "cont yb bn hn turned rows bnw hw xz sig yw2 ywn ywstats init"
        m = Group(**{n: ph.stage(n + "_made") for n in names.split()})
        table = scratch.h2 if l == 0 else scratch.x1
        last_of_slot = m.hw if l == 0 else m.rows
        col = lambda k: (ECHUNK - 1) * CH - k * CH
        with nc.Block() as block:
            @block.sync
            def _(sp):
                ph.start(sp)

                def load(k, q, r):
                    hold(sp, ph.seen, last_of_slot, made(k - U))
                    hold(sp, ph.seen, m.hn, made(k - U))
                    sp.dma_start(yn[:, q], cols_of(scratch.ydT, col(k))).then_inc(in_loaded[q], 16)
                    sp.dma_start(hd[:, q], cols_of(scratch.hdT, col(k))).then_inc(in_loaded[q], 16)
                    sp.dma_start(win[:, q], edge_window(scratch, col(k))).then_inc(in_loaded[q], 16)
                    if l == 0:
                        sp.dma_start(yw[:, q], cols_of(scratch.ywT, col(k))).then_inc(in_loaded[q], 16)
                    else:
                        sp.dma_start(flat(xd, q), rows_of(scratch.xd, col(k))).then_inc(in_loaded[q], 16)

                def store(k, q, r):
                    hold(sp, ph.seen, m.hn, made(k))
                    sp.dma_start(cols_of(scratch.hdT, col(k)), hn[:, q]).then_inc(hn_stored[q], 16)
                    hold(sp, ph.seen, m.rows, made(k))
                    move_rows(sp, rows_of(table, NODES + (ECHUNK - 1) * CH - k * CH), flat(rows, q), rows_stored[q])

                pipeline(sp, ECHUNK, U, [(0, load), (5, store)])
                for q in range(U):
                    sp.wait_ge(hn_stored[q], 16 + 16 * len(range(q, ECHUNK, U)))
                    sp.wait_ge(rows_stored[q], 16 + 32 * len(range(q, ECHUNK, U)))

            @block.vector
            def _(dve):
                dve.memset(yb[:, 1, 0:1], 0.0).then_inc(m.init, 1)
                dve.wait_ge(m.init, made(0))

                def spread(k, q, r):
                    dve.wait_ge(in_loaded[q], 64 * r + 64)
                    dve.tensor_tensor(cont[:, q], win[:, q, 2:CH + 2], win[:, q, 1:CH + 1], ALU.is_equal).then_inc(m.cont, 1)
                    dve.wait_ge(m.cont, made(k))
                    dve.wait_ge(m.yb, made(k - 1))
                    dve.wait_ge(m.bn, made(k - 2))
                    dve.tensor_tensor_scan(yb[:, q % 2, ::-1], cont[:, q, ::-1], yn[:, q, ::-1], yb[:, 1 - q % 2, 0:1],
                                           ALU.mult, ALU.subtract).then_inc(m.yb, 1)

                def make_h(k, q, r):
                    dve.wait_ge(m.bn, made(k))
                    dve.wait_ge(hn_stored[q], 16 * r + 16)
                    dve.wait_ge(m.turned, made(k - U))
                    dve.tensor_tensor(hn[:, q], act1[:, q % 2], hd[:, q], ALU.add).then_inc(m.hn, 1)
                    if l == 0:
                        dve.wait_ge(m.bnw, made(k))
                        dve.wait_ge(m.xz, made(k - U))
                        dve.tensor_tensor(hw[:, q], actw[:, q % 2], hd[:, q], ALU.add).then_inc(m.hw, 1)

                def make_rows(k, q, r):
                    dve.wait_ge(m.turned, made(k))
                    dve.wait_ge(rows_stored[q], 32 * r + 16)
                    dve.tensor_tensor(flat(rows, q), psR[q % 2][0:TILE], flat(xd, q), ALU.add).then_inc(m.rows, 1)

                def make_y(k, q, r):
                    dve.wait_ge(m.sig, made(k))
                    dve.scalar_tensor_tensor(out=yw2[:, q % 2], in0=psX[q % 2][:, 0:CH], scalar=w.bskip[:, 1:2],
                                             in1=sig[:, q % 2], op0=ALU.add, op1=ALU.mult).then_inc(m.yw2, 1)
                    dve.wait_ge(m.yw2, made(k))
                    dve.scalar_tensor_tensor(out=ywn[:, q % 2], in0=cont[:, q], scalar=-1.0, in1=yw2[:, q % 2], op0=ALU.add, op1=ALU.mult).then_inc(m.ywn, 1)
                    dve.wait_ge(m.ywn, made(k))
                    dve.bn_stats(w.wends[:, bass.ds(k * 6, 6)], ywn[:, q % 2]).then_inc(m.ywstats, 1)

                pipeline(dve, ECHUNK, U, [(0, spread), (2, make_h), (5, make_y) if l == 0 else (4, make_rows)])

            @block.scalar
            def _(act):
                def bn(k, q, r):
                    act.wait_ge(m.yb, made(k))
                    act.wait_ge(m.hn, made(k - 2))
                    act.activation(act1[:, q % 2], yb[:, q % 2], ACT.Relu, bias=w.bn[:, 1:2], scale=w.bn[:, 0:1]).then_inc(m.bn, 1)
                    if l == 0:
                        act.wait_ge(m.hw, made(k - 2))
                        act.activation(actw[:, q % 2], yw[:, q], ACT.Relu, bias=w.bn[:, 1:2], scale=w.bn[:, 0:1]).then_inc(m.bnw, 1)

                def make_sig(k, q, r):
                    act.wait_ge(m.xz, made(k))
                    act.wait_ge(m.yw2, made(k - 2))
                    act.activation(sig[:, q % 2], psZ[q % 2][:, 0:CH], ACT.Sigmoid, bias=w.gate_b[:, 1:2]).then_inc(m.sig, 1)
                    act.wait_ge(m.turned, made(k))
                    act.wait_ge(rows_stored[q], 32 * r + 16)
                    act.copy(flat(rows, q), psR[q % 2][0:TILE]).then_inc(m.rows, 1)

                pipeline(act, ECHUNK, U, [(4, make_sig), (1, bn)] if l == 0 else [(1, bn)])

            @block.tensor
            def _(pe):
                def turn(k, q, r):
                    pe.wait_ge(m.hn, made(k))
                    pe.wait_ge(m.rows, made(k - 2))
                    to_rows(pe, psR[q % 2], hn[:, q], w.ident, True, m.turned)
                    if l == 0:
                        pe.wait_ge(m.hw, made(k))
                        pe.wait_ge(m.yw2, made(k - 2))
                        pe.matmul(psZ[q % 2][:, 0:CH], w.gate_h[:, 1], hw[:, q], start=True, stop=True)
                        pe.matmul(psX[q % 2][:, 0:CH], w.Wskip[:, 1], hw[:, q], start=True, stop=True).then_inc(m.xz, 1)
                pipeline(pe, ECHUNK, U, [(3, turn)])


def edge_last(nc, a, w, scratch, out):
    U = 4
    N2 = 2 * TILES
    with phase(nc, "elast") as ph:
        si, ends = (ph.sb(n, [TILE, U, TILES], I32) for n in ("si", "ends"))
        x = ph.sb("x", [TILE, U, N2, D])
        xb = ph.sb("xb", [TILE, U, TILES, D])
        ea = ph.sb("ea", [TILE, U, TILES, D])
        xn = ph.sb("xn", [TILE, 2, N2, D])
        st = ph.sb("st", [TILE, U, N2, 6])
        mv = ph.sb("mv", [TILE, U, N2, 2])
        ve = ph.sb("ve", [TILE, U, N2])
        rstd, nb = ph.sb("rstd", [TILE, U, N2]), ph.sb("nb", [TILE, U, N2])
        g = ph.sb("g", [128, U, 2, CH])
        eT = ph.sb("eT", [128, 2, CH])
        win = ph.sb("win", [128, U, CH + 2], I32)
        cont, cnt = ph.sb("cont", [128, 2, CH]), ph.sb("cnt", [128, 2, CH])
        ones = ph.sb("ones", [128, CH])
        hid, hid2 = ph.sb("hid", [128, 2, 2, CH]), ph.sb("hid2", [128, 2, 2, CH])
        msg, tot = (ph.sb(n, [128, 2, CH]) for n in ("msg", "tot"))
        rcnt = ph.sb("rcnt", [128, 2, CH])
        mean = ph.sb("mean", [128, 2, CH])
        o = ph.sb("o", [TILE, U, TILES, D])
        psT = [ph.ps(f"psT{s}") for s in range(2)]
        psH = [ph.ps(f"psH{s}") for s in range(2)]
        psG = [ph.ps(f"psG{s}") for s in range(2)]
        psM, psO = ph.ps("psM"), ph.ps("psO")
        idx_loaded, ends_loaded, x_loaded, ea_loaded, run_loaded = (
            ph.loaded(n, U) for n in ("idx_loaded", "ends_loaded", "x_loaded", "ea_loaded", "run_loaded"))
        moved, placed = ph.loaded("moved", U), ph.loaded("placed", U)
        names = ("xb stats aggr_seen aggr eps rstd nb xn xT g eaT eT cont cnt rcnt hid0 hid1 hidden psm msg tot mean "
                 "hidden2 hid20 hid21 o_ps o init")
        m = Group(**{n: ph.stage(n + "_made") for n in names.split()})
        per = 16 * TILES
        with nc.Block() as block:
            @block.sync
            def _(sp):
                ph.start(sp)

                def load(k, q, r):
                    hold(sp, ph.seen, m.stats, made(k - U))
                    sp.dma_start(si[:, q], index_slot(scratch.src_row, k * CH)).then_inc(idx_loaded[q], 16)
                    hold(sp, ph.seen, m.xb, made(k - U))
                    hold(sp, ph.seen, m.xn, made(k - U))
                    sp.dma_start(x[:, q, 0:TILES].rearrange("p j f -> p (j f)"), rows_of(scratch.x1, NODES + k * CH)).then_inc(x_loaded[q], 16)

                def load_attr(k, q, r):
                    hold(sp, ph.seen, m.eaT, made(k - U))
                    sp.dma_start(flat(ea, q), rows_of(a["edge_attr_128"], k * CH)).then_inc(ea_loaded[q], 16)

                def load_run(k, q, r):
                    hold(sp, ph.seen, m.cont, made(k - U))
                    sp.dma_start(win[:, q], edge_window(scratch, k * CH)).then_inc(run_loaded[q], 16)

                def load_ends(k, q, r):
                    if not (isinstance(r, int) and r == 0):
                        hold(sp, ph.seen, placed[q], per * r)
                    sp.dma_start(ends[:, q], index_slot(scratch.end_index, k * CH)).then_inc(ends_loaded[q], 16)

                pipeline(sp, ECHUNK, U, [(0, load), (1, load_attr), (2, load_run), (5, load_ends)], peel=U)

            @block.gpsimd
            def _(pool):
                def fetch(k, q, r):
                    pool.wait_ge(idx_loaded[q], 16 * r + 16)
                    pool.wait_ge(m.xn, made(k - U))
                    gather(pool, ph.seen, x[:, q, TILES:N2], scratch.x1, si[:, q], moved[q])

                def make_rstd(k, q, r):
                    s = q
                    pool.wait_ge(m.aggr, made(k))
                    pool.wait_ge(m.xn, made(k - U))
                    pool.tensor_tensor(ve[:, s], mv[:, s, :, 1], w.eps[0:TILE, 0:N2], ALU.add).then_inc(m.eps, 1)
                    pool.wait_ge(m.eps, made(k))
                    pool.tensor_tensor(rstd[:, s], ve[:, s], w.power[0:TILE, 0:N2], ALU.pow).then_inc(m.rstd, 1)

                def add_bias(k, q, r):
                    pool.wait_ge(x_loaded[q], 16 * r + 16)
                    pool.wait_ge(m.o, made(k - U))
                    pool.tensor_tensor(xb[:, q], x[:, q, 0:TILES], w.b2b[:].rearrange("p (o f) -> p o f", o=1).to_broadcast([TILE, TILES, D]), ALU.add).then_inc(m.xb, 1)

                def place(k, q, r):
                    pool.wait_ge(ends_loaded[q], 16 * r + 16)
                    pool.wait_ge(m.o, made(k))
                    scatter_ends(pool, ph.seen, out, o[:, q], ends[:, q], placed[q])

                pipeline(pool, ECHUNK, U, [(2, make_rstd), (0, fetch), (3, add_bias), (7, place)], peel=U)
                for q in range(U):
                    pool.wait_ge(placed[q], per * len(range(q, ECHUNK, U)))

            @block.vector
            def _(dve):
                dve.memset(ones[:], 1.0)
                dve.memset(cnt[:, 1, CH - 1:CH], 0.0)
                dve.memset(tot[:, 1, CH - 1:CH], 0.0).then_inc(m.init, 1)
                dve.wait_ge(m.init, made(0))

                def stats(k, q, r):
                    dve.wait_ge(moved[q], per * r + per)
                    dve.wait_ge(x_loaded[q], 16 * r + 16)
                    dve.wait_ge(m.aggr, made(k - U))
                    norm_stats(dve, x[:, q], st[:, q], m.stats)

                def aggr(k, q, r):
                    dve.wait_ge(m.stats, made(k))
                    dve.wait_ge(m.xn, made(k - U))
                    norm_aggr(dve, st[:, q], mv[:, q], m.aggr_seen, m.aggr)

                def bias(k, q, r):
                    dve.wait_ge(m.rstd, made(k))
                    dve.wait_ge(m.xn, made(k - U))
                    norm_bias(dve, nb[:, q], mv[:, q], rstd[:, q], m.nb)

                def half(k, q, r):
                    dve.wait_ge(m.hidden, made(k))
                    dve.wait_ge(m.psm, made(k - 2))
                    dve.tensor_scalar(hid[:, q % 2, 1], psH[1][:, 0:CH], w.b1a[:, 1:2], 0.0, ALU.add, ALU.max).then_inc(m.hid1, 1)

                def count(k, q, r):
                    s = q % 2
                    dve.wait_ge(run_loaded[q], 16 * r + 16)
                    dve.wait_ge(m.mean, made(k - 2))
                    dve.tensor_tensor(cont[:, s], win[:, q, 1:CH + 1], win[:, q, 0:CH], ALU.is_equal).then_inc(m.cont, 1)
                    dve.wait_ge(m.cont, made(k))
                    dve.wait_ge(m.cnt, made(k - 1))
                    dve.tensor_tensor_scan(cnt[:, s], cont[:, s], ones[:], cnt[:, 1 - s, CH - 1:CH], ALU.mult, ALU.add).then_inc(m.cnt, 1)
                    dve.wait_ge(m.cnt, made(k))
                    dve.reciprocal(rcnt[:, s], cnt[:, s]).then_inc(m.rcnt, 1)

                def total(k, q, r):
                    s = q % 2
                    dve.wait_ge(m.msg, made(k))
                    dve.wait_ge(m.tot, made(k - 1))
                    dve.tensor_tensor_scan(tot[:, s], cont[:, s], msg[:, s], tot[:, 1 - s, CH - 1:CH], ALU.mult, ALU.add).then_inc(m.tot, 1)
                    dve.wait_ge(m.tot, made(k))
                    dve.wait_ge(m.rcnt, made(k))
                    dve.wait_ge(m.hidden2, made(k - 2))
                    dve.tensor_tensor(mean[:, s], tot[:, s], rcnt[:, s], ALU.mult).then_inc(m.mean, 1)

                def half2(k, q, r):
                    dve.wait_ge(m.hidden2, made(k))
                    dve.wait_ge(m.o_ps, made(k - 2))
                    dve.tensor_scalar(hid2[:, q % 2, 1], psG[1][:, 0:CH], w.b2u[:, 1:2], 0.0, ALU.add, ALU.max).then_inc(m.hid21, 1)

                def output(k, q, r):
                    dve.wait_ge(m.o_ps, made(k))
                    dve.wait_ge(m.xb, made(k))
                    if not (isinstance(r, int) and r == 0):
                        dve.wait_ge(placed[q], per * r)
                    dve.tensor_tensor(flat(o, q), psO[0:TILE], flat(xb, q), ALU.add).then_inc(m.o, 1)

                pipeline(dve, ECHUNK, U, [(2, bias), (0, stats), (0, aggr), (6, output), (3, count), (4, total), (5, half2), (3, half)], peel=U)

            @block.tensor
            def _(pe):
                def turn(k, q, r):
                    pe.wait_ge(m.xn, made(k))
                    pe.wait_ge(m.eT, made(k - 1))
                    for j in range(TILES):
                        for s in range(2):
                            last = pe.transpose(psT[s][:, j * TILE:(j + 1) * TILE], xn[:, q % 2, s * TILES + j], w.ident[0:TILE, 0:TILE])
                    last.then_inc(m.xT, 1)

                def message(k, q, r):
                    pe.wait_ge(m.hid0, made(k))
                    pe.wait_ge(m.hid1, made(k))
                    pe.wait_ge(m.msg, made(k - 1))
                    pe.matmul(psM[:, 0:CH], w.W1b[:, 0], hid[:, q % 2, 0], start=True, stop=False)
                    pe.matmul(psM[:, 0:CH], w.W1b[:, 1], hid[:, q % 2, 1], start=False, stop=True).then_inc(m.psm, 1)

                def output(k, q, r):
                    pe.wait_ge(m.hid20, made(k))
                    pe.wait_ge(m.hid21, made(k))
                    pe.wait_ge(m.o, made(k - 1))
                    for j in range(TILES):
                        for h in range(2):
                            last = pe.matmul(psO[0:TILE, j * D:(j + 1) * D], tile_cols(hid2[:, q % 2, h], j, True), w.W2b[:, h],
                                             start=(h == 0), stop=(h == 1))
                    last.then_inc(m.o_ps, 1)

                def turn_attr(k, q, r):
                    pe.wait_ge(ea_loaded[q], 16 * r + 16)
                    pe.wait_ge(m.g, made(k))
                    for j in range(TILES):
                        last = pe.transpose(psT[0][:, j * TILE:(j + 1) * TILE], ea[:, q, j], w.ident[0:TILE, 0:TILE])
                    last.then_inc(m.eaT, 1)

                def hidden(k, q, r):
                    pe.wait_ge(m.eT, made(k))
                    pe.wait_ge(m.hid0, made(k - 1))
                    pe.wait_ge(m.hid1, made(k - 1))
                    for h in range(2):
                        pe.matmul(psH[h][:, 0:CH], w.W1a[:, 0, h * 128:(h + 1) * 128], g[:, q, 1], start=True, stop=False)
                        last = pe.matmul(psH[h][:, 0:CH], w.W1a[:, 1, h * 128:(h + 1) * 128], eT[:, q % 2], start=False, stop=True)
                    last.then_inc(m.hidden, 1)

                def hidden2(k, q, r):
                    pe.wait_ge(m.mean, made(k))
                    pe.wait_ge(m.hid20, made(k - 1))
                    pe.wait_ge(m.hid21, made(k - 1))
                    for h in range(2):
                        pe.matmul(psG[h][:, 0:CH], w.W2a[:, 0, h * 128:(h + 1) * 128], g[:, q, 0], start=True, stop=False)
                        last = pe.matmul(psG[h][:, 0:CH], w.W2a[:, 1, h * 128:(h + 1) * 128], mean[:, q % 2], start=False, stop=True)
                    last.then_inc(m.hidden2, 1)

                pipeline(pe, ECHUNK, U, [(3, turn), (6, output), (4, message), (3, turn_attr), (5, hidden2), (3, hidden)])

            @block.scalar
            def _(act):
                def make_xn(k, q, r):
                    act.wait_ge(m.nb, made(k))
                    act.wait_ge(m.xT, made(k - 2))
                    norm_relu(act, xn[:, q % 2], x[:, q], rstd[:, q], nb[:, q], m.xn)

                def make_g(k, q, r):
                    act.wait_ge(m.xT, made(k))
                    act.wait_ge(m.hidden2, made(k - U))
                    act.activation(by_edge(g[:, q, 0]), by_tile(psT[0]), ACT.Identity)
                    act.activation(by_edge(g[:, q, 1]), by_tile(psT[1]), ACT.Identity).then_inc(m.g, 1)

                def make_msg(k, q, r):
                    act.wait_ge(m.psm, made(k))
                    act.wait_ge(m.tot, made(k - 2))
                    act.activation(msg[:, q % 2], psM[:, 0:CH], ACT.Identity, bias=w.b1b[:, 0:1]).then_inc(m.msg, 1)

                def make_eT(k, q, r):
                    act.wait_ge(m.eaT, made(k))
                    act.wait_ge(m.hidden, made(k - 2))
                    act.activation(by_edge(eT[:, q % 2]), by_tile(psT[0]), ACT.Identity).then_inc(m.eT, 1)

                def half(k, q, r):
                    act.wait_ge(m.hidden, made(k))
                    act.wait_ge(m.psm, made(k - 2))
                    act.activation(hid[:, q % 2, 0], psH[0][:, 0:CH], ACT.Relu, bias=w.b1a[:, 0:1]).then_inc(m.hid0, 1)

                def half2(k, q, r):
                    act.wait_ge(m.hidden2, made(k))
                    act.wait_ge(m.o_ps, made(k - 2))
                    act.activation(hid2[:, q % 2, 0], psG[0][:, 0:CH], ACT.Relu, bias=w.b2u[:, 0:1]).then_inc(m.hid20, 1)

                pipeline(act, ECHUNK, U, [(3, make_g), (2, make_xn), (4, make_msg), (3, make_eT), (5, half2), (3, half)])


def program(nc, a, out):
    dram = lambda n, s, d=F32: nc.dram_tensor(n, s, d, kind="Internal").ap()
    scratch = Group(
        dst_pad=dram("dst_pad", (1, EDGES + 2), I32), end_index=dram("end_index", (EDGES,), I32),
        node_map=dram("node_map", (NODES, MAPW), I32), edge_row=dram("edge_row", (EDGES, MAPW), I32),
        src_row=dram("src_row", (EDGES,), I32),
        hT=dram("hT", (128, NODES)), yT=dram("yT", (128, NODES)),
        h2=dram("h2_rows", (NODES + EDGES, D)), x1=dram("x1_rows", (NODES + EDGES, D)),
        xd=dram("xd_rows", (EDGES, D)), x1d=dram("x1d_rows", (EDGES, D)),
        hdT=dram("hdT", (128, EDGES)), hsT=dram("hsT", (128, EDGES)), ydT=dram("ydT", (128, EDGES)),
        ywT=dram("ywT", (128, EDGES)))
    with ExitStack() as ctx:
        sb = lambda n, s, d=F32: ctx.enter_context(nc.sbuf_tensor(n, s, d))
        L = LAYERS
        w = Group(
            W_in=sb("W_in", [128, D]), Wq=sb("Wq", [128, L, D]), Wk=sb("Wk", [128, L, D]), Wv=sb("Wv", [128, L, D]),
            Wskip=sb("Wskip", [128, L, D]), We=sb("We", [1, L, D]), gate_h=sb("gate_h", [128, L, D]),
            gate_out=sb("gate_out", [128, L, D]), heads=sb("heads", [128, D]), ident=sb("ident", [128, 128]),
            W1a=sb("W1a", [128, 2, 256]), W1b=sb("W1b", [128, 2, D]), W2a=sb("W2a", [128, 2, 256]),
            W2b=sb("W2b", [128, 2, D]), b_in=sb("b_in", [128, 1]), bq=sb("bq", [128, L]), bk=sb("bk", [128, L]),
            bv=sb("bv", [128, L]), bskip=sb("bskip", [128, L]), gamma=sb("gamma", [128, L]), beta=sb("beta", [128, L]),
            gate_b=sb("gate_b", [128, L]), gate_bh=sb("gate_bh", [128, L]), b1a=sb("b1a", [128, 2]),
            b1b=sb("b1b", [128, 1]), b2u=sb("b2u", [128, 2]), b2b=sb("b2b", [TILE, D]),
            power=sb("power", [128, 2 * TILES]), eps=sb("eps", [128, 2 * TILES]), two=sb("two", [128, 1]),
            ystats=sb("ystats", [128, 6 * NCHUNK]), ends=sb("ends", [128, 6 * ECHUNK]), wends=sb("wends", [128, 6 * ECHUNK]),
            bn=sb("bn", [128, 2]))
        prepare(nc, a, w, scratch)
        first_layer_in(nc, a, w, scratch)
        attention(nc, a, w, scratch, 0)
        batch_norm_params(nc, w, 0)
        edge_update(nc, a, w, scratch, 0)
        dense_second(nc, a, w, scratch)
        attention(nc, a, w, scratch, 1)
        batch_norm_params(nc, w, 1)
        dense_last(nc, a, w, scratch, out)
        edge_last(nc, a, w, scratch, out)


_INS = ['x', 'src', 'dst', 'edge_attr_128', 'edge_weight1', 'L0_gnn_W_in', 'L0_gnn_b_in', 'L0_gnn_Wq', 'L0_gnn_bq',
        'L0_gnn_Wk', 'L0_gnn_bk', 'L0_gnn_Wv', 'L0_gnn_bv', 'L0_gnn_We', 'L0_gnn_Wskip', 'L0_gnn_bskip',
        'L0_gnn_Wbeta', 'L0_gnn_bn_gamma', 'L0_gnn_bn_beta', 'L1_gnn_u', 'L1_gnn_W1a', 'L1_gnn_b1a', 'L1_gnn_W1b',
        'L1_gnn_b1b', 'L1_gnn_W2a', 'L1_gnn_b2a', 'L1_gnn_W2b', 'L1_gnn_b2b']


def kernel(**inputs):
    import numpy as _np
    import concourse.bacc as _bacc
    from concourse import mybir as _mybir
    from concourse.bass_utils import run_bass_kernel_spmd as _run

    nc = _bacc.Bacc("TRN2", target_bir_lowering=False, num_devices=1)
    arrays, args = {}, {}
    for name in _INS:
        v = _np.ascontiguousarray(inputs[name])
        arrays[f"in_{name}"] = v
        args[name] = nc.dram_tensor(f"in_{name}", v.shape, _mybir.dt.from_np(v.dtype), kind="ExternalInput").ap()
    out = nc.dram_tensor("out", (NODES, D), F32, kind="ExternalOutput").ap()
    program(nc, args, out)
    return _run(nc, [arrays], core_ids=[0]).results[0]["out"]
```
